# Optimizing a Trainium2 kernel written in Bass

```python
import numpy as np
import jax
import jax.numpy as jnp

def _softmax(x, axis=-1):
    return jax.nn.softmax(x, axis=axis)

def _gelu(x):
    return jax.nn.gelu(x, approximate=True)

def _silu(x):
    return jax.nn.silu(x)

def _sigmoid(x):
    return jax.nn.sigmoid(x)

def _layernorm(x, axis=-1, eps=1e-05):
    m = jnp.mean(x, axis=axis, keepdims=True)
    v = jnp.var(x, axis=axis, keepdims=True)
    return (x - m) / jnp.sqrt(v + eps)

def _scatter_add(tgt, idx, src, axis=0):
    return tgt.at[idx].add(src)

def _segment_sum(src, seg, n):
    return jax.ops.segment_sum(src, seg, n)
kernel_name = 'mk_xattn_ffn_d2_seqx_r4_718905'

def setup_inputs(seed: int=0):
    np.random.seed(seed)
    _w = jnp.asarray

    def _rec_inputs():
        import jax
        import jax.numpy as jnp
        _rk = jax.random.key(seed)
        x = 0.0003765 + 1 * jax.random.normal(jax.random.fold_in(_rk, 1), (8, 512, 256), jnp.float32)
        _lenS = 512 - jax.random.randint(jax.random.fold_in(_rk, 7), (8,), 0, max(1, 512 // 4) + 1, jnp.int32)
        _lenS2 = 64 - jax.random.randint(jax.random.fold_in(_rk, 8), (8,), 0, max(1, 64 // 4) + 1, jnp.int32)
        _ctx_1024P = jax.random.normal(jax.random.fold_in(_rk, 11), (8, 16, 256), jnp.float32)
        _ctx_1024c = jax.random.dirichlet(jax.random.fold_in(_rk, 511), 0.3 * jnp.ones((16,), jnp.float32), (8, 64))
        _ctx_1024t = jnp.einsum('bsk,bkd->bsd', _ctx_1024c, _ctx_1024P)
        _ctx_1024t = _ctx_1024t * jax.lax.rsqrt(jnp.mean(jnp.square(_ctx_1024t)) + 1e-12) * 0.953939
        ctx_1024 = -0.000292821 + 1.00034 * (_ctx_1024t + 0.3 * jax.random.normal(jax.random.fold_in(_rk, 611), (8, 64, 256), jnp.float32))
        return (x, ctx_1024)
    x, ctx_1024 = _rec_inputs()

    def _L0_xattn_setup():
        import jax, jax.numpy as jnp
        import numpy as np
        NUM_HEADS = 16

        def _split_heads(x, h):
            b, s, d = x.shape
            return x.reshape(b, s, h, d // h).transpose(0, 2, 1, 3)
        key = jax.random.key(seed)
        kv, kk, kq = jax.random.split(key, 3)
        shape = (2, 512, 256)
        return {'v': jax.random.normal(kv, shape, dtype=jnp.float32), 'k': jax.random.normal(kk, shape, dtype=jnp.float32), 'q': jax.random.normal(kq, shape, dtype=jnp.float32)}
    _L0_xattn_all = _L0_xattn_setup()
    _L0_xattn_in = {k: v for k, v in _L0_xattn_all.items() if k in ()}
    del _L0_xattn_all

    def _L0_ffn_setup():
        import jax, jax.numpy as jnp
        import numpy as np
        TOPK = 8
        BN_EPS = 1e-05
        key = jax.random.key(seed)
        ks = jax.random.split(key, 5)
        b, n, d = (2, 256, 256)
        h, nk, kd = (8, 64, 128)
        ne = nk * nk
        scale = 0.02
        return {'inputs': jax.random.normal(ks[0], (b, n, d), jnp.float32), 'gamma': jnp.ones((d,), jnp.float32), 'beta': jnp.zeros((d,), jnp.float32), 'w_q': jax.random.normal(ks[1], (2 * h * kd, d), jnp.float32) * scale, 'keys': jax.random.normal(ks[2], (h, nk, 2, kd), jnp.float32) * scale, 'key_in': jax.random.normal(ks[3], (ne, d), jnp.float32) * scale, 'key_out': jax.random.normal(ks[4], (ne, d), jnp.float32) * scale}
    _L0_ffn_all = _L0_ffn_setup()
    _L0_ffn_in = {k: v for k, v in _L0_ffn_all.items() if k in ('gamma', 'beta', 'w_q', 'keys', 'key_in', 'key_out')}
    del _L0_ffn_all

    def _L1_xattn_setup():
        import jax, jax.numpy as jnp
        import numpy as np
        EPS = 1e-05

        def layer_norm(x, w, b):
            mu = jnp.mean(x, axis=-1, keepdims=True)
            var = jnp.mean((x - mu) ** 2, axis=-1, keepdims=True)
            return (x - mu) * jax.lax.rsqrt(var + EPS) * w + b
        key = jax.random.key(seed)
        ks = jax.random.split(key, 8)
        b, Nx, Nz, D = (16, 1024, 64, 256)
        H, Dh = (8, 64)
        inner = H * Dh
        s = 1.0 / np.sqrt(D)
        return {'x': jax.random.normal(ks[0], (b, Nx, D), jnp.float32), 'latents': jax.random.normal(ks[1], (b, Nz, D), jnp.float32), 'ln_media_w': jnp.ones((D,), jnp.float32), 'ln_media_b': jnp.zeros((D,), jnp.float32), 'ln_lat_w': jnp.ones((D,), jnp.float32), 'ln_lat_b': jnp.zeros((D,), jnp.float32), 'Wq': jax.random.normal(ks[2], (D, inner), jnp.float32) * s, 'Wk': jax.random.normal(ks[3], (D, inner), jnp.float32) * s, 'Wv': jax.random.normal(ks[4], (D, inner), jnp.float32) * s, 'Wout': jax.random.normal(ks[5], (inner, D), jnp.float32) * (1.0 / np.sqrt(inner))}
    _L1_xattn_all = _L1_xattn_setup()
    _L1_xattn_in = {k: v for k, v in _L1_xattn_all.items() if k in ('ln_media_w', 'ln_media_b', 'ln_lat_w', 'ln_lat_b', 'Wq', 'Wk', 'Wv', 'Wout')}
    del _L1_xattn_all

    def _L1_ffn_setup():
        import jax, jax.numpy as jnp
        import numpy as np
        EPS = 1e-05

        @jax.custom_vjp
        def ste_quantize(w):
            scale = jnp.maximum(jnp.mean(jnp.abs(w)), EPS)
            return jnp.clip(jnp.round(w / scale), -1.0, 1.0)

        def _ste_fwd(w):
            return (ste_quantize(w), None)

        def _ste_bwd(_, g):
            return (g,)
        ste_quantize.defvjp(_ste_fwd, _ste_bwd)
        key = jax.random.key(seed)
        k1, k2 = jax.random.split(key)
        x = jax.random.normal(k1, (8, 2048, 256), dtype=jnp.float32)
        weight = jax.random.normal(k2, (256, 256), dtype=jnp.float32) * 0.02
        return {'x': x, 'weight': weight}
    _L1_ffn_all = _L1_ffn_setup()
    _L1_ffn_in = {k: v for k, v in _L1_ffn_all.items() if k in ('weight',)}
    del _L1_ffn_all
    return {'x': x, 'ctx_1024': ctx_1024, 'L0_ffn_gamma': _L0_ffn_in['gamma'], 'L0_ffn_beta': _L0_ffn_in['beta'], 'L0_ffn_w_q': _L0_ffn_in['w_q'], 'L0_ffn_keys': _L0_ffn_in['keys'], 'L0_ffn_key_in': _L0_ffn_in['key_in'], 'L0_ffn_key_out': _L0_ffn_in['key_out'], 'L1_xattn_ln_media_w': _L1_xattn_in['ln_media_w'], 'L1_xattn_ln_media_b': _L1_xattn_in['ln_media_b'], 'L1_xattn_ln_lat_w': _L1_xattn_in['ln_lat_w'], 'L1_xattn_ln_lat_b': _L1_xattn_in['ln_lat_b'], 'L1_xattn_Wq': _L1_xattn_in['Wq'], 'L1_xattn_Wk': _L1_xattn_in['Wk'], 'L1_xattn_Wv': _L1_xattn_in['Wv'], 'L1_xattn_Wout': _L1_xattn_in['Wout'], 'L1_ffn_weight': _L1_ffn_in['weight']}

def reference(x, ctx_1024, L0_ffn_gamma, L0_ffn_beta, L0_ffn_w_q, L0_ffn_keys, L0_ffn_key_in, L0_ffn_key_out, L1_xattn_ln_media_w, L1_xattn_ln_media_b, L1_xattn_ln_lat_w, L1_xattn_ln_lat_b, L1_xattn_Wq, L1_xattn_Wk, L1_xattn_Wv, L1_xattn_Wout, L1_ffn_weight):
    import jax
    import jax.numpy as jnp

    def _L0_xattn_ref(v, k, q):
        import jax, jax.numpy as jnp
        import numpy as np
        NUM_HEADS = 16

        def _split_heads(x, h):
            b, s, d = x.shape
            return x.reshape(b, s, h, d // h).transpose(0, 2, 1, 3)
        b = q.shape[0]
        qh = _split_heads(q, NUM_HEADS)
        kh = _split_heads(k, NUM_HEADS)
        vh = _split_heads(v, NUM_HEADS)
        scores = jnp.einsum('bhqd,bhkd->bhqk', qh, kh)
        av = jnp.einsum('bhqk,bhkd->bhqd', jax.nn.silu(scores), vh)
        return av.transpose(0, 2, 1, 3).reshape(b, av.shape[2], -1)

    def _L0_ffn_ref(inputs, gamma, beta, w_q, keys, key_in, key_out):
        import jax, jax.numpy as jnp
        import numpy as np
        TOPK = 8
        BN_EPS = 1e-05
        b, n, d = inputs.shape
        h, nk, _, kd = keys.shape
        k = TOPK
        x = inputs.reshape(b * n, d)
        mu = jnp.mean(x, axis=0)
        var = jnp.mean(jnp.square(x - mu), axis=0)
        xn = (x - mu) * jax.lax.rsqrt(var + BN_EPS) * gamma + beta
        q = (xn @ w_q.T).reshape(b, n, 2, h, kd).transpose(2, 0, 1, 3, 4)
        sim = jnp.einsum('pbnhd,hkpd->pbnhk', q, keys)
        s, i = jax.lax.top_k(sim, k)
        sx, sy = (s[0], s[1])
        ix, iy = (i[0], i[1])
        all_scores = (sx[..., :, None] + sy[..., None, :]).reshape(b, n, h, k * k)
        all_idx = (ix[..., :, None] * nk + iy[..., None, :]).reshape(b, n, h, k * k)
        scores, pk = jax.lax.top_k(all_scores, k)
        idx = jnp.take_along_axis(all_idx, pk, axis=-1)
        w_down = key_in[idx]
        w_up = key_out[idx]
        o = jnp.einsum('bnd,bnhkd->bnhk', inputs, w_down)
        o = jax.nn.gelu(o, approximate=False) * jax.nn.softmax(scores, axis=-1)
        return jnp.einsum('bnhk,bnhkd->bnd', o, w_up)

    def _L1_xattn_ref(x, latents, ln_media_w, ln_media_b, ln_lat_w, ln_lat_b, Wq, Wk, Wv, Wout):
        import jax, jax.numpy as jnp
        import numpy as np
        EPS = 1e-05

        def layer_norm(x, w, b):
            mu = jnp.mean(x, axis=-1, keepdims=True)
            var = jnp.mean((x - mu) ** 2, axis=-1, keepdims=True)
            return (x - mu) * jax.lax.rsqrt(var + EPS) * w + b
        H, Dh = (8, 64)
        scale = Dh ** (-0.5)
        b, Nz, D = latents.shape
        xn = layer_norm(x, ln_media_w, ln_media_b)
        zn = layer_norm(latents, ln_lat_w, ln_lat_b)
        q = (zn @ Wq).reshape(b, Nz, H, Dh).transpose(0, 2, 1, 3)
        kv_in = jnp.concatenate([xn, zn], axis=1)
        F = kv_in.shape[1]
        k = (kv_in @ Wk).reshape(b, F, H, Dh).transpose(0, 2, 1, 3)
        v = (kv_in @ Wv).reshape(b, F, H, Dh).transpose(0, 2, 1, 3)
        sim = jnp.einsum('bhqd,bhfd->bhqf', q * scale, k)
        alphas = jax.nn.softmax(sim, axis=-1)
        out = jnp.einsum('bhqf,bhfd->bhqd', alphas, v)
        out = out.transpose(0, 2, 1, 3).reshape(b, Nz, H * Dh)
        return out @ Wout

    def _L1_ffn_ref(x, weight):
        import jax, jax.numpy as jnp
        import numpy as np
        EPS = 1e-05

        @jax.custom_vjp
        def ste_quantize(w):
            scale = jnp.maximum(jnp.mean(jnp.abs(w)), EPS)
            return jnp.clip(jnp.round(w / scale), -1.0, 1.0)

        def _ste_fwd(w):
            return (ste_quantize(w), None)

        def _ste_bwd(_, g):
            return (g,)
        ste_quantize.defvjp(_ste_fwd, _ste_bwd)
        w_ternary = ste_quantize(weight)
        scale = jnp.maximum(jnp.mean(jnp.abs(weight)), EPS)
        return jnp.einsum('bsi,oi->bso', x, w_ternary * scale)
    x = x + _L0_xattn_ref(ctx_1024, ctx_1024, _layernorm(x, axis=-1))
    x = x + _L0_ffn_ref(_layernorm(x, axis=-1), L0_ffn_gamma, L0_ffn_beta, L0_ffn_w_q, L0_ffn_keys, L0_ffn_key_in, L0_ffn_key_out)
    x = x + _L1_xattn_ref(ctx_1024, _layernorm(x, axis=-1), L1_xattn_ln_media_w, L1_xattn_ln_media_b, L1_xattn_ln_lat_w, L1_xattn_ln_lat_b, L1_xattn_Wq, L1_xattn_Wk, L1_xattn_Wv, L1_xattn_Wout)
    x = x + _L1_ffn_ref(_layernorm(x, axis=-1), L1_ffn_weight)
    return x

_drawn_inputs = setup_inputs


def setup_inputs(seed=0):
    import zlib

    import numpy as np

    out = dict(_drawn_inputs(seed))
    spreads = {'L0_ffn_gamma': (1.0, 0.6),
     'L0_ffn_beta': (0.0, 0.8),
     'L1_xattn_ln_media_w': (1.0, 0.6),
     'L1_xattn_ln_media_b': (0.0, 0.8),
     'L1_xattn_ln_lat_w': (1.0, 0.6),
     'L1_xattn_ln_lat_b': (0.0, 0.8)}
    factors = {'L0_ffn_w_q': 8.0,
     'L0_ffn_keys': 8.0,
     'L0_ffn_key_in': 8.0,
     'L0_ffn_key_out': 8.0,
     'L1_xattn_Wq': 8.0,
     'L1_xattn_Wk': 8.0,
     'L1_xattn_Wv': 6.216,
     'L1_xattn_Wout': 6.404,
     'L1_ffn_weight': 27.783}
    for name, (base, spread) in spreads.items():
        noise = np.random.default_rng([zlib.crc32(name.encode()), seed]).standard_normal(out[name].shape)
        drawn = base * np.exp(spread * noise) if base else spread * noise
        out[name] = jnp.asarray(drawn.astype(out[name].dtype))
    for name, factor in factors.items():
        out[name] = (out[name] * factor).astype(out[name].dtype)
    return out
```

```python
import concourse.bass as bass
from concourse import mybir
from contextlib import ExitStack

F32 = mybir.dt.float32
F32R = mybir.dt.float32r
BF16 = mybir.dt.bfloat16
U32 = mybir.dt.uint32
ALU = mybir.AluOpType
ACT = mybir.ActivationFunctionType
AXX = mybir.AxisListType.X
P = 128
EPS = 1e-5


class Signal:

    def __init__(self, sem, per, start=0):
        self.sem, self.per, self.start = sem, per, start

    def at(self, i, k):
        return i * self.per + (self.start + k)


class Chain:

    def __init__(self, eng, sem, base=0):
        self.eng, self.sem, self.base, self.n = eng, sem, base, 0

    def link(self, ins):
        ins.then_inc(self.sem, 1)
        self.n += 1
        return self.n

    def wait(self, k=None):
        self.eng.wait_ge(self.sem, self.base + (self.n if k is None else k))

    def wait_apart(self, passed):
        wait_apart(self.eng, self.sem, self.base + self.n, passed)


def three_pass(pe, out, w_hi, w_lo, x_hi, x_lo, start, stop):
    pe.matmul(out, w_lo, x_hi, start=start, stop=False)
    pe.matmul(out, w_hi, x_lo, start=False, stop=False)
    return pe.matmul(out, w_hi, x_hi, start=False, stop=stop)


def wait_apart(eng, sem, value, passed):
    eng.wait_ge(sem, value)
    eng.sem_inc(passed, 1)


def attend_context(nc, x, ctx, x1_dram, xt_dram, cst):
    B, N, D = x.shape
    S = ctx.shape[1]
    T, C = N // P, D // P
    PAIRS = D // 32
    ident, neghalf, bn_out = cst["ident"], cst["neghalf"], cst["bn"]
    own = ExitStack()
    with own:
        def sb(name, shape, dt=F32):
            return own.enter_context(nc.sbuf_tensor(name, shape, dt))

        def sig(name, per=0, start=0):
            return Signal(own.enter_context(nc.semaphore(name)), per, start)

        bank = [own.enter_context(nc.psum_tensor(f"a_bank{i}", [P, 512], F32)) for i in range(8)]
        trans, score, outp = bank[0:2], bank[2:6], bank[6:8]

        ctx_rows = sb("a_ctx_rows", [P, B * S // P, D])
        ctx_t = sb("a_ctx_t", [P, C, B * S])
        ctx_twice = sb("a_ctx_twice", [P, B, D])
        mask_k = sb("a_mask_k", [P, 8])
        mask_v = sb("a_mask_v", [P, PAIRS, 2, 16])
        vals = sb("a_vals", [P, B, D])
        keys_f = sb("a_keys_f", [P, 8, S])
        keys_hi = [sb(f"a_keys_hi{p}", [P, C, 8, S], F32R) for p in range(2)]
        keys_lo = [sb(f"a_keys_lo{p}", [P, C, 8, S], F32R) for p in range(2)]
        xa = [sb(f"a_x{p}", [P, T, D]) for p in range(2)]
        rows = [sb(f"a_rows{p}", [P, T, D]) for p in range(2)]
        q_hi = [sb(f"a_q_hi{p}", [P, C, N], F32R) for p in range(2)]
        q_lo = [sb(f"a_q_lo{p}", [P, C, N], F32R) for p in range(2)]
        acts = [sb(f"a_acts{p}", [P, PAIRS, N]) for p in range(2)]
        x1 = [sb(f"a_x1{p}", [P, T, D]) for p in range(2)]
        xt = [sb(f"a_xt{p}", [P, C, N]) for p in range(2)]
        stats = [sb(f"a_stats{p}", [P, T, 6]) for p in range(2)]
        mean_var = [sb(f"a_mean_var{p}", [P, T, 2]) for p in range(2)]
        var_eps = [sb(f"a_var_eps{p}", [P, T]) for p in range(2)]
        rstd = [sb(f"a_rstd{p}", [P, T]) for p in range(2)]
        bn_stats = sb("a_bn_stats", [P, C, B, 6])
        bn_mv = sb("a_bn_mv", [P, C, 2])
        bn_ve = sb("a_bn_ve", [P, C])
        bn_rs = sb("a_bn_rs", [P, C])
        gamma_beta = sb("a_gamma_beta", [P, 2, C])
        bn_tmp = sb("a_bn_tmp", [P, C])

        ctx_in, x_in, gb_in = sig("a_ctx_in"), [sig(f"a_x_in{p}", 16) for p in range(2)], sig("a_gb_in")
        consts, ctx_tr, ctx_ev, vals_done = sig("a_consts"), sig("a_ctx_tr"), sig("a_ctx_ev"), sig("a_vals")
        var_ready, rs_ready, rows_ready = sig("a_var", 4), sig("a_rs", 4), sig("a_rows", 4)
        tr_done = sig("a_tr", 8)
        act_ev, dve_ev = sig("a_act_ev", 8, 2), sig("a_dve_ev", 8, 2)
        keys_ready, score_used = sig("a_keys", 2), sig("a_score_used", 2, 2)
        score_done, silu_done = sig("a_score", 16), sig("a_silu", 16, 4)
        av_done, x1_done = sig("a_av", 4), sig("a_x1", 4, 4)
        x1_kept = [sig(f"a_x1_kept{p}", 16, 16) for p in range(2)]
        xt_kept = [sig(f"a_xt_kept{p}", 16, 16) for p in range(2)]
        dve_own, pool_own = sig("a_dve_own", 16), sig("a_pool_own", 14)
        bn_var, bn_rs_ready, bn_done = sig("a_bn_var"), sig("a_bn_rs"), sig("a_bn_done")
        passed = sig("a_passed")
        TURNS = B // 2
        block = own.enter_context(nc.Block())

        @block.sync
        def _(sp):
            sp.dma_start(ctx_rows[:, :, :], ctx.rearrange("b s d -> (b s) d")
                         .rearrange("(t p) d -> p t d", p=P)).then_inc(ctx_in.sem, 16)
            for half in range(2):
                sp.dma_start(ctx_twice[64 * half:64 * half + 64, :, :],
                             ctx.rearrange("b s d -> s b d")).then_inc(ctx_in.sem, 16)
            sp.dma_start(gamma_beta[:, 0, :], cst["gamma"].rearrange("(c p) -> p c", p=P),
                         allow_slow_non_contiguous=True).then_inc(gb_in.sem, 16)
            sp.dma_start(gamma_beta[:, 1, :], cst["beta"].rearrange("(c p) -> p c", p=P),
                         allow_slow_non_contiguous=True).then_inc(gb_in.sem, 16)
            with sp.Fori(0, TURNS) as i:
                for p in range(2):
                    sp.wait_ge(x1_done.sem, x1_done.at(i, 2 * p + 2 - 4))
                    sp.dma_start(xa[p][:, :, :], x[2 * i + p, :, :].rearrange("(t p) d -> p t d", p=P)) \
                        .then_inc(x_in[p].sem, 16)

        @block.gpsimd
        def _(pool):
            own_chain = Chain(pool, consts.sem)
            own_chain.link(pool.memset(ident[:, :], 0.0))
            own_chain.link(pool.memset(mask_k[:, :], 1.0))
            own_chain.link(pool.memset(neghalf[:, :], -0.5))
            own_chain.link(pool.memset(mask_v[:, :, :, :], 0.0))
            own_chain.wait()
            own_chain.link(pool.affine_select(out=ident[:, :], in_=ident[:, :], compare_op=ALU.not_equal, fill=1.0,
                                              base=0, pattern=[[-1, P]], channel_multiplier=1))
            own_chain.link(pool.affine_select(out=mask_k[:, :], in_=mask_k[:, :], compare_op=ALU.is_ge, fill=0.0,
                                              base=0, pattern=[[-16, 8]], channel_multiplier=1))
            own_chain.wait()
            own_chain.link(pool.memset(mask_v[0:64, :, 0, :], 1.0))
            own_chain.wait()
            own_chain.link(pool.memset(mask_v[64:128, :, 1, :], 1.0))
            own_chain.wait()
            own_chain.link(pool.affine_select(out=mask_k[:, :], in_=mask_k[:, :], compare_op=ALU.is_ge, fill=0.0,
                                              base=15, pattern=[[16, 8]], channel_multiplier=-1))
            own_chain.wait()
            pool.wait_ge(ctx_in.sem, 48)
            for b in range(B):
                pool.tensor_tensor(vals[:, b, :], ctx_twice[:, b, :], mask_v[:, :, :, :].rearrange("p a b c -> p (a b c)"),
                                   ALU.mult).then_inc(vals_done.sem, 1)
            pool.sem_inc(act_ev.sem, act_ev.start)
            pool.sem_inc(dve_ev.sem, dve_ev.start)
            pool.sem_inc(score_used.sem, score_used.start)
            pool.sem_inc(silu_done.sem, silu_done.start)
            pool.sem_inc(x1_done.sem, x1_done.start)
            for p in range(2):
                pool.sem_inc(x1_kept[p].sem, x1_kept[p].start)
                pool.sem_inc(xt_kept[p].sem, xt_kept[p].start)
            pool.wait_ge(ctx_ev.sem, C)

            def rsqrt(i, u, p, chain):
                wait_apart(pool, var_ready.sem, var_ready.at(i, u + 1), passed.sem)
                chain.link(pool.tensor_scalar(var_eps[p][:, :], mean_var[p][:, :, 1], EPS, None, ALU.add))
                chain.wait()
                pool.tensor_tensor(rstd[p][:, :], var_eps[p][:, :], neghalf[:, 0:T], ALU.pow).then_inc(rs_ready.sem, 1)

            with pool.Fori(0, TURNS) as i:
                chain = Chain(pool, pool_own.sem, i * pool_own.per)
                rsqrt(i, 0, 0, chain)
                rsqrt(i, 1, 1, chain)
                for p in range(2):
                    pool.wait_ge(score_used.sem, score_used.at(i, p + 1 - 2))
                    for c in range(C):
                        src = ctx_t[:, c, bass.ds((2 * i + p) * S, S)]
                        chain.link(pool.tensor_tensor(keys_f[:, :, :], src.unsqueeze(1).to_broadcast([P, 8, S]),
                                                      mask_k[:, :].unsqueeze(2).to_broadcast([P, 8, S]), ALU.mult))
                        chain.wait_apart(passed.sem)
                        chain.link(pool.tensor_copy(keys_hi[p][:, c, :, :], keys_f[:, :, :]))
                        chain.wait()
                        last = pool.tensor_tensor(keys_lo[p][:, c, :, :], keys_f[:, :, :],
                                                  keys_hi[p][:, c, :, :].bitcast(F32), ALU.subtract)
                        if c < C - 1:
                            chain.link(last)
                            chain.wait()
                    last.then_inc(keys_ready.sem, 1)
                    pool.wait_ge(keys_ready.sem, keys_ready.at(i, p + 1))
                rsqrt(i, 2, 0, chain)
                rsqrt(i, 3, 1, chain)
                assert chain.n == pool_own.per, chain.n
            pool.wait_ge(bn_var.sem, 1)
            pool.tensor_scalar(bn_ve[:, :], bn_mv[:, :, 1], EPS, None, ALU.add).then_inc(bn_rs_ready.sem, 1)
            pool.wait_ge(bn_rs_ready.sem, 1)
            pool.tensor_tensor(bn_rs[:, :], bn_ve[:, :], neghalf[:, 0:C], ALU.pow).then_inc(bn_rs_ready.sem, 1)

        @block.tensor
        def _(pe):
            pe.wait_ge(consts.sem, 9)
            pe.wait_ge(ctx_in.sem, 48)
            for c in range(C):
                for t in range(B * S // P):
                    last = pe.transpose(trans[c][:, t * P:(t + 1) * P], ctx_rows[:, t, c * P:(c + 1) * P], ident[:, :])
                last.then_inc(ctx_tr.sem, 1)
            pe.wait_ge(ctx_ev.sem, C)
            pe.wait_ge(vals_done.sem, B)

            def transposes(i, u, p):
                pe.wait_ge(rows_ready.sem, rows_ready.at(i, u + 1))
                for c in range(C):
                    pe.wait_ge(act_ev.sem, act_ev.at(i, 2 * u + c + 1 - 2))
                    pe.wait_ge(dve_ev.sem, dve_ev.at(i, 2 * u + c + 1 - 2))
                    for t in range(T):
                        last = pe.transpose(trans[c][:, t * P:(t + 1) * P], rows[p][:, t, c * P:(c + 1) * P], ident[:, :])
                    last.then_inc(tr_done.sem, 1)

            def scores(i, p):
                pe.wait_ge(keys_ready.sem, keys_ready.at(i, p + 1))
                pe.wait_ge(act_ev.sem, act_ev.at(i, 2 * p + 2))
                pe.wait_ge(dve_ev.sem, dve_ev.at(i, 2 * p + 2))
                for g in range(PAIRS):
                    c, pair = g // 4, g % 4
                    k = 8 * p + g
                    pe.wait_ge(silu_done.sem, silu_done.at(i, k + 1 - 4))
                    w_hi = keys_hi[p][:, c, 2 * pair:2 * pair + 2, :].rearrange("p a b -> p (a b)")
                    w_lo = keys_lo[p][:, c, 2 * pair:2 * pair + 2, :].rearrange("p a b -> p (a b)")
                    three_pass(pe, score[k % 4][:, :], w_hi, w_lo, q_hi[p][:, c, :], q_lo[p][:, c, :],
                               True, True).then_inc(score_done.sem, 1)

            def values(i, p):
                pe.wait_ge(silu_done.sem, silu_done.at(i, 8 * p + 8))
                for j in range(T // 2):
                    pe.wait_ge(x1_done.sem, x1_done.at(i, 2 * p + j + 1 - 2))
                    for t in (2 * j, 2 * j + 1):
                        for g in range(PAIRS):
                            last = pe.matmul(outp[j][:, (t % 2) * D + 32 * g:(t % 2) * D + 32 * g + 32],
                                             acts[p][:, g, t * P:(t + 1) * P],
                                             vals[:, bass.ds(2 * i + p, 1), 32 * g:32 * g + 32].rearrange("p a b -> p (a b)"),
                                             start=True, stop=True)
                    last.then_inc(av_done.sem, 1)

            with pe.Fori(0, TURNS) as i:
                transposes(i, 0, 0)
                scores(i, 0)
                transposes(i, 1, 1)
                scores(i, 1)
                values(i, 0)
                values(i, 1)
                transposes(i, 2, 0)
                transposes(i, 3, 1)

        @block.scalar
        def _(act):
            for c in range(C):
                act.wait_ge(ctx_tr.sem, c + 1)
                act.activation(ctx_t[:, c, :], trans[c][:, :], ACT.Copy).then_inc(ctx_ev.sem, 1)

            with act.Fori(0, TURNS) as i:
                for p in range(2):
                    for c in range(C):
                        act.wait_ge(tr_done.sem, tr_done.at(i, 2 * p + c + 1))
                        act.activation(q_hi[p][:, c, :], trans[c][:, :], ACT.Copy).then_inc(act_ev.sem, 1)
                    for g in range(PAIRS):
                        k = 8 * p + g
                        act.wait_ge(score_done.sem, score_done.at(i, k + 1))
                        act.activation(acts[p][:, g, :], score[k % 4][:, :], ACT.Silu).then_inc(silu_done.sem, 1)
                    act.sem_inc(score_used.sem, 1)
                for p in range(2):
                    act.wait_ge(xt_kept[p].sem, xt_kept[p].at(i, 0))
                    for c in range(C):
                        act.wait_ge(tr_done.sem, tr_done.at(i, 4 + 2 * p + c + 1))
                        act.activation(xt[p][:, c, :], trans[c][:, :], ACT.Copy).then_inc(act_ev.sem, 1)
                    act.wait_ge(act_ev.sem, act_ev.at(i, 4 + 2 * p + 2))
                    act.dma_start(xt_dram[:, :, bass.ds((2 * i + p) * N, N)].rearrange("c p n -> p c n"), xt[p][:, :, :]) \
                        .then_inc(xt_kept[p].sem, 16)
                    act.wait_ge(x1_done.sem, x1_done.at(i, 2 * p + 2))
                    act.dma_start(x1_dram[2 * i + p, :, :].rearrange("(t p) d -> p t d", p=P), x1[p][:, :, :]) \
                        .then_inc(x1_kept[p].sem, 16)
            for p in range(2):
                act.wait_ge(xt_kept[p].sem, 16 + 16 * TURNS)
                act.wait_ge(x1_kept[p].sem, 16 + 16 * TURNS)

        @block.vector
        def _(dve):
            def moments(chain, src, p):
                for t in range(T):
                    chain.link(dve.bn_stats(stats[p][:, t, :], src[:, t, :]))
                chain.wait_apart(passed.sem)
                for t in range(T):
                    last = dve.bn_aggr(mean_var[p][:, t, :], stats[p][:, t, :])
                last.then_inc(var_ready.sem, 1)

            def normalise(i, u, p, src):
                dve.wait_ge(var_ready.sem, var_ready.at(i, u + 1))
                dve.wait_ge(rs_ready.sem, rs_ready.at(i, u + 1))
                for t in range(T):
                    last = dve.tensor_scalar(rows[p][:, t, :], src[:, t, :], mean_var[p][:, t, 0:1], rstd[p][:, t:t + 1],
                                             ALU.subtract, ALU.mult)
                last.then_inc(rows_ready.sem, 1)

            with dve.Fori(0, TURNS) as i:
                chain = Chain(dve, dve_own.sem, i * dve_own.per)
                for p in range(2):
                    dve.wait_ge(x_in[p].sem, x_in[p].at(i, 16))
                    moments(chain, xa[p], p)
                for p in range(2):
                    normalise(i, p, p, xa[p])
                for p in range(2):
                    for c in range(C):
                        dve.wait_ge(act_ev.sem, act_ev.at(i, 2 * p + c + 1))
                        dve.tensor_tensor(q_lo[p][:, c, :], trans[c][:, :], q_hi[p][:, c, :].bitcast(F32),
                                          ALU.subtract).then_inc(dve_ev.sem, 1)
                for p in range(2):
                    dve.wait_ge(x1_kept[p].sem, x1_kept[p].at(i, 0))
                    for j in range(T // 2):
                        dve.wait_ge(av_done.sem, av_done.at(i, 2 * p + j + 1))
                        dve.tensor_tensor(x1[p][:, 2 * j:2 * j + 2, :], xa[p][:, 2 * j:2 * j + 2, :],
                                          outp[j][:, :].rearrange("p (t d) -> p t d", t=2), ALU.add) \
                            .then_inc(x1_done.sem, 1)
                    dve.wait_ge(x1_done.sem, x1_done.at(i, 2 * p + 2))
                    moments(chain, x1[p], p)
                for p in range(2):
                    normalise(i, 2 + p, p, x1[p])
                for p in range(2):
                    for c in range(C):
                        dve.wait_ge(act_ev.sem, act_ev.at(i, 4 + 2 * p + c + 1))
                        dve.bn_stats(bn_stats[:, c, bass.ds(2 * i + p, 1), :].rearrange("p a b -> p (a b)"), trans[c][:, :]) \
                            .then_inc(dve_ev.sem, 1)
                assert chain.n == dve_own.per, chain.n
            dve.wait_ge(dve_ev.sem, 2 + 8 * TURNS)
            for c in range(C):
                last = dve.bn_aggr(bn_mv[:, c, :], bn_stats[:, c, :, :].rearrange("p b s -> p (b s)"))
            last.then_inc(bn_var.sem, 1)
            dve.wait_ge(bn_rs_ready.sem, 2)
            dve.wait_ge(gb_in.sem, 32)
            dve.tensor_tensor(bn_out[:, 0, :], bn_rs[:, :], gamma_beta[:, 0, :], ALU.mult).then_inc(bn_done.sem, 1)
            dve.wait_ge(bn_done.sem, 1)
            dve.tensor_tensor(bn_tmp[:, :], bn_mv[:, :, 0], bn_out[:, 0, :], ALU.mult).then_inc(bn_done.sem, 1)
            dve.wait_ge(bn_done.sem, 2)
            dve.tensor_tensor(bn_out[:, 1, :], gamma_beta[:, 1, :], bn_tmp[:, :], ALU.subtract).then_inc(bn_done.sem, 1)
            dve.wait_ge(bn_done.sem, 3)


def retrieve_experts(nc, xt_dram, x1_dram, w_q, keys, key_in, key_out, x2_dram, cst):
    H, K, _, KD = keys.shape
    E, D = key_in.shape
    N = x1_dram.shape[0]
    C, NV, R, T = D // P, E // P, 2 * P, 2
    BLOCKS = N // R
    TOP = 8
    PICKS = H * TOP
    HALF = 32
    ident, bn = cst["ident"], cst["bn"]
    own = ExitStack()
    with own:
        def sb(name, shape, dt=F32):
            return own.enter_context(nc.sbuf_tensor(name, shape, dt))

        def sig(name, per=0, start=0):
            return Signal(own.enter_context(nc.semaphore(name)), per, start)

        bank = [own.enter_context(nc.psum_tensor(f"b_bank{i}", [P, 512], F32)) for i in range(8)]
        down_b, w_b, up_b, sim_b, tr_b = bank[0:2], bank[2:4], bank[4], bank[5:7], bank[7]

        key_hi = sb("b_key_hi", [P, C, NV, P], F32R)
        key_lo = sb("b_key_lo", [P, C, NV, P], F32R)
        key_up = sb("b_key_up", [P, NV, D])
        score_w = sb("b_score_w", [P, C, 2 * H * K])
        gated = sb("b_gated", [P, NV, R])
        hot_u = [sb(f"b_hot_u{h}", [P, P, HALF], BF16) for h in range(2)]
        hot_v = [sb(f"b_hot_v{h}", [P, NV, HALF], BF16) for h in range(2)]
        weigh_v = [sb(f"b_weigh_v{h}", [P, 3, 2, NV, HALF], BF16) for h in range(2)]
        ramp = sb("b_ramp", [P, P, 4], BF16)
        ramp8 = sb("b_ramp8", [P, TOP])
        x_raw = sb("b_x_raw", [P, C, R])
        x_hi = sb("b_x_hi", [P, C, R], F32R)
        x_lo = sb("b_x_lo", [P, C, R], F32R)
        x_norm = sb("b_x_norm", [P, C, R])
        x_rows = sb("b_x_rows", [P, T, D])
        best = sb("b_best", [P, 2, H, TOP])
        best_at = sb("b_best_at", [P, 2, H, TOP], U32)
        pairs = sb("b_pairs", [P, H, TOP, TOP])
        top = sb("b_top", [P, H, TOP])
        top_at = sb("b_top_at", [P, H, TOP], U32)
        coords = sb("b_coords", [P, 2, PICKS], U32)
        coords_f = sb("b_coords_f", [P, 2, PICKS])
        at_f = sb("b_at_f", [P, 2, H, TOP])
        hit = sb("b_hit", [P, 2, H, TOP, TOP])
        delta = sb("b_delta", [P, H, TOP])
        expo = sb("b_expo", [P, H, TOP])
        total = sb("b_total", [P, H])
        share = sb("b_share", [P, H])
        expert = sb("b_expert", [P, 2, PICKS])
        upper = sb("b_upper", [P, PICKS])
        cat = sb("b_cat", [P, 3, 2, PICKS])
        uv = sb("b_uv", [P, 2, PICKS], BF16)
        part = sb("b_part", [P, 3, PICKS], BF16)
        rest = sb("b_rest", [P, PICKS])
        rest2 = sb("b_rest2", [P, PICKS])
        wq_rows = own.enter_context(nc.sbuf_tensor("b_wq_rows", [P, 2, D], F32))

        key_ld, wq_ld, keys_ld, up_ld = sig("b_key_ld"), sig("b_wq_ld"), sig("b_keys_ld"), sig("b_up_ld")
        consts, zeroed = sig("b_consts"), sig("b_zeroed")
        s_tr, s_act, s_dve = sig("b_s_tr"), sig("b_s_act"), sig("b_s_dve")
        passed = sig("b_passed")
        raw_in, xn_ready = sig("b_raw_in", 16), sig("b_xn", 1, 1)
        xh_ready, xl_ready = sig("b_xh", 1), sig("b_xl", 1, 1)
        sims_done, topk_read = sig("b_sims", 2, 2), sig("b_topk_read", 2, 1)
        topk_done, map_done, exp_done = sig("b_topk", 2), sig("b_map", 2, 1), sig("b_exp", 2)
        cat_ready, tr_done = sig("b_cat", 2), sig("b_tr", 2)
        gen_ready, w_done, h_done = sig("b_gen", 4), sig("b_w", 16, 8), sig("b_h", 16, 2)
        down_done, gelu_done = sig("b_down", 16), sig("b_gelu", 16, 2)
        up_done, x2_done = sig("b_up", 2), sig("b_x2", 2, 1)
        rows_in, kept = sig("b_rows_in", 16), sig("b_kept", 32, 32)
        DVE_FIRST, DVE_TURN = 17, 30
        POOL_TILE = 7
        dve_own, pool_own = sig("b_dve_own"), sig("b_pool_own")
        block = own.enter_context(nc.Block())
        xt_view = xt_dram.rearrange("c p n -> p c n")
        setup_rows = gated[:, :, :]
        wq_all = [hot_u[h][:, :, :].rearrange("p a b -> p (a b)").bitcast(F32).rearrange("p (g d) -> p g d", d=D) for h in range(2)]
        old = weigh_v[0][:, :, :, :, :].rearrange("p a b c d -> p (a b c d)").bitcast(F32)
        keys_rows = old[:, 0:1024].rearrange("p (t d) -> p t d", t=4)
        keys_t = old[:, 1024:2048].rearrange("p (a n) -> p a n", a=2)

        @block.sync
        def _(sp):
            sp.dma_start(keys_rows, keys.rearrange("h k p d -> (h k) (p d)").rearrange("(t p) d -> p t d", p=P)) \
                .then_inc(keys_ld.sem, 16)
            wq_v = w_q.rearrange("(g p) d -> p g d", p=KD)
            for h in range(2):
                sp.dma_start(wq_all[h], wq_v[:, 8 * h:8 * h + 8, :]).then_inc(wq_ld.sem, 16)
            sp.dma_start(setup_rows, key_in.rearrange("(u v) d -> u v d", v=NV)).then_inc(key_ld.sem, 16)
            sp.dma_start(key_up[:, :, :], key_out.rearrange("(u v) d -> u v d", v=NV)).then_inc(up_ld.sem, 16)

            def load_x(j):
                sp.wait_ge(xl_ready.sem, xl_ready.at(j, 0))
                sp.wait_ge(xn_ready.sem, xn_ready.at(j, 0))
                sp.dma_start(x_raw[:, :, :], xt_view[:, :, bass.ds(j * R, R)]).then_inc(raw_in.sem, 16)

            def rows_through(j):
                sp.wait_ge(kept.sem, kept.at(j, 0))
                sp.dma_start(x_rows[:, :, :], x1_dram[bass.ds(j * R, R), :].rearrange("(t p) d -> p t d", p=P)) \
                    .then_inc(rows_in.sem, 16)
                for t in range(T):
                    sp.wait_ge(x2_done.sem, x2_done.at(j, t + 1))
                    sp.dma_start(x2_dram[bass.ds(j * R + t * P, P), :], x_rows[:, t, :]).then_inc(kept.sem, 16)

            load_x(0)
            with sp.Fori(0, BLOCKS - 1) as i:
                load_x(i + 1)
                rows_through(i)
            rows_through(BLOCKS - 1)
            sp.wait_ge(kept.sem, kept.at(BLOCKS, 0))

        @block.gpsimd
        def _(pool):
            pool.iota(ramp[:, :, :], [[1, P], [0, 4]], channel_multiplier=0,
                      allow_small_or_imprecise_dtypes=True).then_inc(consts.sem, 1)
            pool.iota(ramp8[:, :], [[1, TOP]], channel_multiplier=0,
                      allow_small_or_imprecise_dtypes=True).then_inc(consts.sem, 1)
            pool.wait_ge(consts.sem, 2)
            for s in (xn_ready, xl_ready, sims_done, topk_read, map_done, w_done, h_done, gelu_done, x2_done, kept):
                pool.sem_inc(s.sem, s.start)
            pool.memset(weigh_v[1][:, :, :, :, :], 0.0).then_inc(zeroed.sem, 1)
            pool.wait_ge(s_dve.sem, 1)
            pool.memset(weigh_v[0][:, :, :, :, :], 0.0).then_inc(zeroed.sem, 1)

            def place_picks(j, t, chain):
                wait_apart(pool, topk_done.sem, topk_done.at(j, t + 1), passed.sem)
                chain.link(pool.tensor_copy(coords_f[:, :, :], coords[:, :, :]))
                chain.link(pool.tensor_copy(at_f[:, :, :, :], best_at[:, :, :, :]))
                for a in range(2):
                    chain.wait()
                    hits = hit[:, a, :, :, :].rearrange("p h k i -> p (h k) i")
                    chain.link(pool.tensor_tensor(hits, coords_f[:, a, :].unsqueeze(2).to_broadcast([P, PICKS, TOP]),
                                                  ramp8[:, :].unsqueeze(1).to_broadcast([P, PICKS, TOP]), ALU.subtract))
                    chain.wait_apart(passed.sem)
                    chain.link(pool.tensor_scalar(hits, hits, 0.0, None, ALU.is_equal))
                    chain.wait()
                    last = pool.tensor_tensor(hit[:, a, :, :, :], hit[:, a, :, :, :],
                                              at_f[:, a, :, :].unsqueeze(2).to_broadcast([P, H, TOP, TOP]), ALU.mult)
                    if a == 0:
                        chain.link(last)
                last.then_inc(map_done.sem, 1)

            def split_low(j):
                pool.wait_ge(xh_ready.sem, xh_ready.at(j, 1))
                pool.tensor_tensor(x_lo[:, :, :], x_raw[:, :, :], x_hi[:, :, :].bitcast(F32), ALU.subtract) \
                    .then_inc(xl_ready.sem, 1)

            def prepare(j):
                chain = Chain(pool, pool_own.sem, j * (2 * POOL_TILE))
                place_picks(j, 0, chain)
                split_low(j)
                place_picks(j, 1, chain)
                assert chain.n == 2 * POOL_TILE, chain.n

            prepare(0)
            with pool.Fori(0, BLOCKS - 1) as i:
                prepare(i + 1)

        @block.tensor
        def _(pe):
            pe.wait_ge(keys_ld.sem, 16)
            for a in range(2):
                for t in range(4):
                    last = pe.transpose(bank[a][:, t * P:(t + 1) * P], keys_rows[:, t, a * KD:(a + 1) * KD], ident[:, :])
                last.then_inc(s_tr.sem, 1)
            pe.wait_ge(wq_ld.sem, 32)
            pe.wait_ge(s_act.sem, 2)
            for a in range(2):
                for c in range(C):
                    for h in range(H):
                        last = pe.matmul(bank[2 + 2 * a + c][:, h * K:(h + 1) * K], wq_all[a][:, h, c * P:(c + 1) * P],
                                         keys_t[:, a, h * K:(h + 1) * K], start=True, stop=True)
                    last.then_inc(s_tr.sem, 1)
            pe.wait_ge(key_ld.sem, 16)
            n = 0
            for c in range(C):
                for v in range(0, NV, 4):
                    b = 6 + n % 2
                    if n >= 2:
                        pe.wait_ge(s_act.sem, 6 + n - 1)
                        pe.wait_ge(s_dve.sem, 1 + n - 1)
                    for k in range(4):
                        last = pe.transpose(bank[b][:, k * P:(k + 1) * P], setup_rows[:, v + k, c * P:(c + 1) * P], ident[:, :])
                    last.then_inc(s_tr.sem, 1)
                    n += 1
            pe.wait_ge(s_act.sem, 6 + n)
            pe.wait_ge(s_dve.sem, 1 + n)
            pe.wait_ge(up_ld.sem, 16)

            def scores(j, t):
                if t == 0:
                    pe.wait_ge(xn_ready.sem, xn_ready.at(j, 1))
                pe.wait_ge(topk_read.sem, topk_read.at(j, t + 1 - 1))
                for a in range(2):
                    for c in range(C):
                        last = pe.matmul(sim_b[a][:, :], x_norm[:, c, t * P:(t + 1) * P],
                                         score_w[:, c, a * H * K:(a + 1) * H * K], start=(c == 0), stop=(c == C - 1))
                last.then_inc(sims_done.sem, 1)

            def down(j):
                pe.wait_ge(xl_ready.sem, xl_ready.at(j, 1))
                for g in range(NV // 2):
                    pe.wait_ge(gelu_done.sem, gelu_done.at(j, g + 1 - 2))
                    for v in (2 * g, 2 * g + 1):
                        o = down_b[g % 2][:, (v % 2) * R:(v % 2 + 1) * R]
                        for c in range(C):
                            last = three_pass(pe, o, key_hi[:, c, v, :], key_lo[:, c, v, :], x_hi[:, c, :], x_lo[:, c, :],
                                              c == 0, c == C - 1)
                    last.then_inc(down_done.sem, 1)

            def turn_picks(j, t):
                pe.wait_ge(cat_ready.sem, cat_ready.at(j, t + 1))
                for k in range(3):
                    last = pe.transpose(tr_b[:, k * P:(k + 1) * P], cat[:, k, :, :].rearrange("p a b -> p (a b)"), ident[:, :])
                last.then_inc(tr_done.sem, 1)

            def weights(j, t):
                for q in range(8):
                    h = q // 4
                    if q % 4 == 0:
                        pe.wait_ge(gen_ready.sem, gen_ready.at(j, 2 * t + h + 1))
                    pe.wait_ge(h_done.sem, h_done.at(j, 8 * t + q + 1 - 2))
                    for mm in range(8):
                        m = (q % 4) * 8 + mm
                        for k in range(3):
                            last = pe.matmul(w_b[q % 2][:, mm * 64:(mm + 1) * 64], hot_u[h][:, :, m],
                                             weigh_v[h][:, k, :, :, m].rearrange("p r v -> p (r v)"),
                                             start=(k == 0), stop=(k == 2))
                    last.then_inc(w_done.sem, 1)

            def up(j, t):
                pe.wait_ge(h_done.sem, h_done.at(j, 8 * t + 8))
                pe.wait_ge(x2_done.sem, x2_done.at(j, t + 1 - 1))
                for v in range(NV):
                    last = pe.matmul(up_b[:, 0:D], gated[:, v, t * P:(t + 1) * P], key_up[:, v, :],
                                     start=(v == 0), stop=(v == NV - 1))
                last.then_inc(up_done.sem, 1)

            scores(0, 0)
            scores(0, 1)
            turn_picks(0, 0)

            def turn(i, more):
                if more:
                    scores(i + 1, 0)
                down(i)
                turn_picks(i, 1)
                weights(i, 0)
                up(i, 0)
                if more:
                    scores(i + 1, 1)
                weights(i, 1)
                up(i, 1)
                if more:
                    turn_picks(i + 1, 0)

            with pe.Fori(0, BLOCKS - 1) as i:
                turn(i, True)
            turn(BLOCKS - 1, False)

        @block.scalar
        def _(act):
            for a in range(2):
                act.wait_ge(s_tr.sem, a + 1)
                act.activation(keys_t[:, a, :], bank[a][:, :], ACT.Copy).then_inc(s_act.sem, 1)
            for a in range(2):
                for c in range(C):
                    act.wait_ge(s_tr.sem, 2 + 2 * a + c + 1)
                    act.activation(score_w[:, c, a * H * K:(a + 1) * H * K], bank[2 + 2 * a + c][:, :], ACT.Copy) \
                        .then_inc(s_act.sem, 1)
            n = 0
            for c in range(C):
                for v in range(0, NV, 4):
                    act.wait_ge(s_tr.sem, 6 + n + 1)
                    act.activation(key_hi[:, c, v:v + 4, :].rearrange("p a b -> p (a b)"), bank[6 + n % 2][:, :], ACT.Copy) \
                        .then_inc(s_act.sem, 1)
                    n += 1

            def normalise(j):
                act.wait_ge(raw_in.sem, raw_in.at(j, 16))
                act.wait_ge(sims_done.sem, sims_done.at(j, 0))
                for c in range(C):
                    last = act.activation(x_norm[:, c, :], x_raw[:, c, :], ACT.Identity,
                                          bias=bn[:, 1, c:c + 1], scale=bn[:, 0, c:c + 1])
                last.then_inc(xn_ready.sem, 1)

            def split_high(j):
                act.activation(x_hi[:, :, :], x_raw[:, :, :], ACT.Copy).then_inc(xh_ready.sem, 1)

            def exps(j, t):
                act.wait_ge(topk_done.sem, topk_done.at(j, t + 1))
                act.activation(expo[:, :, :], delta[:, :, :], ACT.Exp).then_inc(exp_done.sem, 1)

            def gelus(j):
                for g in range(NV // 2):
                    act.wait_ge(down_done.sem, down_done.at(j, g + 1))
                    act.activation(gated[:, 2 * g:2 * g + 2, :].rearrange("p v n -> p (v n)"), down_b[g % 2][:, :], ACT.Gelu) \
                        .then_inc(gelu_done.sem, 1)

            normalise(0)
            split_high(0)
            exps(0, 0)
            exps(0, 1)
            with act.Fori(0, BLOCKS - 1) as i:
                normalise(i + 1)
                gelus(i)
                split_high(i + 1)
                exps(i + 1, 0)
                exps(i + 1, 1)
            gelus(BLOCKS - 1)

        @block.vector
        def _(dve):
            n = 0
            dve.wait_ge(s_tr.sem, 6)
            dve.memset(rest2[:, :], 0.0).then_inc(s_dve.sem, 1)
            for c in range(C):
                for v in range(0, NV, 4):
                    dve.wait_ge(s_act.sem, 6 + n + 1)
                    lo = key_lo[:, c, v:v + 4, :].rearrange("p a b -> p (a b)")
                    hi = key_hi[:, c, v:v + 4, :].rearrange("p a b -> p (a b)").bitcast(F32)
                    dve.tensor_tensor(lo, bank[6 + n % 2][:, :], hi, ALU.subtract).then_inc(s_dve.sem, 1)
                    n += 1
            dve.wait_ge(consts.sem, 2)
            dve.wait_ge(zeroed.sem, 2)

            def choose(j, t, chain):
                dve.wait_ge(map_done.sem, map_done.at(j, t + 1 - 1))
                wait_apart(dve, sims_done.sem, sims_done.at(j, t + 1), passed.sem)
                for a in range(2):
                    for h in range(H):
                        last = dve.max(best[:, a, h, :], sim_b[a][:, h * K:(h + 1) * K])
                chain.link(last)
                chain.wait_apart(passed.sem)
                for a in range(2):
                    for h in range(H):
                        last = dve.max_index(best_at[:, a, h, :], best[:, a, h, :], sim_b[a][:, h * K:(h + 1) * K])
                last.then_inc(topk_read.sem, 1)
                chain.link(dve.tensor_tensor(pairs[:, :, :, :], best[:, 0, :, :].unsqueeze(3).to_broadcast([P, H, TOP, TOP]),
                                             best[:, 1, :, :].unsqueeze(2).to_broadcast([P, H, TOP, TOP]), ALU.add))
                chain.wait_apart(passed.sem)
                for h in range(H):
                    last = dve.max(top[:, h, :], pairs[:, h, :, :].rearrange("p a b -> p (a b)"))
                chain.link(last)
                chain.wait_apart(passed.sem)
                for h in range(H):
                    last = dve.max_index(top_at[:, h, :], top[:, h, :], pairs[:, h, :, :].rearrange("p a b -> p (a b)"))
                chain.link(last)
                dve.tensor_tensor(delta[:, :, :], top[:, :, :], top[:, :, 0:1].to_broadcast([P, H, TOP]), ALU.subtract)
                chain.wait()
                flat = top_at[:, :, :].rearrange("p h k -> p (h k)")
                dve.tensor_scalar(coords[:, 0, :], flat, 3, None, ALU.logical_shift_right)
                dve.tensor_scalar(coords[:, 1, :], flat, 7, None, ALU.bitwise_and).then_inc(topk_done.sem, 1)

            def settle(j, t, chain):
                dve.wait_ge(map_done.sem, map_done.at(j, t + 1))
                chain.link(dve.reduce_sum(expert[:, :, :].rearrange("p a b -> p (a b)"),
                                          hit[:, :, :, :, :].rearrange("p a h k i -> p (a h k) i"), axis=AXX))
                dve.wait_ge(exp_done.sem, exp_done.at(j, t + 1))
                chain.link(dve.reduce_sum(total[:, :], expo[:, :, :], axis=AXX))
                chain.wait()
                chain.link(dve.tensor_scalar(upper[:, :], expert[:, 1, :], float(NV), None, ALU.is_ge))
                chain.link(dve.reciprocal(share[:, :], total[:, :]))
                chain.wait()
                twice = [P, 2, PICKS]
                dve.scalar_tensor_tensor(cat[:, 0, :, :], expert[:, 0, :].unsqueeze(1).to_broadcast(twice), 2.0,
                                         upper[:, :].unsqueeze(1).to_broadcast(twice), ALU.mult, ALU.add)
                dve.scalar_tensor_tensor(cat[:, 1, :, :], upper[:, :].unsqueeze(1).to_broadcast(twice), -float(NV),
                                         expert[:, 1, :].unsqueeze(1).to_broadcast(twice), ALU.mult, ALU.add)
                for k in range(2):
                    last = dve.tensor_tensor(cat[:, 2, k, :].rearrange("p (h k) -> p h k", h=H), expo[:, :, :],
                                             share[:, :].unsqueeze(2).to_broadcast([P, H, TOP]), ALU.mult)
                last.then_inc(cat_ready.sem, 1)

            def take_picks(j, t, chain):
                dve.wait_ge(tr_done.sem, tr_done.at(j, t + 1))
                for r in range(2):
                    on = slice(64 * r, 64 * r + 64)
                    view = tr_b[on, 0:2 * P].rearrange("p (a n) -> p a n", a=2)
                    dve.tensor_copy(uv[on, :, :], view[:, :, 64 * r:64 * r + 64])
                    last = dve.tensor_copy(part[on, 0, :], tr_b[on, 2 * P + 64 * r:2 * P + 64 * r + 64])
                chain.link(last)
                chain.wait()
                for r in range(2):
                    on = slice(64 * r, 64 * r + 64)
                    last = dve.tensor_tensor(rest[on, :], tr_b[on, 2 * P + 64 * r:2 * P + 64 * r + 64], part[on, 0, :],
                                             ALU.subtract)
                chain.link(last)
                chain.wait()
                chain.link(dve.tensor_copy(part[:, 1, :], rest[:, :]))
                chain.wait()
                chain.link(dve.tensor_tensor(rest2[:, :], rest[:, :], part[:, 1, :], ALU.subtract))
                chain.wait()
                chain.link(dve.tensor_copy(part[:, 2, :], rest2[:, :]))

            def one_hots(j, t, chain):
                for h in range(2):
                    dve.wait_ge(w_done.sem, w_done.at(j, 8 * t + 4 * h + 4 - 8))
                    cols = slice(HALF * h, HALF * h + HALF)

                    def equal(out, n, which):
                        return dve.tensor_tensor(
                            out.rearrange("p u (a b) -> p u a b", b=4),
                            ramp[:, 0:n, :].unsqueeze(2).to_broadcast([P, n, HALF // 4, 4]),
                            uv[:, which, cols].rearrange("p (a b) -> p a b", b=4).unsqueeze(1).to_broadcast([P, n, HALF // 4, 4]),
                            ALU.is_equal)

                    chain.link(equal(hot_v[h][:, :, :], NV, 1))
                    equal(hot_u[h][:, :, :], P, 0)
                    chain.wait()
                    for r in range(2):
                        on = slice(64 * r, 64 * r + 64)
                        last = dve.tensor_tensor(weigh_v[h][on, :, r, :, :],
                                                 hot_v[h][on, :, :].unsqueeze(1).to_broadcast([64, 3, NV, HALF]),
                                                 part[on, :, cols].unsqueeze(2).to_broadcast([64, 3, NV, HALF]), ALU.mult)
                    last.then_inc(gen_ready.sem, 1)

            def gate(j, t):
                dve.wait_ge(gelu_done.sem, gelu_done.at(j, NV // 2))
                for q in range(8):
                    dve.wait_ge(w_done.sem, w_done.at(j, 8 * t + q + 1))
                    g = gated[:, :, t * P:(t + 1) * P].rearrange("p v (r m) -> p m r v", r=2)[:, 8 * q:8 * q + 8, :, :]
                    dve.tensor_tensor(g, g, w_b[q % 2][:, :].rearrange("p (m r v) -> p m r v", m=8, r=2), ALU.mult) \
                        .then_inc(h_done.sem, 1)

            def add_rows(j, t):
                if t == 0:
                    dve.wait_ge(rows_in.sem, rows_in.at(j, 16))
                dve.wait_ge(up_done.sem, up_done.at(j, t + 1))
                dve.tensor_tensor(x_rows[:, t, :], x_rows[:, t, :], up_b[:, 0:D], ALU.add).then_inc(x2_done.sem, 1)

            def turn(i, more, chain):
                one_hots(i, 0, chain)
                settle(i, 1, chain)
                if more:
                    choose(i + 1, 0, chain)
                take_picks(i, 1, chain)
                gate(i, 0)
                chain.wait()
                one_hots(i, 1, chain)
                if more:
                    settle(i + 1, 0, chain)
                add_rows(i, 0)
                gate(i, 1)
                if more:
                    choose(i + 1, 1, chain)
                add_rows(i, 1)
                if more:
                    take_picks(i + 1, 0, chain)
                    chain.wait()

            first = Chain(dve, dve_own.sem)
            choose(0, 0, first)
            settle(0, 0, first)
            choose(0, 1, first)
            take_picks(0, 0, first)
            first.wait()
            assert first.n == DVE_FIRST, first.n
            with dve.Fori(0, BLOCKS - 1) as i:
                chain = Chain(dve, dve_own.sem, i * DVE_TURN + DVE_FIRST)
                turn(i, True, chain)
                assert chain.n == DVE_TURN, chain.n
            turn(BLOCKS - 1, False, Chain(dve, dve_own.sem, (BLOCKS - 1) * DVE_TURN + DVE_FIRST))


def attend_latents(nc, ctx, x2_dram, wts, out_dram, cst):
    B, S, D = ctx.shape
    N = x2_dram.shape[0] // B
    INNER = wts["wq"].shape[1]
    H, C, T, CH = 8, D // P, N // P, INNER // P
    DH = INNER // H
    F = N + S
    SCALE = DH ** -0.5
    ident, neghalf = cst["ident"], cst["neghalf"]
    own = ExitStack()
    with own:
        def sb(name, shape, dt=F32):
            return own.enter_context(nc.sbuf_tensor(name, shape, dt))

        def sig(name, per=0, start=0):
            return Signal(own.enter_context(nc.semaphore(name)), per, start)

        score_b = [own.enter_context(nc.psum_tensor(f"c_score{i}", [P, 1024], F32)) for i in range(2)]
        turn_b = [own.enter_context(nc.psum_tensor(f"c_turn{i}", [P, 512], F32)) for i in range(2)]
        sum_b = [own.enter_context(nc.psum_tensor(f"c_sum{i}", [P, 512], F32)) for i in range(2)]
        pool4 = [score_b[i // 2][:, 512 * (i % 2):512 * (i % 2) + 512] for i in range(4)]

        names = ("wq", "wk", "wv")
        w_hi = {n: sb(f"c_{n}_hi", [P, C, INNER], F32R) for n in names}
        w_lo = {n: sb(f"c_{n}_lo", [P, C, INNER], F32R) for n in names}
        w_out = sb("c_w_out", [P, CH, D])
        ternary = sb("c_ternary", [P, C, D], F32R)
        affine = sb("c_affine", [P, 4, C])
        wscale = sb("c_wscale", [P, 3])
        ones = sb("c_ones", [P, P])
        ctx_k_hi = sb("c_ctx_k_hi", [P, CH, B * S], F32R)
        ctx_k_lo = sb("c_ctx_k_lo", [P, CH, B * S], F32R)
        ctx_v = sb("c_ctx_v", [S, B, INNER])
        xz = sb("c_xz", [P, T, D])
        xr = sb("c_xr", [P, T, D])
        z0 = sb("c_z0", [P, T, D])
        z1 = sb("c_z1", [P, T, D])
        zt = sb("c_zt", [P, C, N])
        z_hi = sb("c_z_hi", [P, C, N], F32R)
        z_lo = sb("c_z_lo", [P, C, N], F32R)
        q_hi = [sb(f"c_q_hi{e}", [P, CH, N], F32R) for e in range(2)]
        q_lo = [sb(f"c_q_lo{e}", [P, CH, N], F32R) for e in range(2)]
        k_hi = sb("c_k_hi", [P, CH, N], F32R)
        k_lo = sb("c_k_lo", [P, CH, N], F32R)
        v_rows = sb("c_v_rows", [P, T, INNER])
        v_ctx = sb("c_v_ctx", [S, INNER])
        probs = [sb(f"c_probs{e}", [P, T, F]) for e in range(2)]
        probs_t = [sb(f"c_probs_t{e}", [P, T + 1, N]) for e in range(2)]
        heads = sb("c_heads", [P, CH, N])
        x3 = sb("c_x3", [P, T, D])
        nmax = sb("c_nmax", [P, H * T])
        sums = sb("c_sums", [P, H * T])
        inv = sb("c_inv", [P, H * T])
        stats = sb("c_stats", [P, T, 6])
        mean_var = sb("c_mean_var", [P, 3, T, 2])
        var_eps = sb("c_var_eps", [P, 3, T])
        rstd = sb("c_rstd", [P, 3, T])

        ld_w = {n: sig(f"c_ld_{n}") for n in names}
        ld_misc, ld_ctx = sig("c_ld_misc"), sig("c_ld_ctx")
        s_act, s_dve, s_pe, s_pool = sig("c_s_act"), sig("c_s_dve"), sig("c_s_pe"), sig("c_s_pool")
        passed = sig("c_passed")
        xz_in, xr_in = sig("c_xz_in", 16), sig("c_xr_in", 16)
        var_z, rs_z, z0_done, z1_done = sig("c_var_z", 2), sig("c_rs_z", 2), sig("c_z0", 1, 1), sig("c_z1", 1)
        var_x, rs_x, r3_done = sig("c_var_x", 1), sig("c_rs_x", 1), sig("c_r3", 1)
        zhi_done, zlo_done = sig("c_zhi", 1), sig("c_zlo", 1)
        proj_done, proj_act, proj_dve = sig("c_proj", 14), sig("c_proj_act", 14), sig("c_proj_dve", 8)
        vctx_done = sig("c_vctx", 1)
        score_done, max_done, exp_done = sig("c_score", 32), sig("c_max", 32), sig("c_exp", 32, 2)
        inv_done, norm_done = sig("c_inv", 32), sig("c_norm", 32)
        turned, ev_act, ev_dve = sig("c_turned", 40, 10), sig("c_ev_act", 16, 2), sig("c_ev_dve", 24, 2)
        av_done, heads_done = sig("c_av", 4, 4), sig("c_heads", 4, 1)
        wout_done, x3_done = sig("c_wout", 2), sig("c_x3", 2, 2)
        ft_done, f_hi, f_lo = sig("c_ft", 2), sig("c_fhi", 2), sig("c_flo", 2, 2)
        ff_done, y_done, kept = sig("c_ff", 2), sig("c_y", 2, 2), sig("c_kept", 16, 16)
        SETUP_DVE, SETUP_ACT = 12 + CH, 7 + CH + B
        dve_own, pool_own = sig("c_dve_own"), sig("c_pool_own")
        block = own.enter_context(nc.Block())
        w_raw = {"wq": probs[0][:, :, :].rearrange("p a b -> p (a b)")[:, 0:C * INNER].rearrange("p (c n) -> p c n", c=C),
                 "wk": probs[1][:, :, :].rearrange("p a b -> p (a b)")[:, 0:C * INNER].rearrange("p (c n) -> p c n", c=C),
                 "wv": probs_t[0][:, 0:2, :]}
        ctx_rows, lin_rows, tern_rows, above = xr[:, :, :], x3[:, 0:2, :], z0[:, 0:2, :], z0[:, 2:4, :]
        MEDIA_W, MEDIA_B, LAT_W, LAT_B = range(4)
        slots = [(0, 1), (2,), (3,), (4,)]

        def ev_wait(eng, j, n):
            turn, n = (-1, n + 5 * H) if n < 0 else (0, n)
            hh, fc = n // 5, n % 5
            if fc in (1, 3):
                eng.wait_ge(ev_act.sem, ev_act.at(j, 2 * hh + (fc + 1) // 2 + 16 * turn))
            else:
                eng.wait_ge(ev_dve.sem, ev_dve.at(j, 3 * hh + fc // 2 + 1 + 24 * turn))

        @block.sync
        def _(sp):
            sp.dma_start(ctx_rows, ctx.rearrange("b s d -> (b s) d").rearrange("(t p) d -> p t d", p=P)).then_inc(ld_ctx.sem, 16)
            for k, name in enumerate(("media_w", "media_b", "lat_w", "lat_b")):
                sp.dma_start(affine[:, k, :], wts[name].rearrange("(c p) -> p c", p=P),
                             allow_slow_non_contiguous=True).then_inc(ld_misc.sem, 16)
            sp.dma_start(lin_rows, wts["lin"].rearrange("(t p) d -> p t d", p=P)).then_inc(ld_misc.sem, 16)
            sp.dma_start(w_out[:, :, :], wts["wout"].rearrange("(c p) d -> p c d", p=P)).then_inc(ld_misc.sem, 16)
            for n in names:
                sp.dma_start(w_raw[n], wts[n].rearrange("(c p) n -> p c n", p=P)).then_inc(ld_w[n].sem, 16)

            def load_z(j):
                sp.wait_ge(z0_done.sem, z0_done.at(j, 0))
                sp.dma_start(xz[:, :, :], x2_dram[bass.ds(j * N, N), :].rearrange("(t p) d -> p t d", p=P)).then_inc(xz_in.sem, 16)

            def rows_through(j):
                sp.wait_ge(x3_done.sem, x3_done.at(j, 0))
                sp.dma_start(xr[:, :, :], x2_dram[bass.ds(j * N, N), :].rearrange("(t p) d -> p t d", p=P)).then_inc(xr_in.sem, 16)

            def store(j):
                sp.wait_ge(y_done.sem, y_done.at(j, 2))
                sp.dma_start(out_dram[bass.ds(j * N, N), :].rearrange("(t p) d -> p t d", p=P), x3[:, :, :]).then_inc(kept.sem, 16)

            load_z(0)
            sp.wait_ge(s_dve.sem, SETUP_DVE)
            with sp.Fori(0, B - 1) as i:
                rows_through(i)
                load_z(i + 1)
                store(i)
            rows_through(B - 1)
            store(B - 1)
            sp.wait_ge(kept.sem, kept.at(B, 0))

        @block.gpsimd
        def _(pool):
            chain = Chain(pool, s_pool.sem)
            chain.link(pool.memset(ones[:, :], 1.0))
            for e in range(2):
                for q in (q_hi[e], q_lo[e]):
                    chain.wait()
                    chain.link(pool.memset(q[64 * (1 - e):64 * (1 - e) + 64, :, :].bitcast(U32), 0))
            for s in (z0_done, exp_done, turned, ev_act, ev_dve, av_done, heads_done, x3_done, f_lo, y_done, kept):
                pool.sem_inc(s.sem, s.start)

            def rsqrt(chain, var, rs, j, k, which):
                wait_apart(pool, var.sem, var.at(j, k), passed.sem)
                chain.link(pool.tensor_scalar(var_eps[:, which, :], mean_var[:, which, :, 1], EPS, None, ALU.add))
                chain.wait()
                pool.tensor_tensor(rstd[:, which, :], var_eps[:, which, :], neghalf[:, 0:T], ALU.pow).then_inc(rs.sem, 1)

            pool.wait_ge(s_dve.sem, 2)
            chain.link(pool.tensor_scalar(var_eps[:, 0, :], mean_var[:, 0, :, 1], EPS, None, ALU.add))
            chain.wait()
            chain.link(pool.tensor_tensor(rstd[:, 0, :], var_eps[:, 0, :], neghalf[:, 0:T], ALU.pow))

            def values_of_context(j):
                wait_apart(pool, av_done.sem, av_done.at(j, 0), passed.sem)
                pool.tensor_copy(v_ctx[:, :], ctx_v[:, bass.ds(j, 1), :].rearrange("p a n -> p (a n)")).then_inc(vctx_done.sem, 1)

            def turn(j, more, chain):
                for hh in range(H):
                    for t in range(T):
                        k = T * hh + t
                        wait_apart(pool, inv_done.sem, inv_done.at(j, k + 1), passed.sem)
                        p = probs[hh % 2][:, t, :]
                        pool.tensor_scalar(p, p, inv[:, k:k + 1], None, ALU.mult).then_inc(norm_done.sem, 1)
                    if more and hh == 3:
                        rsqrt(chain, var_z, rs_z, j + 1, 1, 0)
                        rsqrt(chain, var_z, rs_z, j + 1, 2, 1)
                if more:
                    values_of_context(j + 1)
                rsqrt(chain, var_x, rs_x, j, 1, 2)

            pool.wait_ge(s_act.sem, SETUP_ACT)
            first = Chain(pool, pool_own.sem)
            rsqrt(first, var_z, rs_z, 0, 1, 0)
            rsqrt(first, var_z, rs_z, 0, 2, 1)
            values_of_context(0)
            with pool.Fori(0, B - 1) as i:
                turn(i, True, Chain(pool, pool_own.sem, i * 3 + 2))
            turn(B - 1, False, Chain(pool, pool_own.sem, (B - 1) * 3 + 2))

        @block.tensor
        def _(pe):
            n = [0]

            def setup_step(last):
                last.then_inc(s_pe.sem, 1)
                n[0] += 1

            pe.wait_ge(s_dve.sem, 3)
            for c in range(C):
                for t in range(B * S // P):
                    last = pe.transpose(turn_b[c][:, t * P:(t + 1) * P], z1[:, t, c * P:(c + 1) * P], ident[:, :])
                setup_step(last)
            pe.wait_ge(s_pool.sem, 5)
            pe.wait_ge(s_dve.sem, 4)
            setup_step(pe.matmul(sum_b[0][:, 0:1], ones[:, :], wscale[:, 0:1], start=True, stop=True))
            pe.wait_ge(s_dve.sem, 8)
            for c in range(C):
                for t in range(D // P):
                    last = pe.transpose(sum_b[c][:, t * P:(t + 1) * P], tern_rows[:, t, c * P:(c + 1) * P], ident[:, :])
                setup_step(last)
            pe.wait_ge(s_dve.sem, 12)
            for c in range(CH):
                for d in range(C):
                    last = three_pass(pe, pool4[c], w_hi["wk"][:, d, c * P:(c + 1) * P], w_lo["wk"][:, d, c * P:(c + 1) * P],
                                      z_hi[:, d, :], z_lo[:, d, :], d == 0, d == C - 1)
                setup_step(last)
            for b in range(B):
                if b < 4:
                    pe.wait_ge(s_dve.sem, 12 + b + 1)
                else:
                    pe.wait_ge(s_act.sem, SETUP_ACT - B + b - 4 + 1)
                for d in range(C):
                    last = three_pass(pe, pool4[b % 4][0:S, :], z_hi[:, d, b * S:(b + 1) * S], z_lo[:, d, b * S:(b + 1) * S],
                                      w_hi["wv"][:, d, :], w_lo["wv"][:, d, :], d == 0, d == C - 1)
                setup_step(last)
            pe.wait_ge(s_act.sem, SETUP_ACT)

            def project(j):
                pe.wait_ge(z1_done.sem, z1_done.at(j, 1))
                pe.wait_ge(exp_done.sem, exp_done.at(j, 0))
                for c in range(C):
                    for t in range(T):
                        last = pe.transpose(pool4[c][:, t * P:(t + 1) * P], z1[:, t, c * P:(c + 1) * P], ident[:, :])
                    last.then_inc(proj_done.sem, 1)
                pe.wait_ge(zlo_done.sem, zlo_done.at(j, 1))
                for u in range(2, 14):
                    if u in (4, 5):
                        pe.wait_ge(proj_act.sem, proj_act.at(j, u - 4 + 1))
                    elif u > 5:
                        pe.wait_ge(proj_dve.sem, proj_dve.at(j, u - 6 + 1))
                    o = pool4[u % 4]
                    for d in range(C):
                        if u < 10:
                            name, c = ("wq", u - 2) if u < 6 else ("wk", u - 6)
                            cols = slice(c * P, (c + 1) * P)
                            last = three_pass(pe, o, w_hi[name][:, d, cols], w_lo[name][:, d, cols],
                                              z_hi[:, d, :], z_lo[:, d, :], d == 0, d == C - 1)
                        else:
                            cols = slice((u - 10) * P, (u - 9) * P)
                            last = three_pass(pe, o, z_hi[:, d, cols], z_lo[:, d, cols],
                                              w_hi["wv"][:, d, :], w_lo["wv"][:, d, :], d == 0, d == C - 1)
                    last.then_inc(proj_done.sem, 1)

            def scores(j, hh, t):
                k = T * hh + t
                if k >= 2:
                    pe.wait_ge(exp_done.sem, exp_done.at(j, k + 1 - 2))
                c, e = hh // 2, hh % 2
                cols = slice(t * P, (t + 1) * P)
                for o, hi, lo in ((score_b[k % 2][:, 0:N], k_hi[:, c, :], k_lo[:, c, :]),
                                  (score_b[k % 2][:, N:F], ctx_k_hi[:, c, bass.ds(j * S, S)], ctx_k_lo[:, c, bass.ds(j * S, S)])):
                    last = three_pass(pe, o, q_hi[e][:, c, cols], q_lo[e][:, c, cols], hi, lo, True, True)
                last.then_inc(score_done.sem, 1)

            def turn_probs(j, hh, fc):
                n = 5 * hh + fc
                if fc == 0:
                    pe.wait_ge(norm_done.sem, norm_done.at(j, T * hh + T))
                ev_wait(pe, j, n - 2)
                if n < 2:
                    pe.wait_ge(f_lo.sem, f_lo.at(j, n + 1 - 2))
                w = P if fc < T else S
                if w < P:
                    pe.sem_inc(passed.sem, 1)
                for t in range(T):
                    last = pe.transpose(turn_b[n % 2][0:w, t * P:(t + 1) * P], probs[hh % 2][:, t, fc * P:fc * P + w], ident[:, :])
                last.then_inc(turned.sem, 1)

            def weigh_values(j, c):
                for n in (5 * (2 * c + 1) + 3, 5 * (2 * c + 1) + 4):
                    ev_wait(pe, j, n)
                pe.wait_ge(heads_done.sem, heads_done.at(j, c + 1 - 1))
                if c == 0:
                    pe.wait_ge(vctx_done.sem, vctx_done.at(j, 1))
                    pe.wait_ge(y_done.sem, y_done.at(j, 1 - 2))
                for fc in range(T + 1):
                    for e in range(2):
                        cols = slice((2 * c + e) * DH, (2 * c + e + 1) * DH)
                        v = v_rows[:, fc, cols] if fc < T else v_ctx[:, cols]
                        w = P if fc < T else S
                        last = pe.matmul(sum_b[0][DH * e:DH * e + DH, :], v, probs_t[e][0:w, fc, :],
                                         start=(fc == 0), stop=(fc == T))
                last.then_inc(av_done.sem, 1)

            def attend(j):
                pe.wait_ge(proj_act.sem, proj_act.at(j, 14))
                pe.wait_ge(proj_dve.sem, proj_dve.at(j, 8))
                for hh in range(H + 1):
                    for t in range(T):
                        if hh < H:
                            scores(j, hh, t)
                        if hh > 0:
                            for fc in slots[t]:
                                turn_probs(j, hh - 1, fc)
                    if hh > 0 and hh % 2 == 0:
                        weigh_values(j, hh // 2 - 1)

            def out_product(j):
                pe.wait_ge(heads_done.sem, heads_done.at(j, CH))
                pe.wait_ge(y_done.sem, y_done.at(j, 0))
                for half in range(2):
                    for t in (2 * half, 2 * half + 1):
                        for c in range(CH):
                            last = pe.matmul(sum_b[half][:, (t % 2) * D:(t % 2 + 1) * D], heads[:, c, t * P:(t + 1) * P],
                                             w_out[:, c, :], start=(c == 0), stop=(c == CH - 1))
                    last.then_inc(wout_done.sem, 1)

            def ternary_product(j):
                pe.wait_ge(r3_done.sem, r3_done.at(j, 1))
                for c in range(C):
                    ev_wait(pe, j, 5 * H - 2 + c)
                    for t in range(T):
                        last = pe.transpose(turn_b[c][:, t * P:(t + 1) * P], z0[:, t, c * P:(c + 1) * P], ident[:, :])
                    last.then_inc(ft_done.sem, 1)
                pe.wait_ge(f_lo.sem, f_lo.at(j, 2))
                for half in range(2):
                    for t in (2 * half, 2 * half + 1):
                        for c in range(C):
                            o = sum_b[half][:, (t % 2) * D:(t % 2 + 1) * D]
                            pe.matmul(o, z_lo[:, c, t * P:(t + 1) * P], ternary[:, c, :], start=(c == 0), stop=False)
                            last = pe.matmul(o, z_hi[:, c, t * P:(t + 1) * P], ternary[:, c, :], start=False, stop=(c == C - 1))
                    last.then_inc(ff_done.sem, 1)

            project(0)
            with pe.Fori(0, B - 1) as i:
                attend(i)
                out_product(i)
                project(i + 1)
                ternary_product(i)
            attend(B - 1)
            out_product(B - 1)
            ternary_product(B - 1)

        @block.scalar
        def _(act):
            for n in names:
                act.wait_ge(ld_w[n].sem, 16)
                act.activation(w_hi[n][:, :, :], w_raw[n], ACT.Copy).then_inc(s_act.sem, 1)
            act.wait_ge(ld_misc.sem, 96)
            act.wait_ge(s_pe.sem, 2)
            for c in range(C):
                last = act.activation(zt[:, c, :], turn_b[c][:, :], ACT.Identity,
                                      bias=affine[:, MEDIA_B, c:c + 1], scale=affine[:, MEDIA_W, c:c + 1])
            last.then_inc(s_act.sem, 1)
            act.wait_ge(s_act.sem, 4)
            act.activation(z_hi[:, :, :], zt[:, :, :], ACT.Copy).then_inc(s_act.sem, 1)
            for c in range(C):
                act.wait_ge(s_pe.sem, 4 + c)
                act.activation(ternary[:, c, :], sum_b[c][:, 0:D], ACT.Copy, scale=-1.0).then_inc(s_act.sem, 1)
            for c in range(CH):
                act.wait_ge(s_pe.sem, 6 + c)
                act.activation(ctx_k_hi[:, c, :], pool4[c], ACT.Copy).then_inc(s_act.sem, 1)
            for b in range(B):
                act.wait_ge(s_pe.sem, 10 + b)
                act.activation(ctx_v[:, b, :], pool4[b % 4][0:S, :], ACT.Copy).then_inc(s_act.sem, 1)

            def project(j):
                for c in range(C):
                    act.wait_ge(proj_done.sem, proj_done.at(j, c + 1))
                    act.activation(zt[:, c, :], pool4[c], ACT.Identity, bias=affine[:, LAT_B, c:c + 1],
                                   scale=affine[:, LAT_W, c:c + 1]).then_inc(proj_act.sem, 1)
                act.wait_ge(proj_act.sem, proj_act.at(j, 2))
                act.activation(z_hi[:, :, :], zt[:, :, :], ACT.Copy).then_inc(zhi_done.sem, 1)
                for u in range(2, 14):
                    act.wait_ge(proj_done.sem, proj_done.at(j, u + 1))
                    o = pool4[u % 4]
                    if u < 6:
                        act.activation(q_hi[0][0:64, u - 2, :], o[0:64, :], ACT.Copy, scale=SCALE)
                        last = act.activation(q_hi[1][64:128, u - 2, :], o[64:128, :], ACT.Copy, scale=SCALE)
                    elif u < 10:
                        last = act.activation(k_hi[:, u - 6, :], o, ACT.Copy)
                    else:
                        last = act.activation(v_rows[:, u - 10, :], o, ACT.Copy)
                    last.then_inc(proj_act.sem, 1)

            def take_chunk(j, hh, fc):
                n = 5 * hh + fc
                act.wait_ge(turned.sem, turned.at(j, n + 1))
                if fc == 1:
                    act.wait_ge(av_done.sem, av_done.at(j, hh // 2))
                act.activation(probs_t[hh % 2][:, fc, :], turn_b[n % 2][:, :], ACT.Copy).then_inc(ev_act.sem, 1)

            def attend(j):
                for hh in range(H + 1):
                    for t in range(T):
                        if hh < H:
                            k = T * hh + t
                            if t == 0:
                                act.wait_ge(turned.sem, turned.at(j, 5 * hh + 5 - 10))
                            act.wait_ge(max_done.sem, max_done.at(j, k + 1))
                            act.activation(probs[hh % 2][:, t, :], score_b[k % 2][:, 0:F], ACT.Exp, bias=nmax[:, k:k + 1],
                                           accum_out=sums[:, k:k + 1]).then_inc(exp_done.sem, 1)
                        if hh > 0:
                            for fc in slots[t]:
                                if fc in (1, 3):
                                    take_chunk(j, hh - 1, fc)
                    if hh > 0 and hh % 2 == 0:
                        c = hh // 2 - 1
                        act.wait_ge(av_done.sem, av_done.at(j, c + 1))
                        act.activation(heads[:, c, :], sum_b[0][:, :], ACT.Copy).then_inc(heads_done.sem, 1)

            def split_rows(j):
                for c in range(C):
                    act.wait_ge(ft_done.sem, ft_done.at(j, c + 1))
                    act.activation(z_hi[:, c, :], turn_b[c][:, :], ACT.Copy).then_inc(f_hi.sem, 1)

            project(0)
            with act.Fori(0, B - 1) as i:
                attend(i)
                project(i + 1)
                split_rows(i)
            attend(B - 1)
            split_rows(B - 1)

        @block.vector
        def _(dve):
            def moments(chain, src, which):
                for t in range(T):
                    last = dve.bn_stats(stats[:, t, :], src[:, t, :])
                chain.link(last)
                chain.wait_apart(passed.sem)
                for t in range(T):
                    last = dve.bn_aggr(mean_var[:, which, t, :], stats[:, t, :])
                return last

            def normalise(dst, src, which):
                for t in range(T):
                    last = dve.tensor_scalar(dst[:, t, :], src[:, t, :], mean_var[:, which, t, 0:1], rstd[:, which, t:t + 1],
                                             ALU.subtract, ALU.mult)
                return last

            chain = Chain(dve, s_dve.sem)
            dve.wait_ge(ld_ctx.sem, 16)
            chain.link(moments(chain, ctx_rows, 0))
            dve.wait_ge(s_pool.sem, 7)
            dve.wait_ge(s_dve.sem, 2)
            chain.link(normalise(z1, ctx_rows, 0))
            dve.wait_ge(ld_misc.sem, 96)
            chain.link(dve.tensor_reduce(out=wscale[:, 0:1], in_=lin_rows.rearrange("p a b -> p (a b)"), op=ALU.add, axis=AXX,
                                         apply_absolute_value=True))
            dve.wait_ge(s_pe.sem, 3)
            chain.link(dve.tensor_scalar(wscale[:, 1:2], sum_b[0][:, 0:1], 1.0 / (D * D), EPS, ALU.mult, ALU.max))
            chain.wait()
            chain.link(dve.tensor_scalar(wscale[:, 2:3], wscale[:, 1:2], -0.5, None, ALU.mult))
            chain.wait()
            chain.link(dve.tensor_scalar(above, lin_rows, -1.0, wscale[:, 2:3], ALU.mult, ALU.is_lt))
            chain.wait()
            chain.link(dve.scalar_tensor_tensor(tern_rows, lin_rows, wscale[:, 2:3], above, ALU.is_lt, ALU.subtract))
            for k, n in enumerate(names):
                dve.wait_ge(s_act.sem, k + 1)
                chain.link(dve.tensor_tensor(w_lo[n][:, :, :], w_raw[n], w_hi[n][:, :, :].bitcast(F32), ALU.subtract))
            dve.wait_ge(s_act.sem, 5)
            chain.link(dve.tensor_tensor(z_lo[:, :, :], zt[:, :, :], z_hi[:, :, :].bitcast(F32), ALU.subtract))
            for c in range(CH):
                dve.wait_ge(s_act.sem, 7 + c + 1)
                chain.link(dve.tensor_tensor(ctx_k_lo[:, c, :], pool4[c], ctx_k_hi[:, c, :].bitcast(F32), ALU.subtract))
            assert chain.n == SETUP_DVE, chain.n

            def prepare(j, chain):
                dve.wait_ge(xz_in.sem, xz_in.at(j, 16))
                moments(chain, xz, 0).then_inc(var_z.sem, 1)
                dve.wait_ge(rs_z.sem, rs_z.at(j, 1))
                dve.wait_ge(var_z.sem, var_z.at(j, 1))
                normalise(z0, xz, 0).then_inc(z0_done.sem, 1)
                dve.wait_ge(z0_done.sem, z0_done.at(j, 1))
                moments(chain, z0, 1).then_inc(var_z.sem, 1)
                dve.wait_ge(rs_z.sem, rs_z.at(j, 2))
                dve.wait_ge(var_z.sem, var_z.at(j, 2))
                normalise(z1, z0, 1).then_inc(z1_done.sem, 1)

            def project(j):
                dve.wait_ge(zhi_done.sem, zhi_done.at(j, 1))
                dve.tensor_tensor(z_lo[:, :, :], zt[:, :, :], z_hi[:, :, :].bitcast(F32), ALU.subtract).then_inc(zlo_done.sem, 1)
                for u in range(2, 10):
                    dve.wait_ge(proj_act.sem, proj_act.at(j, u + 1))
                    o = pool4[u % 4]
                    if u < 6:
                        for e in range(2):
                            on = slice(64 * e, 64 * e + 64)
                            last = dve.scalar_tensor_tensor(q_lo[e][on, u - 2, :], o[on, :], SCALE,
                                                            q_hi[e][on, u - 2, :].bitcast(F32), ALU.mult, ALU.subtract)
                    else:
                        last = dve.tensor_tensor(k_lo[:, u - 6, :], o, k_hi[:, u - 6, :].bitcast(F32), ALU.subtract)
                    last.then_inc(proj_dve.sem, 1)

            def invert(j, k):
                dve.wait_ge(exp_done.sem, exp_done.at(j, k + 1))
                dve.reciprocal(inv[:, k:k + 1], sums[:, k:k + 1]).then_inc(inv_done.sem, 1)

            def take_chunk(j, hh, fc):
                n = 5 * hh + fc
                dve.wait_ge(turned.sem, turned.at(j, n + 1))
                if fc == 0:
                    dve.wait_ge(av_done.sem, av_done.at(j, hh // 2))
                w = P if fc < T else S
                dve.tensor_copy(probs_t[hh % 2][0:w, fc, :], turn_b[n % 2][0:w, :]).then_inc(ev_dve.sem, 1)

            def attend(j, more, chain):
                for hh in range(H + 1):
                    for t in range(T):
                        k = T * hh + t
                        if hh < H:
                            dve.wait_ge(score_done.sem, score_done.at(j, k + 1))
                            dve.tensor_reduce(out=nmax[:, k:k + 1], in_=score_b[k % 2][:, 0:F], op=ALU.max, axis=AXX,
                                              negate=True).then_inc(max_done.sem, 1)
                        if 0 < k <= T * H:
                            invert(j, k - 1)
                        if hh > 0:
                            for fc in slots[t]:
                                if fc not in (1, 3):
                                    take_chunk(j, hh - 1, fc)
                    if more and hh == 4:
                        prepare(j + 1, chain)

            def add_attention(j, chain):
                dve.wait_ge(xr_in.sem, xr_in.at(j, 16))
                dve.wait_ge(kept.sem, kept.at(j, 0))
                for half in range(2):
                    dve.wait_ge(wout_done.sem, wout_done.at(j, half + 1))
                    dve.tensor_tensor(x3[:, 2 * half:2 * half + 2, :], xr[:, 2 * half:2 * half + 2, :],
                                      sum_b[half][:, :].rearrange("p (t d) -> p t d", t=2), ALU.add).then_inc(x3_done.sem, 1)
                dve.wait_ge(x3_done.sem, x3_done.at(j, 2))
                moments(chain, x3, 2).then_inc(var_x.sem, 1)
                dve.wait_ge(rs_x.sem, rs_x.at(j, 1))
                dve.wait_ge(var_x.sem, var_x.at(j, 1))
                normalise(z0, x3, 2).then_inc(r3_done.sem, 1)

            def finish(j):
                for c in range(C):
                    dve.wait_ge(f_hi.sem, f_hi.at(j, c + 1))
                    dve.tensor_tensor(z_lo[:, c, :], turn_b[c][:, :], z_hi[:, c, :].bitcast(F32), ALU.subtract).then_inc(f_lo.sem, 1)
                for half in range(2):
                    dve.wait_ge(ff_done.sem, ff_done.at(j, half + 1))
                    x = x3[:, 2 * half:2 * half + 2, :].rearrange("p t d -> p (t d)")
                    dve.scalar_tensor_tensor(x, sum_b[half][:, :], wscale[:, 1:2], x, ALU.mult, ALU.add).then_inc(y_done.sem, 1)

            first = Chain(dve, dve_own.sem)
            prepare(0, first)
            project(0)
            with dve.Fori(0, B - 1) as i:
                chain = Chain(dve, dve_own.sem, i * 3 + 2)
                attend(i, True, chain)
                add_attention(i, chain)
                project(i + 1)
                finish(i)
                assert chain.n == 3, chain.n
            chain = Chain(dve, dve_own.sem, (B - 1) * 3 + 2)
            attend(B - 1, False, chain)
            add_attention(B - 1, chain)
            finish(B - 1)


def build(nc, x, ctx, gamma, beta, w_q, keys, key_in, key_out, media_w, media_b, lat_w, lat_b, wq, wk, wv, wout, lin, out):
    B, N, D = x.shape
    with ExitStack() as whole:
        ident = whole.enter_context(nc.sbuf_tensor("ident", [P, P], F32))
        neghalf = whole.enter_context(nc.sbuf_tensor("neghalf", [P, 8], F32))
        bn = whole.enter_context(nc.sbuf_tensor("bn", [P, 2, D // P], F32))
        cst = {"ident": ident, "neghalf": neghalf, "bn": bn, "gamma": gamma, "beta": beta}
        x1 = nc.dram_tensor("x1_rows", (B, N, D), F32).ap()
        xt = nc.dram_tensor("x1_norm_t", (D // P, P, B * N), F32).ap()
        x2 = nc.dram_tensor("x2_rows", (B * N, D), F32).ap()
        attend_context(nc, x, ctx, x1, xt, cst)
        retrieve_experts(nc, xt, x1.rearrange("b n d -> (b n) d"), w_q, keys, key_in, key_out, x2, cst)
        wts = {"media_w": media_w, "media_b": media_b, "lat_w": lat_w, "lat_b": lat_b,
               "wq": wq, "wk": wk, "wv": wv, "wout": wout, "lin": lin}
        attend_latents(nc, ctx, x2, wts, out.rearrange("b n d -> (b n) d"), cst)


_INS = ["x", "ctx_1024", "L0_ffn_gamma", "L0_ffn_beta", "L0_ffn_w_q", "L0_ffn_keys", "L0_ffn_key_in", "L0_ffn_key_out",
        "L1_xattn_ln_media_w", "L1_xattn_ln_media_b", "L1_xattn_ln_lat_w", "L1_xattn_ln_lat_b",
        "L1_xattn_Wq", "L1_xattn_Wk", "L1_xattn_Wv", "L1_xattn_Wout", "L1_ffn_weight"]
_OUTS = [((8, 512, 256), "float32")]


def kernel(**inputs):
    import numpy as _np
    import concourse.bacc as _bacc
    from concourse import mybir as _mybir
    from concourse.bass_utils import run_bass_kernel_spmd as _run

    nc = _bacc.Bacc("TRN2", target_bir_lowering=False, num_devices=1)
    arrays, args = {}, []
    for name in _INS:
        a = _np.ascontiguousarray(inputs[name])
        arrays[f"in_{name}_dram"] = a
        args.append(nc.dram_tensor(f"in_{name}_dram", a.shape, _mybir.dt.from_np(a.dtype), kind="ExternalInput").ap())
    for i, (shape, dtype) in enumerate(_OUTS):
        dt = _mybir.dt.from_np(_np.dtype(dtype))
        args.append(nc.dram_tensor(f"out_{i}_dram", shape, dt, kind="ExternalOutput").ap())
    build(nc, *args)
    r = _run(nc, [arrays], core_ids=[0])
    got = tuple(r.results[0][f"out_{i}_dram"] for i in range(len(_OUTS)))
    return got if len(got) > 1 else got[0]
```

```python
import concourse.bass as bass
from concourse import mybir
from contextlib import ExitStack

F32 = mybir.dt.float32
F32R = mybir.dt.float32r
BF16 = mybir.dt.bfloat16
U32 = mybir.dt.uint32
ALU = mybir.AluOpType
ACT = mybir.ActivationFunctionType
AXX = mybir.AxisListType.X
P = 128
EPS = 1e-5


class Signal:

    def __init__(self, sem, per, start=0):
        self.sem, self.per, self.start = sem, per, start

    def at(self, i, k):
        return i * self.per + (self.start + k)


class Chain:

    def __init__(self, eng, sem, base=0):
        self.eng, self.sem, self.base, self.n = eng, sem, base, 0

    def link(self, ins):
        ins.then_inc(self.sem, 1)
        self.n += 1
        return self.n

    def wait(self, k=None):
        self.eng.wait_ge(self.sem, self.base + (self.n if k is None else k))

    def wait_apart(self, passed):
        wait_apart(self.eng, self.sem, self.base + self.n, passed)


def three_pass(pe, out, w_hi, w_lo, x_hi, x_lo, start, stop):
    pe.matmul(out, w_lo, x_hi, start=start, stop=False)
    pe.matmul(out, w_hi, x_lo, start=False, stop=False)
    return pe.matmul(out, w_hi, x_hi, start=False, stop=stop)


def wait_apart(eng, sem, value, passed):
    eng.wait_ge(sem, value)
    eng.sem_inc(passed, 1)


def attend_context(nc, x, ctx, x1_dram, xt_dram, cst):
    B, N, D = x.shape
    S = ctx.shape[1]
    T, C = N // P, D // P
    PAIRS = D // 32
    ident, neghalf, bn_out = cst["ident"], cst["neghalf"], cst["bn"]
    own = ExitStack()
    with own:
        def sb(name, shape, dt=F32):
            return own.enter_context(nc.sbuf_tensor(name, shape, dt))

        def two(name, shape, dt=F32):
            return [sb(f"{name}{p}", shape, dt) for p in range(2)]

        def sig(name, per=0, start=0):
            return Signal(own.enter_context(nc.semaphore(name)), per, start)

        bank = [own.enter_context(nc.psum_tensor(f"a_bank{i}", [P, 512], F32)) for i in range(8)]
        trans, score, value, back_b = bank[0:2], bank[2:4], bank[4:6], bank[6:8]

        ctx_rows = sb("a_ctx_rows", [P, B * S // P, D])
        ctx_t = sb("a_ctx_t", [P, C, B * S])
        ctx_twice = sb("a_ctx_twice", [P, B, D])
        mask_k = sb("a_mask_k", [P, 8])
        mask_v = sb("a_mask_v", [P, PAIRS, 2, 16])
        vals = two("a_vals", [P, D])
        keys_f = sb("a_keys_f", [P, 8, S])
        keys_hi, keys_lo = two("a_keys_hi", [P, C, 8, S], F32R), two("a_keys_lo", [P, C, 8, S], F32R)
        xa, xr = sb("a_xa", [P, T, D]), sb("a_xr", [P, T, D])
        rows, rows1 = sb("a_rows", [P, T, D]), sb("a_rows1", [P, T, D])
        q_hi, q_lo = sb("a_q_hi", [P, C, N], F32R), sb("a_q_lo", [P, C, N], F32R)
        acts = two("a_acts", [P, PAIRS, N])
        attn_t = sb("a_attn_t", [P, C, N])
        x1 = sb("a_x1", [P, T, D])
        xt = sb("a_xt", [P, C, N])
        stats = sb("a_stats", [P, T, 6])
        mean_var, var_eps, rstd = two("a_mean_var", [P, T, 2]), two("a_var_eps", [P, T]), two("a_rstd", [P, T])
        bn_stats = sb("a_bn_stats", [P, C, B, 6])
        bn_mv = sb("a_bn_mv", [P, C, 2])
        bn_ve, bn_rs, bn_tmp = sb("a_bn_ve", [P, C]), sb("a_bn_rs", [P, C]), sb("a_bn_tmp", [P, C])
        gamma_beta = sb("a_gamma_beta", [P, 2, C])

        ctx_in, gb_in, tables_in = sig("a_ctx_in"), sig("a_gb_in"), sig("a_tables_in")
        xa_in, xr_in = sig("a_xa_in", 16), sig("a_xr_in", 16)
        consts, ctx_tr, ctx_ev, passed = sig("a_consts"), sig("a_ctx_tr"), sig("a_ctx_ev"), sig("a_passed")
        var_x, rs_x, rows_done = sig("a_var_x", 1), sig("a_rs_x", 1), sig("a_rows_done", 1, 1)
        front_tr, q_hi_done, q_lo_done = sig("a_front_tr", 2), sig("a_q_hi_done", 2), sig("a_q_lo_done", 2)
        keys_ready, vals_ready = sig("a_keys_ready", 1), sig("a_vals_ready", 1)
        score_done, silu_done = sig("a_score", 8, 16), sig("a_silu", 8, 2)
        value_done, attn_done = sig("a_value", 2, 4), sig("a_attn", 2, 2)
        back_tr, x1_done = sig("a_back_tr", 2), sig("a_x1_done", 2, 2)
        var_1, rs_1, rows1_done = sig("a_var_1", 1), sig("a_rs_1", 1), sig("a_rows1_done", 1)
        last_tr, xt_done, bn_taken = sig("a_last_tr", 2), sig("a_xt_done", 2), sig("a_bn_taken", C, 3 * C)
        x1_kept, xt_kept = sig("a_x1_kept", 16, 16), sig("a_xt_kept", 16, 16)
        dve_own, pool_own = sig("a_dve_own"), sig("a_pool_own")
        bn_var, bn_rs_ready, bn_done = sig("a_bn_var"), sig("a_bn_rs_ready"), sig("a_bn_done")
        block = own.enter_context(nc.Block())

        def steps(eng, step):
            step(0, 0, True, True, False)
            with eng.Fori(0, (B - 4) // 2) as i:
                step(2 * i + 1, 1, True, True, True)
                step(2 * i + 2, 0, True, True, True)
            step(B - 3, 1, True, True, True)
            step(B - 2, 0, True, False, True)
            step(B - 1, 1, False, False, True)

        def at_batch(dram, b):
            return dram[bass.ds(b, 1), :, :].rearrange("a (t p) d -> p (a t) d", p=P)

        @block.sync
        def _(sp):
            def load_a(b):
                sp.wait_ge(rows_done.sem, rows_done.at(b, 0))
                sp.dma_start(xa[:, :, :], at_batch(x, b)).then_inc(xa_in.sem, 16)

            load_a(0)
            sp.dma_start(ctx_rows[:, :, :], ctx.rearrange("b s d -> (b s) d")
                         .rearrange("(t p) d -> p t d", p=P)).then_inc(ctx_in.sem, 16)
            for half in range(2):
                sp.dma_start(ctx_twice[64 * half:64 * half + 64, :, :],
                             ctx.rearrange("b s d -> s b d")).then_inc(ctx_in.sem, 16)
            load_a(1)
            for k, name in enumerate(("gamma", "beta")):
                sp.dma_start(gamma_beta[:, k, :], cst[name].rearrange("(c p) -> p c", p=P),
                             allow_slow_non_contiguous=True).then_inc(gb_in.sem, 16)
            for dst, src in ((cst["key_rows"], cst["key_in"]), (cst["key_up"], cst["key_out"])):
                sp.dma_start(dst[:, :, :], src.rearrange("(u v) d -> u v d", u=P)).then_inc(tables_in.sem, 16)

            def step(b, p, front, ahead, back):
                sp.wait_ge(x1_done.sem, x1_done.at(b, 0))
                sp.dma_start(xr[:, :, :], at_batch(x, b)).then_inc(xr_in.sem, 16)
                if ahead:
                    load_a(b + 2)
                sp.wait_ge(x1_done.sem, x1_done.at(b, 2))
                sp.dma_start(at_batch(x1_dram, b), x1[:, :, :]).then_inc(x1_kept.sem, 16)

            steps(sp, step)
            sp.wait_ge(tables_in.sem, 32)
            sp.wait_ge(x1_kept.sem, x1_kept.at(B, 0))

        @block.gpsimd
        def _(pool):
            setup = Chain(pool, consts.sem)
            setup.link(pool.memset(ident[:, :], 0.0))
            setup.link(pool.memset(mask_k[:, :], 1.0))
            setup.link(pool.memset(neghalf[:, :], -0.5))
            setup.link(pool.memset(mask_v[:, :, :, :], 0.0))
            setup.wait()
            setup.link(pool.affine_select(out=ident[:, :], in_=ident[:, :], compare_op=ALU.not_equal, fill=1.0,
                                          base=0, pattern=[[-1, P]], channel_multiplier=1))
            setup.link(pool.affine_select(out=mask_k[:, :], in_=mask_k[:, :], compare_op=ALU.is_ge, fill=0.0,
                                          base=0, pattern=[[-16, 8]], channel_multiplier=1))
            for half in range(2):
                setup.wait()
                setup.link(pool.memset(mask_v[64 * half:64 * half + 64, :, half, :], 1.0))
            setup.wait()
            setup.link(pool.affine_select(out=mask_k[:, :], in_=mask_k[:, :], compare_op=ALU.is_ge, fill=0.0,
                                          base=15, pattern=[[16, 8]], channel_multiplier=-1))
            setup.wait()
            for s in (rows_done, score_done, silu_done, value_done, attn_done, x1_done, bn_taken, x1_kept, xt_kept):
                pool.sem_inc(s.sem, s.start)
            pool.wait_ge(ctx_in.sem, 48)
            pool.wait_ge(ctx_ev.sem, C)

            def rsqrt(var, rs, b, which, chain):
                wait_apart(pool, var.sem, var.at(b, 1), passed.sem)
                chain.link(pool.tensor_scalar(var_eps[which][:, :], mean_var[which][:, :, 1], EPS, None, ALU.add))
                chain.wait()
                pool.tensor_tensor(rstd[which][:, :], var_eps[which][:, :], neghalf[:, 0:T], ALU.pow).then_inc(rs.sem, 1)

            def spread_keys(b, p, c, chain):
                if c == 0:
                    pool.wait_ge(score_done.sem, score_done.at(b, 0 - PAIRS))
                else:
                    chain.wait()
                chain.link(pool.tensor_tensor(keys_f[:, :, :],
                                              ctx_t[:, c, bass.ds(b * S, S)].unsqueeze(1).to_broadcast([P, 8, S]),
                                              mask_k[:, :].unsqueeze(2).to_broadcast([P, 8, S]), ALU.mult))
                chain.wait_apart(passed.sem)
                chain.link(pool.tensor_copy(keys_hi[p][:, c, :, :], keys_f[:, :, :]))
                chain.wait()
                last = pool.tensor_tensor(keys_lo[p][:, c, :, :], keys_f[:, :, :],
                                          keys_hi[p][:, c, :, :].bitcast(F32), ALU.subtract)
                if c < C - 1:
                    chain.link(last)
                else:
                    last.then_inc(keys_ready.sem, 1)
                    pool.wait_ge(keys_ready.sem, keys_ready.at(b, 1))

            def spread_values(b, p):
                pool.wait_ge(value_done.sem, value_done.at(b, 0 - C))
                pool.tensor_tensor(vals[p][:, :], ctx_twice[:, bass.ds(b, 1), :].rearrange("p a d -> p (a d)"),
                                   mask_v[:, :, :, :].rearrange("p a b c -> p (a b c)"), ALU.mult).then_inc(vals_ready.sem, 1)

            def spread_ahead(b, p, chain):
                spread_keys(b, p, 0, chain)
                rsqrt(var_x, rs_x, b, 0, chain)
                for c in range(1, C):
                    spread_keys(b, p, c, chain)

            first = Chain(pool, pool_own.sem)
            for b in range(2):
                spread_ahead(b, b, first)
                spread_values(b, b)
            AHEAD = 6
            assert first.n == 2 * AHEAD, first.n

            def step(b, p, front, ahead, back):
                ahead_before = AHEAD * (b if not isinstance(b, int) else min(b, B - 2))
                chain = Chain(pool, pool_own.sem, ahead_before + b + 2 * AHEAD)
                if ahead:
                    spread_ahead(b + 2, p, chain)
                rsqrt(var_1, rs_1, b, 1, chain)
                if ahead:
                    spread_values(b + 2, p)
                assert chain.n == (AHEAD + 1 if ahead else 1), chain.n

            steps(pool, step)
            pool.wait_ge(bn_var.sem, 1)
            pool.tensor_scalar(bn_ve[:, :], bn_mv[:, :, 1], EPS, None, ALU.add).then_inc(bn_rs_ready.sem, 1)
            pool.wait_ge(bn_rs_ready.sem, 1)
            pool.tensor_tensor(bn_rs[:, :], bn_ve[:, :], neghalf[:, 0:C], ALU.pow).then_inc(bn_rs_ready.sem, 1)

        @block.tensor
        def _(pe):
            pe.wait_ge(consts.sem, 9)
            pe.wait_ge(ctx_in.sem, 48)
            for c in range(C):
                for t in range(B * S // P):
                    last = pe.transpose(trans[c][:, t * P:(t + 1) * P], ctx_rows[:, t, c * P:(c + 1) * P], ident[:, :])
                last.then_inc(ctx_tr.sem, 1)
            pe.wait_ge(ctx_ev.sem, C)

            def front(b, p):
                pe.wait_ge(rows_done.sem, rows_done.at(b, 1))
                for c in range(C):
                    pe.wait_ge(bn_taken.sem, bn_taken.at(b, c + 1 - 3 * C))
                    for t in range(T):
                        last = pe.transpose(trans[c][:, t * P:(t + 1) * P], rows[:, t, c * P:(c + 1) * P], ident[:, :])
                    last.then_inc(front_tr.sem, 1)
                pe.wait_ge(keys_ready.sem, keys_ready.at(b, 1))
                pe.wait_ge(q_hi_done.sem, q_hi_done.at(b, C))
                pe.wait_ge(q_lo_done.sem, q_lo_done.at(b, C))
                for g in range(PAIRS):
                    c, pair = g // 4, g % 4
                    pe.wait_ge(silu_done.sem, silu_done.at(b, g + 1 - 2))
                    w_hi = keys_hi[p][:, c, 2 * pair:2 * pair + 2, :].rearrange("p a b -> p (a b)")
                    w_lo = keys_lo[p][:, c, 2 * pair:2 * pair + 2, :].rearrange("p a b -> p (a b)")
                    three_pass(pe, score[g % 2][:, :], w_hi, w_lo, q_hi[:, c, :], q_lo[:, c, :],
                               True, True).then_inc(score_done.sem, 1)

            def values(b, p):
                pe.wait_ge(silu_done.sem, silu_done.at(b, PAIRS))
                for c in range(C):
                    pe.wait_ge(vals_ready.sem, vals_ready.at(b, 1))
                    pe.wait_ge(attn_done.sem, attn_done.at(b, c + 1 - 2))
                    for pair in range(4):
                        g = 4 * c + pair
                        last = pe.matmul(value[c][32 * pair:32 * pair + 32, :], vals[p][:, 32 * g:32 * g + 32],
                                         acts[p][:, g, :], start=True, stop=True)
                    last.then_inc(value_done.sem, 1)
                pe.wait_ge(attn_done.sem, attn_done.at(b, C))
                for j in range(T // 2):
                    pe.wait_ge(x1_done.sem, x1_done.at(b, j + 1 - 2))
                    for t in (2 * j, 2 * j + 1):
                        for c in range(C):
                            last = pe.transpose(back_b[j][:, (t % 2) * D + c * P:(t % 2) * D + (c + 1) * P],
                                                attn_t[:, c, t * P:(t + 1) * P], ident[:, :])
                    last.then_inc(back_tr.sem, 1)

            def back(b):
                pe.wait_ge(rows1_done.sem, rows1_done.at(b, 1))
                for c in range(C):
                    pe.wait_ge(bn_taken.sem, bn_taken.at(b, c + 1 - C))
                    for t in range(T):
                        last = pe.transpose(trans[c][:, t * P:(t + 1) * P], rows1[:, t, c * P:(c + 1) * P], ident[:, :])
                    last.then_inc(last_tr.sem, 1)

            def step(b, p, has_front, ahead, has_back):
                if has_front:
                    front(b + 1, 1 - p)
                if has_back:
                    back(b - 1)
                values(b, p)

            front(0, 0)
            steps(pe, step)
            back(B - 1)

        @block.scalar
        def _(act):
            for c in range(C):
                act.wait_ge(ctx_tr.sem, c + 1)
                act.activation(ctx_t[:, c, :], trans[c][:, :], ACT.Copy).then_inc(ctx_ev.sem, 1)

            def front(b, p):
                for c in range(C):
                    act.wait_ge(front_tr.sem, front_tr.at(b, c + 1))
                    act.activation(q_hi[:, c, :], trans[c][:, :], ACT.Copy).then_inc(q_hi_done.sem, 1)
                for g in range(PAIRS):
                    act.wait_ge(score_done.sem, score_done.at(b, g + 1))
                    act.activation(acts[p][:, g, :], score[g % 2][:, :], ACT.Silu).then_inc(silu_done.sem, 1)

            def back(b):
                act.wait_ge(xt_kept.sem, xt_kept.at(b, 0))
                for c in range(C):
                    act.wait_ge(last_tr.sem, last_tr.at(b, c + 1))
                    act.activation(xt[:, c, :], trans[c][:, :], ACT.Copy).then_inc(xt_done.sem, 1)
                act.wait_ge(xt_done.sem, xt_done.at(b, C))
                act.dma_start(xt_dram[:, :, bass.ds(b * N, N)].rearrange("c p n -> p c n"), xt[:, :, :]).then_inc(xt_kept.sem, 16)

            def step(b, p, has_front, ahead, has_back):
                if has_front:
                    front(b + 1, 1 - p)
                if has_back:
                    back(b - 1)
                for c in range(C):
                    act.wait_ge(value_done.sem, value_done.at(b, c + 1))
                    act.activation(attn_t[:, c, :], value[c][:, :], ACT.Copy).then_inc(attn_done.sem, 1)

            front(0, 0)
            steps(act, step)
            back(B - 1)
            act.wait_ge(xt_kept.sem, xt_kept.at(B, 0))

        @block.vector
        def _(dve):
            def moments(chain, src, which):
                for t in range(T):
                    last = dve.bn_stats(stats[:, t, :], src[:, t, :])
                chain.link(last)
                chain.wait_apart(passed.sem)
                for t in range(T):
                    last = dve.bn_aggr(mean_var[which][:, t, :], stats[:, t, :])
                return last

            def normalise(dst, src, which):
                for t in range(T):
                    last = dve.tensor_scalar(dst[:, t, :], src[:, t, :], mean_var[which][:, t, 0:1], rstd[which][:, t:t + 1],
                                             ALU.subtract, ALU.mult)
                return last

            def front_moments(b, chain):
                dve.wait_ge(xa_in.sem, xa_in.at(b, 16))
                moments(chain, xa, 0).then_inc(var_x.sem, 1)

            def front_rows(b):
                dve.wait_ge(rs_x.sem, rs_x.at(b, 1))
                dve.wait_ge(var_x.sem, var_x.at(b, 1))
                normalise(rows, xa, 0).then_inc(rows_done.sem, 1)

            def queries_low(b):
                for c in range(C):
                    dve.wait_ge(q_hi_done.sem, q_hi_done.at(b, c + 1))
                    dve.tensor_tensor(q_lo[:, c, :], trans[c][:, :], q_hi[:, c, :].bitcast(F32),
                                      ALU.subtract).then_inc(q_lo_done.sem, 1)

            def back(b):
                for c in range(C):
                    dve.wait_ge(xt_done.sem, xt_done.at(b, c + 1))
                    dve.bn_stats(bn_stats[:, c, bass.ds(b, 1), :].rearrange("p a b -> p (a b)"), trans[c][:, :]) \
                        .then_inc(bn_taken.sem, 1)

            def step(b, p, has_front, ahead, has_back):
                done = 2 * b if not isinstance(b, int) or b <= B - 2 else 2 * (B - 2) + (b - (B - 2))
                chain = Chain(dve, dve_own.sem, done + 2)
                if ahead:
                    front_moments(b + 2, chain)
                if has_back:
                    back(b - 1)
                if ahead:
                    front_rows(b + 2)
                dve.wait_ge(xr_in.sem, xr_in.at(b, 16))
                dve.wait_ge(x1_kept.sem, x1_kept.at(b, 0))
                for j in range(T // 2):
                    dve.wait_ge(back_tr.sem, back_tr.at(b, j + 1))
                    dve.tensor_tensor(x1[:, 2 * j:2 * j + 2, :], xr[:, 2 * j:2 * j + 2, :],
                                      back_b[j][:, :].rearrange("p (t d) -> p t d", t=2), ALU.add).then_inc(x1_done.sem, 1)
                dve.wait_ge(x1_done.sem, x1_done.at(b, 2))
                moments(chain, x1, 1).then_inc(var_1.sem, 1)
                if ahead:
                    queries_low(b + 2)
                dve.wait_ge(rs_1.sem, rs_1.at(b, 1))
                dve.wait_ge(var_1.sem, var_1.at(b, 1))
                normalise(rows1, x1, 1).then_inc(rows1_done.sem, 1)

            first = Chain(dve, dve_own.sem)
            front_moments(0, first)
            front_rows(0)
            queries_low(0)
            front_moments(1, first)
            front_rows(1)
            queries_low(1)
            steps(dve, step)
            back(B - 1)
            dve.wait_ge(bn_taken.sem, bn_taken.at(B, 0))
            for c in range(C):
                last = dve.bn_aggr(bn_mv[:, c, :], bn_stats[:, c, :, :].rearrange("p b s -> p (b s)"))
            last.then_inc(bn_var.sem, 1)
            dve.wait_ge(bn_rs_ready.sem, 2)
            dve.wait_ge(gb_in.sem, 32)
            dve.tensor_tensor(bn_out[:, 0, :], bn_rs[:, :], gamma_beta[:, 0, :], ALU.mult).then_inc(bn_done.sem, 1)
            dve.wait_ge(bn_done.sem, 1)
            dve.tensor_tensor(bn_tmp[:, :], bn_mv[:, :, 0], bn_out[:, 0, :], ALU.mult).then_inc(bn_done.sem, 1)
            dve.wait_ge(bn_done.sem, 2)
            dve.tensor_tensor(bn_out[:, 1, :], gamma_beta[:, 1, :], bn_tmp[:, :], ALU.subtract).then_inc(bn_done.sem, 1)
            dve.wait_ge(bn_done.sem, 3)


def retrieve_experts(nc, xt_dram, x1_dram, w_q, keys, x2_dram, cst):
    H, K, _, KD = keys.shape
    E, D = cst["key_in"].shape
    N = x1_dram.shape[0]
    C, NV, R, T = D // P, E // P, 2 * P, 2
    BLOCKS = N // R
    TOP = 8
    PICKS = H * TOP
    HALF = 32
    ident, bn = cst["ident"], cst["bn"]
    own = ExitStack()
    with own:
        def sb(name, shape, dt=F32):
            return own.enter_context(nc.sbuf_tensor(name, shape, dt))

        def sig(name, per=0, start=0):
            return Signal(own.enter_context(nc.semaphore(name)), per, start)

        bank = [own.enter_context(nc.psum_tensor(f"b_bank{i}", [P, 512], F32)) for i in range(8)]
        down_b, up_b, sim_b, tr_b = bank[0:2], bank[4], bank[5:7], bank[7]
        w_b = bank[2:4] + down_b

        key_hi = sb("b_key_hi", [P, C, NV, P], F32R)
        key_lo = sb("b_key_lo", [P, C, NV, P], F32R)
        key_up, gated = cst["key_up"], cst["key_rows"]
        score_w = sb("b_score_w", [P, C, 2 * H * K])
        hot_u = [sb(f"b_hot_u{h}", [P, P, HALF], BF16) for h in range(2)]
        hot_v = [sb(f"b_hot_v{h}", [P, NV, HALF], BF16) for h in range(2)]
        weigh_v = [sb(f"b_weigh_v{h}", [P, 3, 2, NV, HALF], BF16) for h in range(2)]
        ramp = sb("b_ramp", [P, P, 4], BF16)
        ramp8 = sb("b_ramp8", [P, TOP])
        x_raw = sb("b_x_raw", [P, C, R])
        x_hi = sb("b_x_hi", [P, C, R], F32R)
        x_lo = sb("b_x_lo", [P, C, R], F32R)
        x_norm = sb("b_x_norm", [P, C, R])
        x_rows = sb("b_x_rows", [P, T, D])
        best = sb("b_best", [P, 2, H, TOP])
        best_at = sb("b_best_at", [P, 2, H, TOP], U32)
        pairs = sb("b_pairs", [P, H, TOP, TOP])
        top = sb("b_top", [P, H, TOP])
        top_at = sb("b_top_at", [P, H, TOP], U32)
        coords = sb("b_coords", [P, 2, PICKS], U32)
        coords_f = sb("b_coords_f", [P, 2, PICKS])
        at_f = sb("b_at_f", [P, 2, H, TOP])
        hit = sb("b_hit", [P, 2, H, TOP, TOP])
        delta = sb("b_delta", [P, H, TOP])
        expo = sb("b_expo", [P, H, TOP])
        total = sb("b_total", [P, H])
        share = sb("b_share", [P, H])
        expert = sb("b_expert", [P, 2, PICKS])
        upper = sb("b_upper", [P, PICKS])
        cat = sb("b_cat", [P, 3, 2, PICKS])
        uv = sb("b_uv", [P, 2, PICKS], BF16)
        part = sb("b_part", [P, 3, PICKS], BF16)
        rest = sb("b_rest", [P, PICKS])
        rest2 = sb("b_rest2", [P, PICKS])
        wq_ld, keys_ld = sig("b_wq_ld"), sig("b_keys_ld")
        consts, zeroed = sig("b_consts"), sig("b_zeroed")
        s_tr, s_act, s_dve = sig("b_s_tr"), sig("b_s_act"), sig("b_s_dve")
        passed = sig("b_passed")
        raw_in, xn_ready = sig("b_raw_in", 16), sig("b_xn", 1, 1)
        xh_ready, xl_ready = sig("b_xh", 1), sig("b_xl", 1, 1)
        sims_done, topk_read = sig("b_sims", 2, 2), sig("b_topk_read", 2, 1)
        topk_done, map_done, exp_done = sig("b_topk", 2), sig("b_map", 2, 1), sig("b_exp", 2)
        cat_ready, tr_done = sig("b_cat", 2), sig("b_tr", 2)
        gen_ready, w_done, h_done = sig("b_gen", 4), sig("b_w", 16, 8), sig("b_h", 16, 4)
        down_done, gelu_done = sig("b_down", 16), sig("b_gelu", 16, 2)
        up_done, x2_done = sig("b_up", 2), sig("b_x2", 2, 1)
        rows_in, kept = sig("b_rows_in", 16), sig("b_kept", 32, 32)
        DVE_FIRST, DVE_TURN = 17, 30
        POOL_TILE = 7
        dve_own, pool_own = sig("b_dve_own"), sig("b_pool_own")
        block = own.enter_context(nc.Block())
        xt_view = xt_dram.rearrange("c p n -> p c n")
        setup_rows = gated
        wq_all = [hot_u[h][:, :, :].rearrange("p a b -> p (a b)").bitcast(F32).rearrange("p (g d) -> p g d", d=D) for h in range(2)]
        old = weigh_v[0][:, :, :, :, :].rearrange("p a b c d -> p (a b c d)").bitcast(F32)
        keys_rows = old[:, 0:1024].rearrange("p (t d) -> p t d", t=4)
        keys_t = old[:, 1024:2048].rearrange("p (a n) -> p a n", a=2)

        @block.sync
        def _(sp):
            sp.dma_start(keys_rows, keys.rearrange("h k p d -> (h k) (p d)").rearrange("(t p) d -> p t d", p=P)) \
                .then_inc(keys_ld.sem, 16)
            wq_v = w_q.rearrange("(g p) d -> p g d", p=KD)
            for h in range(2):
                sp.dma_start(wq_all[h], wq_v[:, 8 * h:8 * h + 8, :]).then_inc(wq_ld.sem, 16)

            def load_x(j):
                sp.wait_ge(xl_ready.sem, xl_ready.at(j, 0))
                sp.wait_ge(xn_ready.sem, xn_ready.at(j, 0))
                sp.dma_start(x_raw[:, :, :], xt_view[:, :, bass.ds(j * R, R)]).then_inc(raw_in.sem, 16)

            def rows_through(j, ahead):
                sp.wait_ge(kept.sem, kept.at(j, 0))
                sp.dma_start(x_rows[:, :, :], x1_dram[bass.ds(j * R, R), :].rearrange("(t p) d -> p t d", p=P)) \
                    .then_inc(rows_in.sem, 16)
                for t in range(T):
                    sp.wait_ge(x2_done.sem, x2_done.at(j, t + 1))
                    sp.dma_start(x2_dram[bass.ds(j * R + t * P, P), :], x_rows[:, t, :]).then_inc(kept.sem, 16)
                    if ahead and t == 0:
                        load_x(j + 2)

            load_x(0)
            load_x(1)
            with sp.Fori(0, BLOCKS - 2) as i:
                rows_through(i, True)
            rows_through(BLOCKS - 2, False)
            rows_through(BLOCKS - 1, False)
            sp.wait_ge(kept.sem, kept.at(BLOCKS, 0))

        @block.gpsimd
        def _(pool):
            pool.iota(ramp[:, :, :], [[1, P], [0, 4]], channel_multiplier=0,
                      allow_small_or_imprecise_dtypes=True).then_inc(consts.sem, 1)
            pool.iota(ramp8[:, :], [[1, TOP]], channel_multiplier=0,
                      allow_small_or_imprecise_dtypes=True).then_inc(consts.sem, 1)
            pool.wait_ge(consts.sem, 2)
            for s in (xn_ready, xl_ready, sims_done, topk_read, map_done, w_done, h_done, gelu_done, x2_done, kept):
                pool.sem_inc(s.sem, s.start)
            pool.memset(weigh_v[1][:, :, :, :, :], 0.0).then_inc(zeroed.sem, 1)
            pool.wait_ge(s_dve.sem, 1)
            pool.memset(weigh_v[0][:, :, :, :, :], 0.0).then_inc(zeroed.sem, 1)

            def place_picks(j, t, chain):
                wait_apart(pool, topk_done.sem, topk_done.at(j, t + 1), passed.sem)
                chain.link(pool.tensor_copy(coords_f[:, :, :], coords[:, :, :]))
                chain.link(pool.tensor_copy(at_f[:, :, :, :], best_at[:, :, :, :]))
                for a in range(2):
                    chain.wait()
                    hits = hit[:, a, :, :, :].rearrange("p h k i -> p (h k) i")
                    chain.link(pool.tensor_tensor(hits, coords_f[:, a, :].unsqueeze(2).to_broadcast([P, PICKS, TOP]),
                                                  ramp8[:, :].unsqueeze(1).to_broadcast([P, PICKS, TOP]), ALU.subtract))
                    chain.wait_apart(passed.sem)
                    chain.link(pool.tensor_scalar(hits, hits, 0.0, None, ALU.is_equal))
                    chain.wait()
                    last = pool.tensor_tensor(hit[:, a, :, :, :], hit[:, a, :, :, :],
                                              at_f[:, a, :, :].unsqueeze(2).to_broadcast([P, H, TOP, TOP]), ALU.mult)
                    if a == 0:
                        chain.link(last)
                last.then_inc(map_done.sem, 1)

            def split_low(j):
                pool.wait_ge(xh_ready.sem, xh_ready.at(j, 1))
                pool.tensor_tensor(x_lo[:, :, :], x_raw[:, :, :], x_hi[:, :, :].bitcast(F32), ALU.subtract) \
                    .then_inc(xl_ready.sem, 1)

            def prepare(j):
                chain = Chain(pool, pool_own.sem, j * (2 * POOL_TILE))
                place_picks(j, 0, chain)
                split_low(j)
                place_picks(j, 1, chain)
                assert chain.n == 2 * POOL_TILE, chain.n

            prepare(0)
            with pool.Fori(0, BLOCKS - 1) as i:
                prepare(i + 1)

        @block.tensor
        def _(pe):
            pe.wait_ge(keys_ld.sem, 16)
            for a in range(2):
                for t in range(4):
                    last = pe.transpose(bank[a][:, t * P:(t + 1) * P], keys_rows[:, t, a * KD:(a + 1) * KD], ident[:, :])
                last.then_inc(s_tr.sem, 1)
            pe.wait_ge(wq_ld.sem, 32)
            pe.wait_ge(s_act.sem, 2)
            for a in range(2):
                for c in range(C):
                    for h in range(H):
                        last = pe.matmul(bank[2 + 2 * a + c][:, h * K:(h + 1) * K], wq_all[a][:, h, c * P:(c + 1) * P],
                                         keys_t[:, a, h * K:(h + 1) * K], start=True, stop=True)
                    last.then_inc(s_tr.sem, 1)
            n = 0
            for c in range(C):
                for v in range(0, NV, 4):
                    b = (6 + n % 4) % 8
                    if n >= 4:
                        pe.wait_ge(s_act.sem, 6 + n - 3)
                        pe.wait_ge(s_dve.sem, 1 + n - 3)
                    for k in range(4):
                        last = pe.transpose(bank[b][:, k * P:(k + 1) * P], setup_rows[:, v + k, c * P:(c + 1) * P], ident[:, :])
                    last.then_inc(s_tr.sem, 1)
                    n += 1
            pe.wait_ge(s_act.sem, 6 + n)
            pe.wait_ge(s_dve.sem, 1 + n)

            def scores(j, t):
                if t == 0:
                    pe.wait_ge(xn_ready.sem, xn_ready.at(j, 1))
                pe.wait_ge(topk_read.sem, topk_read.at(j, t + 1 - 1))
                for a in range(2):
                    for c in range(C):
                        last = pe.matmul(sim_b[a][:, :], x_norm[:, c, t * P:(t + 1) * P],
                                         score_w[:, c, a * H * K:(a + 1) * H * K], start=(c == 0), stop=(c == C - 1))
                last.then_inc(sims_done.sem, 1)

            def down(j):
                pe.wait_ge(xl_ready.sem, xl_ready.at(j, 1))
                for g in range(NV // 2):
                    pe.wait_ge(gelu_done.sem, gelu_done.at(j, g + 1 - 2))
                    for v in (2 * g, 2 * g + 1):
                        o = down_b[g % 2][:, (v % 2) * R:(v % 2 + 1) * R]
                        for c in range(C):
                            last = three_pass(pe, o, key_hi[:, c, v, :], key_lo[:, c, v, :], x_hi[:, c, :], x_lo[:, c, :],
                                              c == 0, c == C - 1)
                    last.then_inc(down_done.sem, 1)

            def turn_picks(j, t):
                pe.wait_ge(cat_ready.sem, cat_ready.at(j, t + 1))
                for k in range(3):
                    last = pe.transpose(tr_b[:, k * P:(k + 1) * P], cat[:, k, :, :].rearrange("p a b -> p (a b)"), ident[:, :])
                last.then_inc(tr_done.sem, 1)

            def weights(j, t):
                for q in range(8):
                    h = q // 4
                    if q % 4 == 0:
                        pe.wait_ge(gen_ready.sem, gen_ready.at(j, 2 * t + h + 1))
                    if t == 0 and q == 2:
                        pe.wait_ge(gelu_done.sem, gelu_done.at(j, NV // 2))
                    pe.wait_ge(h_done.sem, h_done.at(j, 8 * t + q + 1 - 4))
                    for mm in range(8):
                        m = (q % 4) * 8 + mm
                        for k in range(3):
                            last = pe.matmul(w_b[q % 4][:, mm * 64:(mm + 1) * 64], hot_u[h][:, :, m],
                                             weigh_v[h][:, k, :, :, m].rearrange("p r v -> p (r v)"),
                                             start=(k == 0), stop=(k == 2))
                    last.then_inc(w_done.sem, 1)

            def up(j, t):
                pe.wait_ge(h_done.sem, h_done.at(j, 8 * t + 8))
                pe.wait_ge(x2_done.sem, x2_done.at(j, t + 1 - 1))
                for v in range(NV):
                    last = pe.matmul(up_b[:, 0:D], gated[:, v, t * P:(t + 1) * P], key_up[:, v, :],
                                     start=(v == 0), stop=(v == NV - 1))
                last.then_inc(up_done.sem, 1)

            scores(0, 0)
            scores(0, 1)
            turn_picks(0, 0)

            def turn(i, more):
                if more:
                    scores(i + 1, 0)
                down(i)
                turn_picks(i, 1)
                weights(i, 0)
                up(i, 0)
                if more:
                    scores(i + 1, 1)
                weights(i, 1)
                up(i, 1)
                if more:
                    turn_picks(i + 1, 0)

            with pe.Fori(0, BLOCKS - 1) as i:
                turn(i, True)
            turn(BLOCKS - 1, False)

        @block.scalar
        def _(act):
            for a in range(2):
                act.wait_ge(s_tr.sem, a + 1)
                act.activation(keys_t[:, a, :], bank[a][:, :], ACT.Copy).then_inc(s_act.sem, 1)
            for a in range(2):
                for c in range(C):
                    act.wait_ge(s_tr.sem, 2 + 2 * a + c + 1)
                    act.activation(score_w[:, c, a * H * K:(a + 1) * H * K], bank[2 + 2 * a + c][:, :], ACT.Copy) \
                        .then_inc(s_act.sem, 1)
            n = 0
            for c in range(C):
                for v in range(0, NV, 4):
                    act.wait_ge(s_tr.sem, 6 + n + 1)
                    act.activation(key_hi[:, c, v:v + 4, :].rearrange("p a b -> p (a b)"), bank[(6 + n % 4) % 8][:, :], ACT.Copy) \
                        .then_inc(s_act.sem, 1)
                    n += 1

            def normalise(j):
                act.wait_ge(raw_in.sem, raw_in.at(j, 16))
                act.wait_ge(sims_done.sem, sims_done.at(j, 0))
                for c in range(C):
                    last = act.activation(x_norm[:, c, :], x_raw[:, c, :], ACT.Identity,
                                          bias=bn[:, 1, c:c + 1], scale=bn[:, 0, c:c + 1])
                last.then_inc(xn_ready.sem, 1)

            def split_high(j):
                act.activation(x_hi[:, :, :], x_raw[:, :, :], ACT.Copy).then_inc(xh_ready.sem, 1)

            def exps(j, t):
                act.wait_ge(topk_done.sem, topk_done.at(j, t + 1))
                act.activation(expo[:, :, :], delta[:, :, :], ACT.Exp).then_inc(exp_done.sem, 1)

            def gelus(j):
                for g in range(NV // 2):
                    act.wait_ge(down_done.sem, down_done.at(j, g + 1))
                    act.activation(gated[:, 2 * g:2 * g + 2, :].rearrange("p v n -> p (v n)"), down_b[g % 2][:, :], ACT.Gelu) \
                        .then_inc(gelu_done.sem, 1)

            normalise(0)
            split_high(0)
            exps(0, 0)
            exps(0, 1)
            with act.Fori(0, BLOCKS - 1) as i:
                normalise(i + 1)
                gelus(i)
                split_high(i + 1)
                exps(i + 1, 0)
                exps(i + 1, 1)
            gelus(BLOCKS - 1)

        @block.vector
        def _(dve):
            n = 0
            dve.wait_ge(s_tr.sem, 6)
            dve.memset(rest2[:, :], 0.0).then_inc(s_dve.sem, 1)
            for c in range(C):
                for v in range(0, NV, 4):
                    dve.wait_ge(s_act.sem, 6 + n + 1)
                    lo = key_lo[:, c, v:v + 4, :].rearrange("p a b -> p (a b)")
                    hi = key_hi[:, c, v:v + 4, :].rearrange("p a b -> p (a b)").bitcast(F32)
                    dve.tensor_tensor(lo, bank[(6 + n % 4) % 8][:, :], hi, ALU.subtract).then_inc(s_dve.sem, 1)
                    n += 1
            dve.wait_ge(consts.sem, 2)
            dve.wait_ge(zeroed.sem, 2)

            def choose(j, t, chain):
                dve.wait_ge(map_done.sem, map_done.at(j, t + 1 - 1))
                wait_apart(dve, sims_done.sem, sims_done.at(j, t + 1), passed.sem)
                for a in range(2):
                    for h in range(H):
                        last = dve.max(best[:, a, h, :], sim_b[a][:, h * K:(h + 1) * K])
                chain.link(last)
                chain.wait_apart(passed.sem)
                for a in range(2):
                    for h in range(H):
                        last = dve.max_index(best_at[:, a, h, :], best[:, a, h, :], sim_b[a][:, h * K:(h + 1) * K])
                last.then_inc(topk_read.sem, 1)
                chain.link(dve.tensor_tensor(pairs[:, :, :, :], best[:, 0, :, :].unsqueeze(3).to_broadcast([P, H, TOP, TOP]),
                                             best[:, 1, :, :].unsqueeze(2).to_broadcast([P, H, TOP, TOP]), ALU.add))
                chain.wait_apart(passed.sem)
                for h in range(H):
                    last = dve.max(top[:, h, :], pairs[:, h, :, :].rearrange("p a b -> p (a b)"))
                chain.link(last)
                chain.wait_apart(passed.sem)
                for h in range(H):
                    last = dve.max_index(top_at[:, h, :], top[:, h, :], pairs[:, h, :, :].rearrange("p a b -> p (a b)"))
                chain.link(last)
                dve.tensor_tensor(delta[:, :, :], top[:, :, :], top[:, :, 0:1].to_broadcast([P, H, TOP]), ALU.subtract)
                chain.wait()
                flat = top_at[:, :, :].rearrange("p h k -> p (h k)")
                dve.tensor_scalar(coords[:, 0, :], flat, 3, None, ALU.logical_shift_right)
                dve.tensor_scalar(coords[:, 1, :], flat, 7, None, ALU.bitwise_and).then_inc(topk_done.sem, 1)

            def settle(j, t, chain):
                dve.wait_ge(map_done.sem, map_done.at(j, t + 1))
                chain.link(dve.reduce_sum(expert[:, :, :].rearrange("p a b -> p (a b)"),
                                          hit[:, :, :, :, :].rearrange("p a h k i -> p (a h k) i"), axis=AXX))
                dve.wait_ge(exp_done.sem, exp_done.at(j, t + 1))
                chain.link(dve.reduce_sum(total[:, :], expo[:, :, :], axis=AXX))
                chain.wait()
                chain.link(dve.tensor_scalar(upper[:, :], expert[:, 1, :], float(NV), None, ALU.is_ge))
                chain.link(dve.reciprocal(share[:, :], total[:, :]))
                chain.wait()
                twice = [P, 2, PICKS]
                dve.scalar_tensor_tensor(cat[:, 0, :, :], expert[:, 0, :].unsqueeze(1).to_broadcast(twice), 2.0,
                                         upper[:, :].unsqueeze(1).to_broadcast(twice), ALU.mult, ALU.add)
                dve.scalar_tensor_tensor(cat[:, 1, :, :], upper[:, :].unsqueeze(1).to_broadcast(twice), -float(NV),
                                         expert[:, 1, :].unsqueeze(1).to_broadcast(twice), ALU.mult, ALU.add)
                for k in range(2):
                    last = dve.tensor_tensor(cat[:, 2, k, :].rearrange("p (h k) -> p h k", h=H), expo[:, :, :],
                                             share[:, :].unsqueeze(2).to_broadcast([P, H, TOP]), ALU.mult)
                last.then_inc(cat_ready.sem, 1)

            def take_picks(j, t, chain):
                dve.wait_ge(tr_done.sem, tr_done.at(j, t + 1))
                for r in range(2):
                    on = slice(64 * r, 64 * r + 64)
                    view = tr_b[on, 0:2 * P].rearrange("p (a n) -> p a n", a=2)
                    dve.tensor_copy(uv[on, :, :], view[:, :, 64 * r:64 * r + 64])
                    last = dve.tensor_copy(part[on, 0, :], tr_b[on, 2 * P + 64 * r:2 * P + 64 * r + 64])
                chain.link(last)
                chain.wait()
                for r in range(2):
                    on = slice(64 * r, 64 * r + 64)
                    last = dve.tensor_tensor(rest[on, :], tr_b[on, 2 * P + 64 * r:2 * P + 64 * r + 64], part[on, 0, :],
                                             ALU.subtract)
                chain.link(last)
                chain.wait()
                chain.link(dve.tensor_copy(part[:, 1, :], rest[:, :]))
                chain.wait()
                chain.link(dve.tensor_tensor(rest2[:, :], rest[:, :], part[:, 1, :], ALU.subtract))
                chain.wait()
                chain.link(dve.tensor_copy(part[:, 2, :], rest2[:, :]))

            def one_hots(j, t, chain):
                for h in range(2):
                    dve.wait_ge(w_done.sem, w_done.at(j, 8 * t + 4 * h + 4 - 8))
                    cols = slice(HALF * h, HALF * h + HALF)

                    def equal(out, n, which):
                        return dve.tensor_tensor(
                            out.rearrange("p u (a b) -> p u a b", b=4),
                            ramp[:, 0:n, :].unsqueeze(2).to_broadcast([P, n, HALF // 4, 4]),
                            uv[:, which, cols].rearrange("p (a b) -> p a b", b=4).unsqueeze(1).to_broadcast([P, n, HALF // 4, 4]),
                            ALU.is_equal)

                    chain.link(equal(hot_v[h][:, :, :], NV, 1))
                    equal(hot_u[h][:, :, :], P, 0)
                    chain.wait()
                    for r in range(2):
                        on = slice(64 * r, 64 * r + 64)
                        last = dve.tensor_tensor(weigh_v[h][on, :, r, :, :],
                                                 hot_v[h][on, :, :].unsqueeze(1).to_broadcast([64, 3, NV, HALF]),
                                                 part[on, :, cols].unsqueeze(2).to_broadcast([64, 3, NV, HALF]), ALU.mult)
                    last.then_inc(gen_ready.sem, 1)

            def gate(j, t):
                dve.wait_ge(gelu_done.sem, gelu_done.at(j, NV // 2))
                for q in range(8):
                    dve.wait_ge(w_done.sem, w_done.at(j, 8 * t + q + 1))
                    g = gated[:, :, t * P:(t + 1) * P].rearrange("p v (r m) -> p m r v", r=2)[:, 8 * q:8 * q + 8, :, :]
                    dve.tensor_tensor(g, g, w_b[q % 4][:, :].rearrange("p (m r v) -> p m r v", m=8, r=2), ALU.mult) \
                        .then_inc(h_done.sem, 1)

            def add_rows(j, t):
                if t == 0:
                    dve.wait_ge(rows_in.sem, rows_in.at(j, 16))
                dve.wait_ge(up_done.sem, up_done.at(j, t + 1))
                dve.tensor_tensor(x_rows[:, t, :], x_rows[:, t, :], up_b[:, 0:D], ALU.add).then_inc(x2_done.sem, 1)

            def turn(i, more, chain):
                one_hots(i, 0, chain)
                settle(i, 1, chain)
                if more:
                    choose(i + 1, 0, chain)
                take_picks(i, 1, chain)
                gate(i, 0)
                chain.wait()
                one_hots(i, 1, chain)
                if more:
                    settle(i + 1, 0, chain)
                add_rows(i, 0)
                gate(i, 1)
                if more:
                    choose(i + 1, 1, chain)
                add_rows(i, 1)
                if more:
                    take_picks(i + 1, 0, chain)
                    chain.wait()

            first = Chain(dve, dve_own.sem)
            choose(0, 0, first)
            settle(0, 0, first)
            choose(0, 1, first)
            take_picks(0, 0, first)
            first.wait()
            assert first.n == DVE_FIRST, first.n
            with dve.Fori(0, BLOCKS - 1) as i:
                chain = Chain(dve, dve_own.sem, i * DVE_TURN + DVE_FIRST)
                turn(i, True, chain)
                assert chain.n == DVE_TURN, chain.n
            turn(BLOCKS - 1, False, Chain(dve, dve_own.sem, (BLOCKS - 1) * DVE_TURN + DVE_FIRST))


def attend_latents(nc, ctx, x2_dram, wts, out_dram, cst):
    B, S, D = ctx.shape
    N = x2_dram.shape[0] // B
    INNER = wts["wq"].shape[1]
    H, C, T, CH = 8, D // P, N // P, INNER // P
    DH = INNER // H
    F = N + S
    SCALE = DH ** -0.5
    ident, neghalf = cst["ident"], cst["neghalf"]
    own = ExitStack()
    with own:
        def sb(name, shape, dt=F32):
            return own.enter_context(nc.sbuf_tensor(name, shape, dt))

        def sig(name, per=0, start=0):
            return Signal(own.enter_context(nc.semaphore(name)), per, start)

        score_b = [own.enter_context(nc.psum_tensor(f"c_score{i}", [P, 1024], F32)) for i in range(2)]
        turn_b = [own.enter_context(nc.psum_tensor(f"c_turn{i}", [P, 512], F32)) for i in range(2)]
        sum_b = [own.enter_context(nc.psum_tensor(f"c_sum{i}", [P, 512], F32)) for i in range(2)]
        pool4 = [score_b[i // 2][:, 512 * (i % 2):512 * (i % 2) + 512] for i in range(4)]

        names = ("wq", "wk", "wv")
        w_hi = {n: sb(f"c_{n}_hi", [P, C, INNER], F32R) for n in names}
        w_lo = {n: sb(f"c_{n}_lo", [P, C, INNER], F32R) for n in names}
        w_out = sb("c_w_out", [P, CH, D])
        ternary = sb("c_ternary", [P, C, D], F32R)
        affine = sb("c_affine", [P, 4, C])
        wscale = sb("c_wscale", [P, 3])
        ones = sb("c_ones", [P, P])
        ctx_k_hi = sb("c_ctx_k_hi", [P, CH, B * S], F32R)
        ctx_k_lo = sb("c_ctx_k_lo", [P, CH, B * S], F32R)
        ctx_v = sb("c_ctx_v", [S, B, INNER])
        xz = sb("c_xz", [P, T, D])
        xr = sb("c_xr", [P, T, D])
        z0 = sb("c_z0", [P, T, D])
        z1 = sb("c_z1", [P, T, D])
        zt = sb("c_zt", [P, C, N])
        z_hi = sb("c_z_hi", [P, C, N], F32R)
        z_lo = sb("c_z_lo", [P, C, N], F32R)
        q_hi = [sb(f"c_q_hi{e}", [P, CH, N], F32R) for e in range(2)]
        q_lo = [sb(f"c_q_lo{e}", [P, CH, N], F32R) for e in range(2)]
        k_hi = sb("c_k_hi", [P, CH, N], F32R)
        k_lo = sb("c_k_lo", [P, CH, N], F32R)
        v_rows = sb("c_v_rows", [P, T, INNER])
        v_ctx = sb("c_v_ctx", [S, INNER])
        probs = [sb(f"c_probs{e}", [P, T, F]) for e in range(2)]
        probs_t = [sb(f"c_probs_t{e}", [P, T + 1, N]) for e in range(2)]
        heads = sb("c_heads", [P, CH, N])
        r_hi = sb("c_r_hi", [P, C, N], F32R)
        r_lo = sb("c_r_lo", [P, C, N], F32R)
        x3 = sb("c_x3", [P, T, D])
        nmax = sb("c_nmax", [P, H * T])
        sums = sb("c_sums", [P, H * T])
        inv = sb("c_inv", [P, H * T])
        stats = sb("c_stats", [P, T, 6])
        mean_var = sb("c_mean_var", [P, 3, T, 2])
        var_eps = sb("c_var_eps", [P, 3, T])
        rstd = sb("c_rstd", [P, 3, T])

        ld_w = {n: sig(f"c_ld_{n}") for n in names}
        ld_misc, ld_ctx = sig("c_ld_misc"), sig("c_ld_ctx")
        s_act, s_dve, s_pe, s_pool = sig("c_s_act"), sig("c_s_dve"), sig("c_s_pe"), sig("c_s_pool")
        passed = sig("c_passed")
        xz_in, xr_in = sig("c_xz_in", 16), sig("c_xr_in", 16)
        var_z, rs_z, z0_done, z1_done = sig("c_var_z", 2), sig("c_rs_z", 2), sig("c_z0", 1, 1), sig("c_z1", 1)
        var_x, rs_x, r3_done = sig("c_var_x", 1), sig("c_rs_x", 1), sig("c_r3", 1)
        zhi_done, zlo_done = sig("c_zhi", 1), sig("c_zlo", 1)
        proj_done, proj_act, proj_dve = sig("c_proj", 14), sig("c_proj_act", 14), sig("c_proj_dve", 8)
        vctx_done = sig("c_vctx", 1)
        score_done, max_done, exp_done = sig("c_score", 32), sig("c_max", 32), sig("c_exp", 32, 2)
        inv_done, norm_done = sig("c_inv", 32), sig("c_norm", 32)
        turned, ev_act, ev_dve = sig("c_turned", 40, 10), sig("c_ev_act", 24, 2), sig("c_ev_dve", 16, 2)
        av_done, heads_done = sig("c_av", 4, 4), sig("c_heads", 4, 1)
        wout_done, x3_done = sig("c_wout", 2), sig("c_x3", 2, 2)
        ft_done, f_hi, f_lo = sig("c_ft", 2), sig("c_fhi", 2), sig("c_flo", 2, 2)
        ff_done, y_done, kept = sig("c_ff", 2), sig("c_y", 2, 4), sig("c_kept", 16, 16)
        SETUP_DVE, SETUP_ACT = 12 + CH, 7 + CH + B
        dve_own, pool_own = sig("c_dve_own"), sig("c_pool_own")
        block = own.enter_context(nc.Block())
        w_raw = {"wq": probs[0][:, :, :].rearrange("p a b -> p (a b)")[:, 0:C * INNER].rearrange("p (c n) -> p c n", c=C),
                 "wk": probs[1][:, :, :].rearrange("p a b -> p (a b)")[:, 0:C * INNER].rearrange("p (c n) -> p c n", c=C),
                 "wv": probs_t[0][:, 0:2, :]}
        ctx_rows, lin_rows, tern_rows, above = xr[:, :, :], x3[:, 0:2, :], z0[:, 0:2, :], z0[:, 2:4, :]
        MEDIA_W, MEDIA_B, LAT_W, LAT_B = range(4)
        slots = [(), (0, 1), (2,), (3, 4)]
        SCALAR_CHUNKS = (1, 2, 3)
        pair_turns = {2 * c + 3: c for c in range(CH - 1)}

        def ev_wait(eng, j, n):
            turn, n = (-1, n + 5 * H) if n < 0 else (0, n)
            hh, fc = n // 5, n % 5
            if fc in SCALAR_CHUNKS:
                eng.wait_ge(ev_act.sem, ev_act.at(j, 3 * hh + fc + 24 * turn))
            else:
                eng.wait_ge(ev_dve.sem, ev_dve.at(j, 2 * hh + fc // 4 + 1 + 16 * turn))

        @block.sync
        def _(sp):
            sp.dma_start(ctx_rows, ctx.rearrange("b s d -> (b s) d").rearrange("(t p) d -> p t d", p=P)).then_inc(ld_ctx.sem, 16)
            for k, name in enumerate(("media_w", "media_b", "lat_w", "lat_b")):
                sp.dma_start(affine[:, k, :], wts[name].rearrange("(c p) -> p c", p=P),
                             allow_slow_non_contiguous=True).then_inc(ld_misc.sem, 16)
            sp.dma_start(lin_rows, wts["lin"].rearrange("(t p) d -> p t d", p=P)).then_inc(ld_misc.sem, 16)
            sp.dma_start(w_out[:, :, :], wts["wout"].rearrange("(c p) d -> p c d", p=P)).then_inc(ld_misc.sem, 16)
            for n in names:
                sp.dma_start(w_raw[n], wts[n].rearrange("(c p) n -> p c n", p=P)).then_inc(ld_w[n].sem, 16)

            def load_z(j):
                sp.wait_ge(z0_done.sem, z0_done.at(j, 0))
                sp.dma_start(xz[:, :, :], x2_dram[bass.ds(j * N, N), :].rearrange("(t p) d -> p t d", p=P)).then_inc(xz_in.sem, 16)

            def rows_through(j):
                sp.wait_ge(x3_done.sem, x3_done.at(j, 0))
                sp.dma_start(xr[:, :, :], x2_dram[bass.ds(j * N, N), :].rearrange("(t p) d -> p t d", p=P)).then_inc(xr_in.sem, 16)

            def store(j):
                sp.wait_ge(y_done.sem, y_done.at(j, 2))
                sp.dma_start(out_dram[bass.ds(j * N, N), :].rearrange("(t p) d -> p t d", p=P), x3[:, :, :]).then_inc(kept.sem, 16)

            load_z(0)
            sp.wait_ge(s_dve.sem, SETUP_DVE)
            with sp.Fori(0, B - 1) as i:
                rows_through(i)
                load_z(i + 1)
                store(i)
            rows_through(B - 1)
            store(B - 1)
            sp.wait_ge(kept.sem, kept.at(B, 0))

        @block.gpsimd
        def _(pool):
            chain = Chain(pool, s_pool.sem)
            chain.link(pool.memset(ones[:, :], 1.0))
            for e in range(2):
                for q in (q_hi[e], q_lo[e]):
                    chain.wait()
                    chain.link(pool.memset(q[64 * (1 - e):64 * (1 - e) + 64, :, :].bitcast(U32), 0))
            for s in (z0_done, exp_done, turned, ev_act, ev_dve, av_done, heads_done, x3_done, f_lo, y_done, kept):
                pool.sem_inc(s.sem, s.start)

            def rsqrt(chain, var, rs, j, k, which):
                wait_apart(pool, var.sem, var.at(j, k), passed.sem)
                chain.link(pool.tensor_scalar(var_eps[:, which, :], mean_var[:, which, :, 1], EPS, None, ALU.add))
                chain.wait()
                pool.tensor_tensor(rstd[:, which, :], var_eps[:, which, :], neghalf[:, 0:T], ALU.pow).then_inc(rs.sem, 1)

            pool.wait_ge(s_dve.sem, 2)
            chain.link(pool.tensor_scalar(var_eps[:, 0, :], mean_var[:, 0, :, 1], EPS, None, ALU.add))
            chain.wait()
            chain.link(pool.tensor_tensor(rstd[:, 0, :], var_eps[:, 0, :], neghalf[:, 0:T], ALU.pow))

            def values_of_context(j):
                wait_apart(pool, av_done.sem, av_done.at(j, 0), passed.sem)
                pool.tensor_copy(v_ctx[:, :], ctx_v[:, bass.ds(j, 1), :].rearrange("p a n -> p (a n)")).then_inc(vctx_done.sem, 1)

            def turn(j, more, chain):
                if more:
                    rsqrt(chain, var_z, rs_z, j + 1, 1, 0)
                    rsqrt(chain, var_z, rs_z, j + 1, 2, 1)
                if more:
                    values_of_context(j + 1)
                rsqrt(chain, var_x, rs_x, j, 1, 2)

            pool.wait_ge(s_act.sem, SETUP_ACT)
            first = Chain(pool, pool_own.sem)
            rsqrt(first, var_z, rs_z, 0, 1, 0)
            rsqrt(first, var_z, rs_z, 0, 2, 1)
            values_of_context(0)
            with pool.Fori(0, B - 1) as i:
                turn(i, True, Chain(pool, pool_own.sem, i * 3 + 2))
            turn(B - 1, False, Chain(pool, pool_own.sem, (B - 1) * 3 + 2))

        @block.tensor
        def _(pe):
            n = [0]

            def setup_step(last):
                last.then_inc(s_pe.sem, 1)
                n[0] += 1

            pe.wait_ge(s_dve.sem, 3)
            for c in range(C):
                for t in range(B * S // P):
                    last = pe.transpose(turn_b[c][:, t * P:(t + 1) * P], z1[:, t, c * P:(c + 1) * P], ident[:, :])
                setup_step(last)
            pe.wait_ge(s_pool.sem, 5)
            pe.wait_ge(s_dve.sem, 4)
            setup_step(pe.matmul(sum_b[0][:, 0:1], ones[:, :], wscale[:, 0:1], start=True, stop=True))
            pe.wait_ge(s_dve.sem, 8)
            for c in range(C):
                for t in range(D // P):
                    last = pe.transpose(sum_b[c][:, t * P:(t + 1) * P], tern_rows[:, t, c * P:(c + 1) * P], ident[:, :])
                setup_step(last)
            pe.wait_ge(s_dve.sem, 12)
            for c in range(CH):
                for d in range(C):
                    last = three_pass(pe, pool4[c], w_hi["wk"][:, d, c * P:(c + 1) * P], w_lo["wk"][:, d, c * P:(c + 1) * P],
                                      z_hi[:, d, :], z_lo[:, d, :], d == 0, d == C - 1)
                setup_step(last)
            for b in range(B):
                if b < 4:
                    pe.wait_ge(s_dve.sem, 12 + b + 1)
                else:
                    pe.wait_ge(s_act.sem, SETUP_ACT - B + b - 4 + 1)
                for d in range(C):
                    last = three_pass(pe, pool4[b % 4][0:S, :], z_hi[:, d, b * S:(b + 1) * S], z_lo[:, d, b * S:(b + 1) * S],
                                      w_hi["wv"][:, d, :], w_lo["wv"][:, d, :], d == 0, d == C - 1)
                setup_step(last)
            pe.wait_ge(s_act.sem, SETUP_ACT)

            def turn_rows(j, c):
                if c == 0:
                    pe.wait_ge(z1_done.sem, z1_done.at(j, 1))
                    pe.wait_ge(y_done.sem, y_done.at(j, 0 - 2))
                else:
                    pe.wait_ge(proj_act.sem, proj_act.at(j, c))
                for t in range(T):
                    last = pe.transpose(sum_b[1][:, t * P:(t + 1) * P], z1[:, t, c * P:(c + 1) * P], ident[:, :])
                last.then_inc(proj_done.sem, 1)

            def project(j, first, last_one):
                if first == 2:
                    pe.wait_ge(exp_done.sem, exp_done.at(j, 0))
                    pe.wait_ge(zlo_done.sem, zlo_done.at(j, 1))
                for u in range(first, last_one + 1):
                    if 6 <= u < 10:
                        pe.wait_ge(proj_act.sem, proj_act.at(j, u - 4 + 1))
                    elif u >= 10:
                        pe.wait_ge(proj_dve.sem, proj_dve.at(j, u - 10 + 1))
                    o = pool4[u % 4]
                    for d in range(C):
                        if u >= 6:
                            name, c = ("wq", u - 6) if u < 10 else ("wk", u - 10)
                            cols = slice(c * P, (c + 1) * P)
                            last = three_pass(pe, o, w_hi[name][:, d, cols], w_lo[name][:, d, cols],
                                              z_hi[:, d, :], z_lo[:, d, :], d == 0, d == C - 1)
                        else:
                            cols = slice((u - 2) * P, (u - 1) * P)
                            last = three_pass(pe, o, z_hi[:, d, cols], z_lo[:, d, cols],
                                              w_hi["wv"][:, d, :], w_lo["wv"][:, d, :], d == 0, d == C - 1)
                    last.then_inc(proj_done.sem, 1)

            def scores(j, hh, t):
                k = T * hh + t
                if k >= 2:
                    pe.wait_ge(exp_done.sem, exp_done.at(j, k + 1 - 2))
                c, e = hh // 2, hh % 2
                cols = slice(t * P, (t + 1) * P)
                for o, hi, lo in ((score_b[k % 2][:, 0:N], k_hi[:, c, :], k_lo[:, c, :]),
                                  (score_b[k % 2][:, N:F], ctx_k_hi[:, c, bass.ds(j * S, S)], ctx_k_lo[:, c, bass.ds(j * S, S)])):
                    last = three_pass(pe, o, q_hi[e][:, c, cols], q_lo[e][:, c, cols], hi, lo, True, True)
                last.then_inc(score_done.sem, 1)

            def turn_probs(j, hh, fc):
                n = 5 * hh + fc
                if fc == 0:
                    pe.wait_ge(norm_done.sem, norm_done.at(j, T * hh + T))
                ev_wait(pe, j, n - 2)
                if n < 2:
                    pe.wait_ge(f_lo.sem, f_lo.at(j, n + 1 - 2))
                w = P if fc < T else S
                if w < P:
                    pe.sem_inc(passed.sem, 1)
                for t in range(T):
                    last = pe.transpose(turn_b[n % 2][0:w, t * P:(t + 1) * P], probs[hh % 2][:, t, fc * P:fc * P + w], ident[:, :])
                last.then_inc(turned.sem, 1)

            def weigh_values(j, c):
                for n in (5 * (2 * c + 1) + 3, 5 * (2 * c + 1) + 4):
                    ev_wait(pe, j, n)
                pe.wait_ge(heads_done.sem, heads_done.at(j, c + 1 - 1))
                if c == 0:
                    pe.wait_ge(vctx_done.sem, vctx_done.at(j, 1))
                    pe.wait_ge(y_done.sem, y_done.at(j, 1 - 2))
                for fc in range(T + 1):
                    for e in range(2):
                        cols = slice((2 * c + e) * DH, (2 * c + e + 1) * DH)
                        v = v_rows[:, fc, cols] if fc < T else v_ctx[:, cols]
                        w = P if fc < T else S
                        last = pe.matmul(sum_b[0][DH * e:DH * e + DH, :], v, probs_t[e][0:w, fc, :],
                                         start=(fc == 0), stop=(fc == T))
                last.then_inc(av_done.sem, 1)

            def attend(j, more):
                pe.wait_ge(proj_act.sem, proj_act.at(j, 14))
                pe.wait_ge(proj_dve.sem, proj_dve.at(j, 8))
                for hh in range(H + 1):
                    for t in range(T):
                        if hh < H:
                            scores(j, hh, t)
                        if t == 0 and more and hh == H:
                            turn_rows(j + 1, 1)
                        if t == 1 and hh in pair_turns:
                            weigh_values(j, pair_turns[hh])
                        if hh > 0:
                            for fc in slots[t]:
                                turn_probs(j, hh - 1, fc)
                    if more and hh == H - 1:
                        turn_rows(j + 1, 0)
                weigh_values(j, CH - 1)

            def out_product(j, more):
                pe.wait_ge(heads_done.sem, heads_done.at(j, CH))
                if more:
                    pe.wait_ge(proj_act.sem, proj_act.at(j + 1, C))
                else:
                    pe.wait_ge(y_done.sem, y_done.at(j, 0))
                for half in range(2):
                    for t in (2 * half, 2 * half + 1):
                        for c in range(CH):
                            last = pe.matmul(sum_b[half][:, (t % 2) * D:(t % 2 + 1) * D], heads[:, c, t * P:(t + 1) * P],
                                             w_out[:, c, :], start=(c == 0), stop=(c == CH - 1))
                    last.then_inc(wout_done.sem, 1)

            def ternary_rows(j):
                pe.wait_ge(r3_done.sem, r3_done.at(j, 1))
                for c in range(C):
                    ev_wait(pe, j, 5 * H - 2 + c)
                    for t in range(T):
                        last = pe.transpose(turn_b[c][:, t * P:(t + 1) * P], z0[:, t, c * P:(c + 1) * P], ident[:, :])
                    last.then_inc(ft_done.sem, 1)

            def ternary_product(j):
                pe.wait_ge(f_lo.sem, f_lo.at(j, 2))
                for half in range(2):
                    for t in (2 * half, 2 * half + 1):
                        for c in range(C):
                            o = sum_b[half][:, (t % 2) * D:(t % 2 + 1) * D]
                            pe.matmul(o, r_lo[:, c, t * P:(t + 1) * P], ternary[:, c, :], start=(c == 0), stop=False)
                            last = pe.matmul(o, r_hi[:, c, t * P:(t + 1) * P], ternary[:, c, :], start=False, stop=(c == C - 1))
                    last.then_inc(ff_done.sem, 1)

            for c in range(C):
                turn_rows(0, c)
            project(0, 2, 13)
            with pe.Fori(0, B - 1) as i:
                attend(i, True)
                project(i + 1, 2, 5)
                out_product(i, True)
                project(i + 1, 6, 11)
                ternary_rows(i)
                project(i + 1, 12, 13)
                ternary_product(i)
            attend(B - 1, False)
            out_product(B - 1, False)
            ternary_rows(B - 1)
            ternary_product(B - 1)

        @block.scalar
        def _(act):
            for n in names:
                act.wait_ge(ld_w[n].sem, 16)
                act.activation(w_hi[n][:, :, :], w_raw[n], ACT.Copy).then_inc(s_act.sem, 1)
            act.wait_ge(ld_misc.sem, 96)
            act.wait_ge(s_pe.sem, 2)
            for c in range(C):
                last = act.activation(zt[:, c, :], turn_b[c][:, :], ACT.Identity,
                                      bias=affine[:, MEDIA_B, c:c + 1], scale=affine[:, MEDIA_W, c:c + 1])
            last.then_inc(s_act.sem, 1)
            act.wait_ge(s_act.sem, 4)
            act.activation(z_hi[:, :, :], zt[:, :, :], ACT.Copy).then_inc(s_act.sem, 1)
            for c in range(C):
                act.wait_ge(s_pe.sem, 4 + c)
                act.activation(ternary[:, c, :], sum_b[c][:, 0:D], ACT.Copy, scale=-1.0).then_inc(s_act.sem, 1)
            for c in range(CH):
                act.wait_ge(s_pe.sem, 6 + c)
                act.activation(ctx_k_hi[:, c, :], pool4[c], ACT.Copy).then_inc(s_act.sem, 1)
            for b in range(B):
                act.wait_ge(s_pe.sem, 10 + b)
                act.activation(ctx_v[:, b, :], pool4[b % 4][0:S, :], ACT.Copy).then_inc(s_act.sem, 1)

            def take_rows(j, c):
                if c < C:
                    act.wait_ge(proj_done.sem, proj_done.at(j, c + 1))
                    act.activation(zt[:, c, :], sum_b[1][:, :], ACT.Identity, bias=affine[:, LAT_B, c:c + 1],
                                   scale=affine[:, LAT_W, c:c + 1]).then_inc(proj_act.sem, 1)
                else:
                    act.wait_ge(proj_act.sem, proj_act.at(j, C))
                    act.activation(z_hi[:, :, :], zt[:, :, :], ACT.Copy).then_inc(zhi_done.sem, 1)

            def project(j, first, last_one):
                for u in range(first, last_one + 1):
                    act.wait_ge(proj_done.sem, proj_done.at(j, u + 1))
                    o = pool4[u % 4]
                    if u < 6:
                        last = act.activation(v_rows[:, u - 2, :], o, ACT.Copy)
                    elif u < 10:
                        act.activation(q_hi[0][0:64, u - 6, :], o[0:64, :], ACT.Copy, scale=SCALE)
                        last = act.activation(q_hi[1][64:128, u - 6, :], o[64:128, :], ACT.Copy, scale=SCALE)
                    else:
                        last = act.activation(k_hi[:, u - 10, :], o, ACT.Copy)
                    last.then_inc(proj_act.sem, 1)

            def take_chunk(j, hh, fc):
                n = 5 * hh + fc
                act.wait_ge(turned.sem, turned.at(j, n + 1))
                if fc == 1:
                    act.wait_ge(av_done.sem, av_done.at(j, hh // 2))
                act.activation(probs_t[hh % 2][:, fc, :], turn_b[n % 2][:, :], ACT.Copy).then_inc(ev_act.sem, 1)

            def attend(j, more):
                def take_heads(c):
                    act.wait_ge(av_done.sem, av_done.at(j, c + 1))
                    act.activation(heads[:, c, :], sum_b[0][:, :], ACT.Copy).then_inc(heads_done.sem, 1)

                for hh in range(H + 1):
                    if more and hh == H:
                        take_rows(j + 1, 0)
                        take_rows(j + 1, 1)
                    for t in range(T):
                        if hh < H:
                            k = T * hh + t
                            if t == 0:
                                act.wait_ge(turned.sem, turned.at(j, 5 * hh + 5 - 10))
                            act.wait_ge(max_done.sem, max_done.at(j, k + 1))
                            act.activation(probs[hh % 2][:, t, :], score_b[k % 2][:, 0:F], ACT.Exp, bias=nmax[:, k:k + 1],
                                           accum_out=sums[:, k:k + 1]).then_inc(exp_done.sem, 1)
                        if t == 1 and hh in pair_turns:
                            take_heads(pair_turns[hh])
                        if hh > 0:
                            for fc in slots[t]:
                                if fc in SCALAR_CHUNKS:
                                    take_chunk(j, hh - 1, fc)
                        if t == 1 and more and hh == H:
                            take_rows(j + 1, C)
                take_heads(CH - 1)

            def split_rows(j):
                for c in range(C):
                    act.wait_ge(ft_done.sem, ft_done.at(j, c + 1))
                    act.activation(r_hi[:, c, :], turn_b[c][:, :], ACT.Copy).then_inc(f_hi.sem, 1)

            for c in range(C + 1):
                take_rows(0, c)
            project(0, 2, 13)
            with act.Fori(0, B - 1) as i:
                attend(i, True)
                project(i + 1, 2, 11)
                split_rows(i)
                project(i + 1, 12, 13)
            attend(B - 1, False)
            split_rows(B - 1)

        @block.vector
        def _(dve):
            def moments(chain, src, which):
                for t in range(T):
                    last = dve.bn_stats(stats[:, t, :], src[:, t, :])
                chain.link(last)
                chain.wait_apart(passed.sem)
                for t in range(T):
                    last = dve.bn_aggr(mean_var[:, which, t, :], stats[:, t, :])
                return last

            def normalise(dst, src, which):
                for t in range(T):
                    last = dve.tensor_scalar(dst[:, t, :], src[:, t, :], mean_var[:, which, t, 0:1], rstd[:, which, t:t + 1],
                                             ALU.subtract, ALU.mult)
                return last

            chain = Chain(dve, s_dve.sem)
            dve.wait_ge(ld_ctx.sem, 16)
            chain.link(moments(chain, ctx_rows, 0))
            dve.wait_ge(s_pool.sem, 7)
            dve.wait_ge(s_dve.sem, 2)
            chain.link(normalise(z1, ctx_rows, 0))
            dve.wait_ge(ld_misc.sem, 96)
            chain.link(dve.tensor_reduce(out=wscale[:, 0:1], in_=lin_rows.rearrange("p a b -> p (a b)"), op=ALU.add, axis=AXX,
                                         apply_absolute_value=True))
            dve.wait_ge(s_pe.sem, 3)
            chain.link(dve.tensor_scalar(wscale[:, 1:2], sum_b[0][:, 0:1], 1.0 / (D * D), EPS, ALU.mult, ALU.max))
            chain.wait()
            chain.link(dve.tensor_scalar(wscale[:, 2:3], wscale[:, 1:2], -0.5, None, ALU.mult))
            chain.wait()
            chain.link(dve.tensor_scalar(above, lin_rows, -1.0, wscale[:, 2:3], ALU.mult, ALU.is_lt))
            chain.wait()
            chain.link(dve.scalar_tensor_tensor(tern_rows, lin_rows, wscale[:, 2:3], above, ALU.is_lt, ALU.subtract))
            for k, n in enumerate(names):
                dve.wait_ge(s_act.sem, k + 1)
                chain.link(dve.tensor_tensor(w_lo[n][:, :, :], w_raw[n], w_hi[n][:, :, :].bitcast(F32), ALU.subtract))
            dve.wait_ge(s_act.sem, 5)
            chain.link(dve.tensor_tensor(z_lo[:, :, :], zt[:, :, :], z_hi[:, :, :].bitcast(F32), ALU.subtract))
            for c in range(CH):
                dve.wait_ge(s_act.sem, 7 + c + 1)
                chain.link(dve.tensor_tensor(ctx_k_lo[:, c, :], pool4[c], ctx_k_hi[:, c, :].bitcast(F32), ALU.subtract))
            assert chain.n == SETUP_DVE, chain.n

            def prepare(j, chain, step):
                if step == 0:
                    dve.wait_ge(xz_in.sem, xz_in.at(j, 16))
                    moments(chain, xz, 0).then_inc(var_z.sem, 1)
                elif step == 1:
                    dve.wait_ge(rs_z.sem, rs_z.at(j, 1))
                    dve.wait_ge(var_z.sem, var_z.at(j, 1))
                    normalise(z0, xz, 0).then_inc(z0_done.sem, 1)
                    dve.wait_ge(z0_done.sem, z0_done.at(j, 1))
                    moments(chain, z0, 1).then_inc(var_z.sem, 1)
                else:
                    dve.wait_ge(rs_z.sem, rs_z.at(j, 2))
                    dve.wait_ge(var_z.sem, var_z.at(j, 2))
                    normalise(z1, z0, 1).then_inc(z1_done.sem, 1)

            def split_low(j):
                dve.wait_ge(zhi_done.sem, zhi_done.at(j, 1))
                dve.tensor_tensor(z_lo[:, :, :], zt[:, :, :], z_hi[:, :, :].bitcast(F32), ALU.subtract).then_inc(zlo_done.sem, 1)

            def project(j, first, last_one):
                for u in range(first, last_one + 1):
                    dve.wait_ge(proj_act.sem, proj_act.at(j, u + 1))
                    o = pool4[u % 4]
                    if u < 10:
                        for e in range(2):
                            on = slice(64 * e, 64 * e + 64)
                            last = dve.scalar_tensor_tensor(q_lo[e][on, u - 6, :], o[on, :], SCALE,
                                                            q_hi[e][on, u - 6, :].bitcast(F32), ALU.mult, ALU.subtract)
                    else:
                        last = dve.tensor_tensor(k_lo[:, u - 10, :], o, k_hi[:, u - 10, :].bitcast(F32), ALU.subtract)
                    last.then_inc(proj_dve.sem, 1)

            def invert(j, k):
                dve.wait_ge(exp_done.sem, exp_done.at(j, k + 1))
                dve.reciprocal(inv[:, k:k + 1], sums[:, k:k + 1]).then_inc(inv_done.sem, 1)
                dve.wait_ge(inv_done.sem, inv_done.at(j, k + 1))
                p = probs[k // T % 2][:, k % T, :]
                dve.tensor_scalar(p, p, inv[:, k:k + 1], None, ALU.mult).then_inc(norm_done.sem, 1)

            def take_chunk(j, hh, fc):
                n = 5 * hh + fc
                dve.wait_ge(turned.sem, turned.at(j, n + 1))
                if fc == 0:
                    dve.wait_ge(av_done.sem, av_done.at(j, hh // 2))
                w = P if fc < T else S
                dve.tensor_copy(probs_t[hh % 2][0:w, fc, :], turn_b[n % 2][0:w, :]).then_inc(ev_dve.sem, 1)

            def attend(j, more, chain):
                for hh in range(H + 1):
                    for t in range(T):
                        k = T * hh + t
                        if t == 0 and hh > 0:
                            invert(j, k - 1)
                        if hh < H:
                            dve.wait_ge(score_done.sem, score_done.at(j, k + 1))
                            dve.tensor_reduce(out=nmax[:, k:k + 1], in_=score_b[k % 2][:, 0:F], op=ALU.max, axis=AXX,
                                              negate=True).then_inc(max_done.sem, 1)
                        if t > 0 and hh < H:
                            invert(j, k - 1)
                        if t == 1 and more and hh in pair_turns:
                            prepare(j + 1, chain, pair_turns[hh])
                        if hh > 0:
                            for fc in slots[t]:
                                if fc not in SCALAR_CHUNKS:
                                    take_chunk(j, hh - 1, fc)
                if more:
                    split_low(j + 1)

            def add_attention(j, chain, more):
                dve.wait_ge(xr_in.sem, xr_in.at(j, 16))
                dve.wait_ge(kept.sem, kept.at(j, 0))
                for half in range(2):
                    dve.wait_ge(wout_done.sem, wout_done.at(j, half + 1))
                    dve.tensor_tensor(x3[:, 2 * half:2 * half + 2, :], xr[:, 2 * half:2 * half + 2, :],
                                      sum_b[half][:, :].rearrange("p (t d) -> p t d", t=2), ALU.add).then_inc(x3_done.sem, 1)
                dve.wait_ge(x3_done.sem, x3_done.at(j, 2))
                moments(chain, x3, 2).then_inc(var_x.sem, 1)
                if more:
                    project(j + 1, 6, 7)
                dve.wait_ge(rs_x.sem, rs_x.at(j, 1))
                dve.wait_ge(var_x.sem, var_x.at(j, 1))
                normalise(z0, x3, 2).then_inc(r3_done.sem, 1)

            def split_rows(j):
                for c in range(C):
                    dve.wait_ge(f_hi.sem, f_hi.at(j, c + 1))
                    dve.tensor_tensor(r_lo[:, c, :], turn_b[c][:, :], r_hi[:, c, :].bitcast(F32), ALU.subtract).then_inc(f_lo.sem, 1)

            def finish(j):
                for half in range(2):
                    dve.wait_ge(ff_done.sem, ff_done.at(j, half + 1))
                    x = x3[:, 2 * half:2 * half + 2, :].rearrange("p t d -> p (t d)")
                    dve.scalar_tensor_tensor(x, sum_b[half][:, :], wscale[:, 1:2], x, ALU.mult, ALU.add).then_inc(y_done.sem, 1)

            first = Chain(dve, dve_own.sem)
            for step in range(3):
                prepare(0, first, step)
            split_low(0)
            project(0, 6, 13)
            with dve.Fori(0, B - 1) as i:
                chain = Chain(dve, dve_own.sem, i * 3 + 2)
                attend(i, True, chain)
                add_attention(i, chain, True)
                project(i + 1, 8, 11)
                split_rows(i)
                project(i + 1, 12, 13)
                finish(i)
                assert chain.n == 3, chain.n
            chain = Chain(dve, dve_own.sem, (B - 1) * 3 + 2)
            attend(B - 1, False, chain)
            add_attention(B - 1, chain, False)
            split_rows(B - 1)
            finish(B - 1)


def build(nc, x, ctx, gamma, beta, w_q, keys, key_in, key_out, media_w, media_b, lat_w, lat_b, wq, wk, wv, wout, lin, out):
    B, N, D = x.shape
    with ExitStack() as whole:
        ident = whole.enter_context(nc.sbuf_tensor("ident", [P, P], F32))
        neghalf = whole.enter_context(nc.sbuf_tensor("neghalf", [P, 8], F32))
        bn = whole.enter_context(nc.sbuf_tensor("bn", [P, 2, D // P], F32))
        cst = {"ident": ident, "neghalf": neghalf, "bn": bn, "gamma": gamma, "beta": beta}
        x1 = nc.dram_tensor("x1_rows", (B, N, D), F32).ap()
        xt = nc.dram_tensor("x1_norm_t", (D // P, P, B * N), F32).ap()
        x2 = nc.dram_tensor("x2_rows", (B * N, D), F32).ap()
        with ExitStack() as tables:
            rows = (P, key_in.shape[0] // P, D)
            cst["key_rows"] = tables.enter_context(nc.sbuf_tensor("key_rows", rows, F32))
            cst["key_up"] = tables.enter_context(nc.sbuf_tensor("key_up", rows, F32))
            cst["key_in"], cst["key_out"] = key_in, key_out
            attend_context(nc, x, ctx, x1, xt, cst)
            retrieve_experts(nc, xt, x1.rearrange("b n d -> (b n) d"), w_q, keys, x2, cst)
        wts = {"media_w": media_w, "media_b": media_b, "lat_w": lat_w, "lat_b": lat_b,
               "wq": wq, "wk": wk, "wv": wv, "wout": wout, "lin": lin}
        attend_latents(nc, ctx, x2, wts, out.rearrange("b n d -> (b n) d"), cst)


_INS = ["x", "ctx_1024", "L0_ffn_gamma", "L0_ffn_beta", "L0_ffn_w_q", "L0_ffn_keys", "L0_ffn_key_in", "L0_ffn_key_out",
        "L1_xattn_ln_media_w", "L1_xattn_ln_media_b", "L1_xattn_ln_lat_w", "L1_xattn_ln_lat_b",
        "L1_xattn_Wq", "L1_xattn_Wk", "L1_xattn_Wv", "L1_xattn_Wout", "L1_ffn_weight"]
_OUTS = [((8, 512, 256), "float32")]


def kernel(**inputs):
    import numpy as _np
    import concourse.bacc as _bacc
    from concourse import mybir as _mybir
    from concourse.bass_utils import run_bass_kernel_spmd as _run

    nc = _bacc.Bacc("TRN2", target_bir_lowering=False, num_devices=1)
    arrays, args = {}, []
    for name in _INS:
        a = _np.ascontiguousarray(inputs[name])
        arrays[f"in_{name}_dram"] = a
        args.append(nc.dram_tensor(f"in_{name}_dram", a.shape, _mybir.dt.from_np(a.dtype), kind="ExternalInput").ap())
    for i, (shape, dtype) in enumerate(_OUTS):
        dt = _mybir.dt.from_np(_np.dtype(dtype))
        args.append(nc.dram_tensor(f"out_{i}_dram", shape, dt, kind="ExternalOutput").ap())
    build(nc, *args)
    r = _run(nc, [arrays], core_ids=[0])
    got = tuple(r.results[0][f"out_{i}_dram"] for i in range(len(_OUTS)))
    return got if len(got) > 1 else got[0]
```

```python
import concourse.bass as bass
from concourse import mybir
from contextlib import ExitStack

F32 = mybir.dt.float32
F32R = mybir.dt.float32r
BF16 = mybir.dt.bfloat16
U32 = mybir.dt.uint32
ALU = mybir.AluOpType
ACT = mybir.ActivationFunctionType
AXX = mybir.AxisListType.X
AXXY = mybir.AxisListType.XY
P = 128
EPS = 1e-5
PICK_HALF = 32


class Signal:

    def __init__(self, sem, per, start=0):
        self.sem, self.per, self.start = sem, per, start

    def at(self, i, k):
        return i * self.per + (self.start + k)


class Chain:

    def __init__(self, eng, sem, base=0):
        self.eng, self.sem, self.base, self.n = eng, sem, base, 0

    def link(self, ins):
        ins.then_inc(self.sem, 1)
        self.n += 1
        return self.n

    def wait(self, k=None):
        self.eng.wait_ge(self.sem, self.base + (self.n if k is None else k))

    def wait_apart(self, passed):
        wait_apart(self.eng, self.sem, self.base + self.n, passed)


def three_pass(pe, out, w_hi, w_lo, x_hi, x_lo, start, stop):
    pe.matmul(out, w_lo, x_hi, start=start, stop=False)
    pe.matmul(out, w_hi, x_lo, start=False, stop=False)
    return pe.matmul(out, w_hi, x_hi, start=False, stop=stop)


def wait_apart(eng, sem, value, passed):
    eng.wait_ge(sem, value)
    eng.sem_inc(passed, 1)


def attend_context(nc, x, ctx, x1_dram, xt_dram, cst):
    B, N, D = x.shape
    S = ctx.shape[1]
    T, C = N // P, D // P
    PAIRS = D // 32
    SLICE = cst["key_rows"].shape[1] // B
    ident, neghalf, bn_out = cst["ident"], cst["neghalf"], cst["bn"]
    own = ExitStack()
    with own:
        def sb(name, shape, dt=F32):
            return own.enter_context(nc.sbuf_tensor(name, shape, dt))

        def two(name, shape, dt=F32):
            return [sb(f"{name}{p}", shape, dt) for p in range(2)]

        def sig(name, per=0, start=0):
            return Signal(own.enter_context(nc.semaphore(name)), per, start)

        bank = [own.enter_context(nc.psum_tensor(f"a_bank{i}", [P, 512], F32)) for i in range(8)]
        trans, score, value, back_b = bank[0:2], bank[2:6], bank[4:6], bank[6:8]

        ctx_rows = sb("a_ctx_rows", [P, B * S // P, D])
        ctx_hi, ctx_lo = sb("a_ctx_hi", [P, C, B * S], F32R), sb("a_ctx_lo", [P, C, B * S], F32R)
        ctx_twice = sb("a_ctx_twice", [P, B, D])
        mask_k = sb("a_mask_k", [P, 8])
        mask_v = sb("a_mask_v", [P, PAIRS, 2, 16])
        vals = two("a_vals", [P, D])
        keys_hi, keys_lo = two("a_keys_hi", [P, C, 8, S], F32R), two("a_keys_lo", [P, C, 8, S], F32R)
        xa, xr = sb("a_xa", [P, T, D]), sb("a_xr", [P, T, D])
        rows, rows1 = sb("a_rows", [P, T, D]), sb("a_rows1", [P, T, D])
        q_hi, q_lo = sb("a_q_hi", [P, C, N], F32R), sb("a_q_lo", [P, C, N], F32R)
        acts = two("a_acts", [P, PAIRS, N])
        attn_t = sb("a_attn_t", [P, C, N])
        x1 = sb("a_x1", [P, T, D])
        xt = sb("a_xt", [P, C, N])
        stats = sb("a_stats", [P, T, 6])
        mean_var, var_eps, rstd = two("a_mean_var", [P, T, 2]), two("a_var_eps", [P, T]), two("a_rstd", [P, T])
        bn_stats = sb("a_bn_stats", [P, C, B, 6])
        bn_mv = sb("a_bn_mv", [P, C, 2])
        bn_ve, bn_rs, bn_tmp = sb("a_bn_ve", [P, C]), sb("a_bn_rs", [P, C]), sb("a_bn_tmp", [P, C])
        gamma_beta = sb("a_gamma_beta", [P, 2, C])

        ctx_in, gb_in, tables_in = sig("a_ctx_in"), sig("a_gb_in"), sig("a_tables_in")
        xa_in, xr_in = sig("a_xa_in", 16), sig("a_xr_in", 16)
        consts, ctx_tr, ctx_ev, passed = sig("a_consts"), sig("a_ctx_tr"), sig("a_ctx_ev"), sig("a_passed")
        ctx_lo_done = sig("a_ctx_lo_done")
        var_x, rs_x, rows_done = sig("a_var_x", 1), sig("a_rs_x", 1), sig("a_rows_done", 1, 1)
        front_tr, q_hi_done, q_lo_done = sig("a_front_tr", 2), sig("a_q_hi_done", 2), sig("a_q_lo_done", 2)
        keys_ready, vals_ready = sig("a_keys_ready", 2 * C), sig("a_vals_ready", 1)
        score_done, silu_done = sig("a_score", 8, 16), sig("a_silu", 8, 4)
        value_done, attn_done = sig("a_value", 2, 4), sig("a_attn", 2, 2)
        back_tr, x1_done = sig("a_back_tr", 2), sig("a_x1_done", 2, 2)
        var_1, rs_1, rows1_done = sig("a_var_1", 1), sig("a_rs_1", 1), sig("a_rows1_done", 1)
        last_tr, xt_done, bn_taken = sig("a_last_tr", 2), sig("a_xt_done", 2), sig("a_bn_taken", C, 3 * C)
        x1_kept, xt_kept = sig("a_x1_kept", 16, 16), sig("a_xt_kept", 16, 16)
        dve_own, pool_own = sig("a_dve_own"), sig("a_pool_own")
        bn_var, bn_rs_ready, bn_done = sig("a_bn_var"), sig("a_bn_rs_ready"), sig("a_bn_done")
        block = own.enter_context(nc.Block())

        def steps(eng, step):
            step(0, 0, True, True, False)
            with eng.Fori(0, (B - 4) // 2) as i:
                step(2 * i + 1, 1, True, True, True)
                step(2 * i + 2, 0, True, True, True)
            step(B - 3, 1, True, True, True)
            step(B - 2, 0, True, False, True)
            step(B - 1, 1, False, False, True)

        def at_batch(dram, b):
            return dram[bass.ds(b, 1), :, :].rearrange("a (t p) d -> p (a t) d", p=P)

        def spread_keys(eng, b, p, c):
            if c == 0:
                eng.wait_ge(score_done.sem, score_done.at(b, 0 - PAIRS))
            for dst, src in ((keys_hi[p], ctx_hi), (keys_lo[p], ctx_lo)):
                eng.tensor_tensor(dst[:, c, :, :], src[:, c, bass.ds(b * S, S)].unsqueeze(1).to_broadcast([P, 8, S]).bitcast(F32),
                                  mask_k[:, :].unsqueeze(2).to_broadcast([P, 8, S]), ALU.mult).then_inc(keys_ready.sem, 1)

        def links_before(b):
            return 2 + (2 * b if not isinstance(b, int) or b <= B - 2 else B - 2 + b)

        @block.sync
        def _(sp):
            def load_a(b):
                sp.wait_ge(rows_done.sem, rows_done.at(b, 0))
                sp.dma_start(xa[:, :, :], at_batch(x, b)).then_inc(xa_in.sem, 16)

            load_a(0)
            sp.dma_start(ctx_rows[:, :, :], ctx.rearrange("b s d -> (b s) d")
                         .rearrange("(t p) d -> p t d", p=P)).then_inc(ctx_in.sem, 16)
            for half in range(2):
                sp.dma_start(ctx_twice[64 * half:64 * half + 64, :, :],
                             ctx.rearrange("b s d -> s b d")).then_inc(ctx_in.sem, 16)
            load_a(1)
            for k, name in enumerate(("gamma", "beta")):
                sp.dma_start(gamma_beta[:, k, :], cst[name].rearrange("(c p) -> p c", p=P),
                             allow_slow_non_contiguous=True).then_inc(gb_in.sem, 16)

            def load_r(b):
                sp.wait_ge(x1_done.sem, x1_done.at(b, 0))
                sp.dma_start(xr[:, :, :], at_batch(x, b)).then_inc(xr_in.sem, 16)

            load_r(0)
            load_a(2)

            def step(b, p, front, ahead, back):
                if not isinstance(b, int) or b == 0:
                    load_a(b + 3)
                for dst, src in ((cst["key_rows"], cst["key_in"]), (cst["key_up"], cst["key_out"])):
                    sp.dma_start(dst[:, bass.ds(b * SLICE, SLICE), :],
                                 src.rearrange("(u v) d -> u v d", u=P)[:, bass.ds(b * SLICE, SLICE), :]).then_inc(tables_in.sem, 16)
                if not back:
                    for dst, src in cst["key_loads"]:
                        sp.dma_start(dst, src).then_inc(tables_in.sem, 16)
                sp.wait_ge(x1_done.sem, x1_done.at(b, 2))
                sp.dma_start(at_batch(x1_dram, b), x1[:, :, :]).then_inc(x1_kept.sem, 16)
                if front:
                    load_r(b + 1)

            steps(sp, step)
            sp.wait_ge(tables_in.sem, 16 * (2 * B + len(cst["key_loads"])))
            sp.wait_ge(x1_kept.sem, x1_kept.at(B, 0))

        @block.gpsimd
        def _(pool):
            setup = Chain(pool, consts.sem)
            setup.link(pool.memset(ident[:, :], 0.0))
            setup.link(pool.memset(mask_k[:, :], 1.0))
            setup.link(pool.memset(neghalf[:, :], -0.5))
            setup.link(pool.memset(mask_v[:, :, :, :], 0.0))
            setup.wait()
            setup.link(pool.affine_select(out=ident[:, :], in_=ident[:, :], compare_op=ALU.not_equal, fill=1.0,
                                          base=0, pattern=[[-1, P]], channel_multiplier=1))
            setup.link(pool.affine_select(out=mask_k[:, :], in_=mask_k[:, :], compare_op=ALU.is_ge, fill=0.0,
                                          base=0, pattern=[[-16, 8]], channel_multiplier=1))
            for half in range(2):
                setup.wait()
                setup.link(pool.memset(mask_v[64 * half:64 * half + 64, :, half, :], 1.0))
            setup.wait()
            setup.link(pool.affine_select(out=mask_k[:, :], in_=mask_k[:, :], compare_op=ALU.is_ge, fill=0.0,
                                          base=15, pattern=[[16, 8]], channel_multiplier=-1))
            setup.wait()
            for s in (rows_done, score_done, silu_done, value_done, attn_done, x1_done, bn_taken, x1_kept, xt_kept):
                pool.sem_inc(s.sem, s.start)

            def rsqrt(var, rs, b, which, chain):
                wait_apart(pool, var.sem, var.at(b, 1), passed.sem)
                chain.link(pool.tensor_scalar(var_eps[which][:, :], mean_var[which][:, :, 1], EPS, None, ALU.add))
                chain.wait()
                pool.tensor_tensor(rstd[which][:, :], var_eps[which][:, :], neghalf[:, 0:T], ALU.pow).then_inc(rs.sem, 1)

            def spread_values(b, p):
                pool.wait_ge(value_done.sem, value_done.at(b, 0 - C))
                pool.tensor_tensor(vals[p][:, :], ctx_twice[:, bass.ds(b, 1), :].rearrange("p a d -> p (a d)"),
                                   mask_v[:, :, :, :].rearrange("p a b c -> p (a b c)"), ALU.mult).then_inc(vals_ready.sem, 1)

            first = Chain(pool, pool_own.sem)
            rsqrt(var_x, rs_x, 0, 0, first)
            pool.wait_ge(ctx_in.sem, 48)
            spread_values(0, 0)
            pool.wait_ge(ctx_lo_done.sem, C)
            for c in range(C):
                spread_keys(pool, 1, 1, c)
            rsqrt(var_x, rs_x, 1, 0, first)
            spread_values(1, 1)

            def step(b, p, front, ahead, back):
                chain = Chain(pool, pool_own.sem, links_before(b))
                if ahead:
                    spread_keys(pool, b + 2, p, 0)
                    rsqrt(var_x, rs_x, b + 2, 0, chain)
                    for c in range(1, C):
                        spread_keys(pool, b + 2, p, c)
                rsqrt(var_1, rs_1, b, 1, chain)
                if ahead:
                    spread_values(b + 2, p)
                assert chain.n == (2 if ahead else 1), chain.n

            steps(pool, step)
            pool.wait_ge(bn_var.sem, 1)
            pool.tensor_scalar(bn_ve[:, :], bn_mv[:, :, 1], EPS, None, ALU.add).then_inc(bn_rs_ready.sem, 1)
            pool.wait_ge(bn_rs_ready.sem, 1)
            pool.tensor_tensor(bn_rs[:, :], bn_ve[:, :], neghalf[:, 0:C], ALU.pow).then_inc(bn_rs_ready.sem, 1)

        @block.tensor
        def _(pe):
            pe.wait_ge(consts.sem, 9)
            pe.wait_ge(ctx_in.sem, 48)
            for c in range(C):
                for t in range(B * S // P):
                    last = pe.transpose(trans[c][:, t * P:(t + 1) * P], ctx_rows[:, t, c * P:(c + 1) * P], ident[:, :])
                last.then_inc(ctx_tr.sem, 1)
            pe.wait_ge(ctx_ev.sem, C)
            pe.wait_ge(ctx_lo_done.sem, C)

            def front_turn(b):
                pe.wait_ge(rows_done.sem, rows_done.at(b, 1))
                for c in range(C):
                    pe.wait_ge(bn_taken.sem, bn_taken.at(b, c + 1 - 3 * C))
                    for t in range(T):
                        last = pe.transpose(trans[c][:, t * P:(t + 1) * P], rows[:, t, c * P:(c + 1) * P], ident[:, :])
                    last.then_inc(front_tr.sem, 1)

            def front_scores(b, p):
                pe.wait_ge(keys_ready.sem, keys_ready.at(b, 2 * C))
                pe.wait_ge(q_hi_done.sem, q_hi_done.at(b, C))
                pe.wait_ge(q_lo_done.sem, q_lo_done.at(b, C))
                for g in range(PAIRS):
                    c, pair = g // 4, g % 4
                    pe.wait_ge(silu_done.sem, silu_done.at(b, g + 1 - 4))
                    w_hi = keys_hi[p][:, c, 2 * pair:2 * pair + 2, :].rearrange("p a b -> p (a b)")
                    w_lo = keys_lo[p][:, c, 2 * pair:2 * pair + 2, :].rearrange("p a b -> p (a b)")
                    three_pass(pe, score[g % 4][:, :], w_hi, w_lo, q_hi[:, c, :], q_lo[:, c, :],
                               True, True).then_inc(score_done.sem, 1)

            def values(b, p, has_front):
                pe.wait_ge(silu_done.sem, silu_done.at(b, PAIRS))
                for c in range(C):
                    if has_front:
                        pe.wait_ge(silu_done.sem, silu_done.at(b + 1, PAIRS - C + c + 1))
                    pe.wait_ge(vals_ready.sem, vals_ready.at(b, 1))
                    pe.wait_ge(attn_done.sem, attn_done.at(b, c + 1 - 2))
                    for pair in range(4):
                        g = 4 * c + pair
                        last = pe.matmul(value[c][32 * pair:32 * pair + 32, :], vals[p][:, 32 * g:32 * g + 32],
                                         acts[p][:, g, :], start=True, stop=True)
                    last.then_inc(value_done.sem, 1)

            def values_back(b):
                pe.wait_ge(attn_done.sem, attn_done.at(b, C))
                for j in range(T // 2):
                    pe.wait_ge(x1_done.sem, x1_done.at(b, j + 1 - 2))
                    for t in (2 * j, 2 * j + 1):
                        for c in range(C):
                            last = pe.transpose(back_b[j][:, (t % 2) * D + c * P:(t % 2) * D + (c + 1) * P],
                                                attn_t[:, c, t * P:(t + 1) * P], ident[:, :])
                    last.then_inc(back_tr.sem, 1)

            def back(b):
                pe.wait_ge(rows1_done.sem, rows1_done.at(b, 1))
                for c in range(C):
                    pe.wait_ge(bn_taken.sem, bn_taken.at(b, c + 1 - C))
                    for t in range(T):
                        last = pe.transpose(trans[c][:, t * P:(t + 1) * P], rows1[:, t, c * P:(c + 1) * P], ident[:, :])
                    last.then_inc(last_tr.sem, 1)

            def step(b, p, has_front, ahead, has_back):
                if has_front:
                    front_scores(b + 1, 1 - p)
                if has_back:
                    back(b - 1)
                values(b, p, has_front)
                if ahead:
                    front_turn(b + 2)
                values_back(b)

            front_turn(0)
            front_scores(0, 0)
            front_turn(1)
            steps(pe, step)
            back(B - 1)

        @block.scalar
        def _(act):
            for c in range(C):
                act.wait_ge(ctx_tr.sem, c + 1)
                act.activation(ctx_hi[:, c, :], trans[c][:, :], ACT.Copy).then_inc(ctx_ev.sem, 1)

            def queries_high(b):
                for c in range(C):
                    act.wait_ge(front_tr.sem, front_tr.at(b, c + 1))
                    act.activation(q_hi[:, c, :], trans[c][:, :], ACT.Copy).then_inc(q_hi_done.sem, 1)

            def silus(b, p):
                for g in range(PAIRS):
                    act.wait_ge(score_done.sem, score_done.at(b, g + 1))
                    act.activation(acts[p][:, g, :], score[g % 4][:, :], ACT.Silu).then_inc(silu_done.sem, 1)

            def back(b):
                act.wait_ge(xt_kept.sem, xt_kept.at(b, 0))
                for c in range(C):
                    act.wait_ge(last_tr.sem, last_tr.at(b, c + 1))
                    act.activation(xt[:, c, :], trans[c][:, :], ACT.Copy).then_inc(xt_done.sem, 1)
                act.wait_ge(xt_done.sem, xt_done.at(b, C))
                act.dma_start(xt_dram[:, :, bass.ds(b * N, N)].rearrange("c p n -> p c n"), xt[:, :, :]).then_inc(xt_kept.sem, 16)

            def step(b, p, has_front, ahead, has_back):
                if has_front:
                    silus(b + 1, 1 - p)
                if has_back:
                    back(b - 1)
                for c in range(C):
                    act.wait_ge(value_done.sem, value_done.at(b, c + 1))
                    act.activation(attn_t[:, c, :], value[c][:, :], ACT.Copy).then_inc(attn_done.sem, 1)
                if ahead:
                    queries_high(b + 2)

            queries_high(0)
            silus(0, 0)
            queries_high(1)
            steps(act, step)
            back(B - 1)
            act.wait_ge(xt_kept.sem, xt_kept.at(B, 0))

        @block.vector
        def _(dve):
            def moments(chain, src, which):
                for t in range(T):
                    last = dve.bn_stats(stats[:, t, :], src[:, t, :])
                chain.link(last)
                chain.wait_apart(passed.sem)
                for t in range(T):
                    last = dve.bn_aggr(mean_var[which][:, t, :], stats[:, t, :])
                return last

            def normalise(dst, src, which):
                for t in range(T):
                    last = dve.tensor_scalar(dst[:, t, :], src[:, t, :], mean_var[which][:, t, 0:1], rstd[which][:, t:t + 1],
                                             ALU.subtract, ALU.mult)
                return last

            def front_moments(b, chain):
                dve.wait_ge(xa_in.sem, xa_in.at(b, 16))
                moments(chain, xa, 0).then_inc(var_x.sem, 1)

            def front_rows(b):
                dve.wait_ge(rs_x.sem, rs_x.at(b, 1))
                dve.wait_ge(var_x.sem, var_x.at(b, 1))
                normalise(rows, xa, 0).then_inc(rows_done.sem, 1)

            def queries_low(b):
                for c in range(C):
                    dve.wait_ge(q_hi_done.sem, q_hi_done.at(b, c + 1))
                    dve.tensor_tensor(q_lo[:, c, :], trans[c][:, :], q_hi[:, c, :].bitcast(F32),
                                      ALU.subtract).then_inc(q_lo_done.sem, 1)

            def back(b):
                for c in range(C):
                    dve.wait_ge(xt_done.sem, xt_done.at(b, c + 1))
                    dve.bn_stats(bn_stats[:, c, bass.ds(b, 1), :].rearrange("p a b -> p (a b)"), trans[c][:, :]) \
                        .then_inc(bn_taken.sem, 1)

            def step(b, p, has_front, ahead, has_back):
                chain = Chain(dve, dve_own.sem, links_before(b))
                if ahead:
                    front_moments(b + 2, chain)
                    front_rows(b + 2)
                if has_back:
                    back(b - 1)
                if ahead:
                    queries_low(b + 2)
                dve.wait_ge(xr_in.sem, xr_in.at(b, 16))
                dve.wait_ge(x1_kept.sem, x1_kept.at(b, 0))
                for j in range(T // 2):
                    dve.wait_ge(back_tr.sem, back_tr.at(b, j + 1))
                    dve.tensor_tensor(x1[:, 2 * j:2 * j + 2, :], xr[:, 2 * j:2 * j + 2, :],
                                      back_b[j][:, :].rearrange("p (t d) -> p t d", t=2), ALU.add).then_inc(x1_done.sem, 1)
                dve.wait_ge(x1_done.sem, x1_done.at(b, 2))
                moments(chain, x1, 1).then_inc(var_1.sem, 1)
                dve.wait_ge(rs_1.sem, rs_1.at(b, 1))
                dve.wait_ge(var_1.sem, var_1.at(b, 1))
                normalise(rows1, x1, 1).then_inc(rows1_done.sem, 1)

            first = Chain(dve, dve_own.sem)
            front_moments(0, first)
            front_rows(0)
            for c in range(C):
                dve.wait_ge(ctx_ev.sem, c + 1)
                dve.tensor_tensor(ctx_lo[:, c, :], trans[c][:, :], ctx_hi[:, c, :].bitcast(F32), ALU.subtract) \
                    .then_inc(ctx_lo_done.sem, 1)
            dve.wait_ge(ctx_lo_done.sem, C)
            dve.wait_ge(consts.sem, 9)
            for c in range(C):
                spread_keys(dve, 0, 0, c)
            queries_low(0)
            front_moments(1, first)
            front_rows(1)
            queries_low(1)
            assert first.n == links_before(0), first.n
            steps(dve, step)
            back(B - 1)
            dve.wait_ge(bn_taken.sem, bn_taken.at(B, 0))
            for c in range(C):
                last = dve.bn_aggr(bn_mv[:, c, :], bn_stats[:, c, :, :].rearrange("p b s -> p (b s)"))
            last.then_inc(bn_var.sem, 1)
            dve.wait_ge(bn_rs_ready.sem, 2)
            dve.wait_ge(gb_in.sem, 32)
            dve.tensor_tensor(bn_out[:, 0, :], bn_rs[:, :], gamma_beta[:, 0, :], ALU.mult).then_inc(bn_done.sem, 1)
            dve.wait_ge(bn_done.sem, 1)
            dve.tensor_tensor(bn_tmp[:, :], bn_mv[:, :, 0], bn_out[:, 0, :], ALU.mult).then_inc(bn_done.sem, 1)
            dve.wait_ge(bn_done.sem, 2)
            dve.tensor_tensor(bn_out[:, 1, :], gamma_beta[:, 1, :], bn_tmp[:, :], ALU.subtract).then_inc(bn_done.sem, 1)
            dve.wait_ge(bn_done.sem, 3)


def retrieve_experts(nc, xt_dram, x1_dram, w_q, keys, x2_dram, cst):
    H, K, _, KD = keys.shape
    E, D = cst["key_in"].shape
    N = x1_dram.shape[0]
    C, NV, R, T = D // P, E // P, 2 * P, 2
    BLOCKS = N // R
    TOP = 8
    PICKS = H * TOP
    HALF = PICK_HALF
    ident, bn = cst["ident"], cst["bn"]
    own = ExitStack()
    with own:
        def sb(name, shape, dt=F32):
            return own.enter_context(nc.sbuf_tensor(name, shape, dt))

        def sig(name, per=0, start=0):
            return Signal(own.enter_context(nc.semaphore(name)), per, start)

        bank = [own.enter_context(nc.psum_tensor(f"b_bank{i}", [P, 512], F32)) for i in range(8)]
        down_b, up_b, sim_b, tr_b = bank[0:2], bank[4], bank[5:7], bank[7]
        w_b = bank[2:4] + down_b

        key_hi = sb("b_key_hi", [P, C, NV, P], F32R)
        key_lo = sb("b_key_lo", [P, C, NV, P], F32R)
        key_up, gated = cst["key_up"], cst["key_rows"]
        score_w = sb("b_score_w", [P, C, 2 * H * K])
        hot_u = cst["hot_u"]
        hot_v = [sb(f"b_hot_v{h}", [P, NV, HALF], BF16) for h in range(2)]
        weigh_v = [cst["weigh_v0"], sb("b_weigh_v1", [P, 3, 2, NV, HALF], BF16)]
        ramp = sb("b_ramp", [P, P, 4], BF16)
        ramp8 = sb("b_ramp8", [P, TOP])
        x_raw = sb("b_x_raw", [P, C, R])
        x_hi = sb("b_x_hi", [P, C, R], F32R)
        x_lo = sb("b_x_lo", [P, C, R], F32R)
        x_norm = sb("b_x_norm", [P, C, R])
        x_rows = sb("b_x_rows", [P, T, D])
        best = sb("b_best", [P, 2, H, TOP])
        best_at = sb("b_best_at", [P, 2, H, TOP], U32)
        pairs = sb("b_pairs", [P, H, TOP, TOP])
        top = sb("b_top", [P, H, TOP])
        top_at = sb("b_top_at", [P, H, TOP], U32)
        coords = sb("b_coords", [P, 2, PICKS], U32)
        coords_f = sb("b_coords_f", [P, 2, PICKS])
        at_f = sb("b_at_f", [P, 2, H, TOP])
        hit = sb("b_hit", [P, 2, H, TOP, TOP])
        delta = sb("b_delta", [P, H, TOP])
        expo = sb("b_expo", [P, H, TOP])
        total = sb("b_total", [P, H])
        share = sb("b_share", [P, H])
        expert = sb("b_expert", [P, 2, PICKS])
        upper = sb("b_upper", [P, PICKS])
        cat = sb("b_cat", [P, 3, 2, PICKS])
        uv = sb("b_uv", [P, 2, PICKS], BF16)
        part = sb("b_part", [P, 3, PICKS], BF16)
        rest = sb("b_rest", [P, PICKS])
        rest2 = sb("b_rest2", [P, PICKS])
        consts, zeroed = sig("b_consts"), sig("b_zeroed")
        s_tr, s_act, s_dve = sig("b_s_tr"), sig("b_s_act"), sig("b_s_dve")
        passed = sig("b_passed")
        raw_in, xn_ready = sig("b_raw_in", 16), sig("b_xn", 1, 1)
        xh_ready, xl_ready = sig("b_xh", 1), sig("b_xl", 1, 1)
        sims_done, topk_read = sig("b_sims", 2, 2), sig("b_topk_read", 2, 1)
        topk_done, map_done, exp_done = sig("b_topk", 2), sig("b_map", 2, 1), sig("b_exp", 2)
        cat_ready, tr_done = sig("b_cat", 2), sig("b_tr", 2)
        gen_ready, w_done, h_done = sig("b_gen", 4), sig("b_w", 16, 8), sig("b_h", 16, 4)
        down_done, gelu_done = sig("b_down", 16), sig("b_gelu", 16, 2)
        up_done, x2_done = sig("b_up", 2), sig("b_x2", 2, 1)
        rows_in, kept = sig("b_rows_in", 16), sig("b_kept", 32, 32)
        DVE_FIRST, DVE_TURN = 17, 30
        POOL_TILE = 7
        dve_own, pool_own = sig("b_dve_own"), sig("b_pool_own")
        block = own.enter_context(nc.Block())
        xt_view = xt_dram.rearrange("c p n -> p c n")
        setup_rows = gated
        wq_all, keys_rows, keys_t = cst["wq_all"], cst["keys_rows"], cst["keys_t"]

        @block.sync
        def _(sp):
            def load_x(j):
                sp.wait_ge(xl_ready.sem, xl_ready.at(j, 0))
                sp.wait_ge(xn_ready.sem, xn_ready.at(j, 0))
                sp.dma_start(x_raw[:, :, :], xt_view[:, :, bass.ds(j * R, R)]).then_inc(raw_in.sem, 16)

            def rows_through(j, ahead):
                sp.wait_ge(kept.sem, kept.at(j, 0))
                sp.dma_start(x_rows[:, :, :], x1_dram[bass.ds(j * R, R), :].rearrange("(t p) d -> p t d", p=P)) \
                    .then_inc(rows_in.sem, 16)
                for t in range(T):
                    sp.wait_ge(x2_done.sem, x2_done.at(j, t + 1))
                    sp.dma_start(x2_dram[bass.ds(j * R + t * P, P), :], x_rows[:, t, :]).then_inc(kept.sem, 16)
                    if ahead and t == 0:
                        load_x(j + 2)

            load_x(0)
            load_x(1)
            with sp.Fori(0, BLOCKS - 2) as i:
                rows_through(i, True)
            rows_through(BLOCKS - 2, False)
            rows_through(BLOCKS - 1, False)
            sp.wait_ge(kept.sem, kept.at(BLOCKS, 0))

        @block.gpsimd
        def _(pool):
            pool.iota(ramp[:, :, :], [[1, P], [0, 4]], channel_multiplier=0,
                      allow_small_or_imprecise_dtypes=True).then_inc(consts.sem, 1)
            pool.iota(ramp8[:, :], [[1, TOP]], channel_multiplier=0,
                      allow_small_or_imprecise_dtypes=True).then_inc(consts.sem, 1)
            pool.wait_ge(consts.sem, 2)
            for s in (xn_ready, xl_ready, sims_done, topk_read, map_done, w_done, h_done, gelu_done, x2_done, kept):
                pool.sem_inc(s.sem, s.start)
            pool.memset(weigh_v[1][:, :, :, :, :], 0.0).then_inc(zeroed.sem, 1)
            pool.wait_ge(s_tr.sem, 6)
            pool.memset(weigh_v[0][:, :, :, :, :], 0.0).then_inc(zeroed.sem, 1)

            def place_picks(j, t, chain):
                wait_apart(pool, topk_done.sem, topk_done.at(j, t + 1), passed.sem)
                chain.link(pool.tensor_copy(coords_f[:, :, :], coords[:, :, :]))
                chain.link(pool.tensor_copy(at_f[:, :, :, :], best_at[:, :, :, :]))
                for a in range(2):
                    chain.wait()
                    hits = hit[:, a, :, :, :].rearrange("p h k i -> p (h k) i")
                    chain.link(pool.tensor_tensor(hits, coords_f[:, a, :].unsqueeze(2).to_broadcast([P, PICKS, TOP]),
                                                  ramp8[:, :].unsqueeze(1).to_broadcast([P, PICKS, TOP]), ALU.subtract))
                    chain.wait_apart(passed.sem)
                    chain.link(pool.tensor_scalar(hits, hits, 0.0, None, ALU.is_equal))
                    chain.wait()
                    last = pool.tensor_tensor(hit[:, a, :, :, :], hit[:, a, :, :, :],
                                              at_f[:, a, :, :].unsqueeze(2).to_broadcast([P, H, TOP, TOP]), ALU.mult)
                    if a == 0:
                        chain.link(last)
                last.then_inc(map_done.sem, 1)

            def split_low(j):
                pool.wait_ge(xh_ready.sem, xh_ready.at(j, 1))
                pool.tensor_tensor(x_lo[:, :, :], x_raw[:, :, :], x_hi[:, :, :].bitcast(F32), ALU.subtract) \
                    .then_inc(xl_ready.sem, 1)

            def prepare(j):
                chain = Chain(pool, pool_own.sem, j * (2 * POOL_TILE))
                place_picks(j, 0, chain)
                if not isinstance(j, int):
                    split_low(j)
                place_picks(j, 1, chain)
                assert chain.n == 2 * POOL_TILE, chain.n

            split_low(0)
            prepare(0)
            with pool.Fori(0, BLOCKS - 1) as i:
                prepare(i + 1)

        @block.tensor
        def _(pe):
            for a in range(2):
                for t in range(4):
                    last = pe.transpose(bank[a][:, t * P:(t + 1) * P], keys_rows[:, t, a * KD:(a + 1) * KD], ident[:, :])
                last.then_inc(s_tr.sem, 1)
            pe.wait_ge(s_act.sem, 2)
            for a in range(2):
                for c in range(C):
                    for h in range(H):
                        last = pe.matmul(bank[2 + 2 * a + c][:, h * K:(h + 1) * K], wq_all[a][:, h, c * P:(c + 1) * P],
                                         keys_t[:, a, h * K:(h + 1) * K], start=True, stop=True)
                    last.then_inc(s_tr.sem, 1)
            n = 0
            for c in range(C):
                for v in range(0, NV, 4):
                    b = (6 + n % 4) % 8
                    if n >= 4:
                        pe.wait_ge(s_act.sem, 6 + n - 3)
                        pe.wait_ge(s_dve.sem, n - 3)
                    for k in range(4):
                        last = pe.transpose(bank[b][:, k * P:(k + 1) * P], setup_rows[:, v + k, c * P:(c + 1) * P], ident[:, :])
                    last.then_inc(s_tr.sem, 1)
                    n += 1
            pe.wait_ge(s_act.sem, 6 + n)
            pe.wait_ge(s_dve.sem, n)

            def scores(j, t):
                if t == 0:
                    pe.wait_ge(xn_ready.sem, xn_ready.at(j, 1))
                pe.wait_ge(topk_read.sem, topk_read.at(j, t + 1 - 1))
                for a in range(2):
                    for c in range(C):
                        last = pe.matmul(sim_b[a][:, :], x_norm[:, c, t * P:(t + 1) * P],
                                         score_w[:, c, a * H * K:(a + 1) * H * K], start=(c == 0), stop=(c == C - 1))
                last.then_inc(sims_done.sem, 1)

            def down(j, groups=range(NV // 2)):
                pe.wait_ge(xl_ready.sem, xl_ready.at(j, 1))
                for g in groups:
                    pe.wait_ge(gelu_done.sem, gelu_done.at(j, g + 1 - 2))
                    for v in (2 * g, 2 * g + 1):
                        o = down_b[g % 2][:, (v % 2) * R:(v % 2 + 1) * R]
                        for c in range(C):
                            last = three_pass(pe, o, key_hi[:, c, v, :], key_lo[:, c, v, :], x_hi[:, c, :], x_lo[:, c, :],
                                              c == 0, c == C - 1)
                    last.then_inc(down_done.sem, 1)

            def turn_picks(j, t):
                pe.wait_ge(cat_ready.sem, cat_ready.at(j, t + 1))
                for k in range(3):
                    last = pe.transpose(tr_b[:, k * P:(k + 1) * P], cat[:, k, :, :].rearrange("p a b -> p (a b)"), ident[:, :])
                last.then_inc(tr_done.sem, 1)

            def weights(j, t):
                for q in range(8):
                    h = q // 4
                    if q % 4 == 0:
                        pe.wait_ge(gen_ready.sem, gen_ready.at(j, 2 * t + h + 1))
                    if t == 0 and q == 2:
                        pe.wait_ge(gelu_done.sem, gelu_done.at(j, NV // 2))
                    pe.wait_ge(h_done.sem, h_done.at(j, 8 * t + q + 1 - 4))
                    for mm in range(8):
                        m = (q % 4) * 8 + mm
                        for k in range(3):
                            last = pe.matmul(w_b[q % 4][:, mm * 64:(mm + 1) * 64], hot_u[h][:, :, m],
                                             weigh_v[h][:, k, :, :, m].rearrange("p r v -> p (r v)"),
                                             start=(k == 0), stop=(k == 2))
                    last.then_inc(w_done.sem, 1)

            def up(j, t):
                pe.wait_ge(h_done.sem, h_done.at(j, 8 * t + 8))
                pe.wait_ge(x2_done.sem, x2_done.at(j, t + 1 - 1))
                for v in range(NV):
                    last = pe.matmul(up_b[:, 0:D], gated[:, v, t * P:(t + 1) * P], key_up[:, v, :],
                                     start=(v == 0), stop=(v == NV - 1))
                last.then_inc(up_done.sem, 1)

            scores(0, 0)
            scores(0, 1)

            def turn(i, more):
                if isinstance(i, int) and i == 0:
                    down(0, range(0, NV // 4))
                    turn_picks(0, 0)
                    down(0, range(NV // 4, NV // 2))
                    scores(1, 0)
                else:
                    if more:
                        scores(i + 1, 0)
                    down(i)
                turn_picks(i, 1)
                weights(i, 0)
                if more:
                    scores(i + 1, 1)
                up(i, 0)
                weights(i, 1)
                if more:
                    turn_picks(i + 1, 0)
                up(i, 1)

            turn(0, True)
            with pe.Fori(0, BLOCKS - 2) as i:
                turn(i + 1, True)
            turn(BLOCKS - 1, False)

        @block.scalar
        def _(act):
            for a in range(2):
                act.wait_ge(s_tr.sem, a + 1)
                act.activation(keys_t[:, a, :], bank[a][:, :], ACT.Copy).then_inc(s_act.sem, 1)
            for a in range(2):
                for c in range(C):
                    act.wait_ge(s_tr.sem, 2 + 2 * a + c + 1)
                    act.activation(score_w[:, c, a * H * K:(a + 1) * H * K], bank[2 + 2 * a + c][:, :], ACT.Copy) \
                        .then_inc(s_act.sem, 1)
            n = 0
            for c in range(C):
                for v in range(0, NV, 4):
                    act.wait_ge(s_tr.sem, 6 + n + 1)
                    act.activation(key_hi[:, c, v:v + 4, :].rearrange("p a b -> p (a b)"), bank[(6 + n % 4) % 8][:, :], ACT.Copy) \
                        .then_inc(s_act.sem, 1)
                    n += 1

            def normalise(j):
                act.wait_ge(raw_in.sem, raw_in.at(j, 16))
                act.wait_ge(sims_done.sem, sims_done.at(j, 0))
                for c in range(C):
                    last = act.activation(x_norm[:, c, :], x_raw[:, c, :], ACT.Identity,
                                          bias=bn[:, 1, c:c + 1], scale=bn[:, 0, c:c + 1])
                last.then_inc(xn_ready.sem, 1)

            def split_high(j):
                act.activation(x_hi[:, :, :], x_raw[:, :, :], ACT.Copy).then_inc(xh_ready.sem, 1)

            def exps(j, t):
                act.wait_ge(topk_done.sem, topk_done.at(j, t + 1))
                act.activation(expo[:, :, :], delta[:, :, :], ACT.Exp).then_inc(exp_done.sem, 1)

            def gelus(j):
                for g in range(NV // 2):
                    act.wait_ge(down_done.sem, down_done.at(j, g + 1))
                    act.activation(gated[:, 2 * g:2 * g + 2, :].rearrange("p v n -> p (v n)"), down_b[g % 2][:, :], ACT.Gelu) \
                        .then_inc(gelu_done.sem, 1)

            normalise(0)
            split_high(0)
            exps(0, 0)
            normalise(1)
            gelus(0)
            exps(0, 1)
            split_high(1)
            exps(1, 0)
            exps(1, 1)
            with act.Fori(0, BLOCKS - 2) as i:
                normalise(i + 2)
                gelus(i + 1)
                split_high(i + 2)
                exps(i + 2, 0)
                exps(i + 2, 1)
            gelus(BLOCKS - 1)

        @block.vector
        def _(dve):
            n = 0
            for c in range(C):
                for v in range(0, NV, 4):
                    dve.wait_ge(s_act.sem, 6 + n + 1)
                    lo = key_lo[:, c, v:v + 4, :].rearrange("p a b -> p (a b)")
                    hi = key_hi[:, c, v:v + 4, :].rearrange("p a b -> p (a b)").bitcast(F32)
                    dve.tensor_tensor(lo, bank[(6 + n % 4) % 8][:, :], hi, ALU.subtract).then_inc(s_dve.sem, 1)
                    n += 1
            dve.wait_ge(consts.sem, 2)
            dve.wait_ge(zeroed.sem, 2)

            def choose(j, t, chain):
                dve.wait_ge(map_done.sem, map_done.at(j, t + 1 - 1))
                wait_apart(dve, sims_done.sem, sims_done.at(j, t + 1), passed.sem)
                for a in range(2):
                    for h in range(H):
                        last = dve.max(best[:, a, h, :], sim_b[a][:, h * K:(h + 1) * K])
                chain.link(last)
                chain.wait_apart(passed.sem)
                for a in range(2):
                    for h in range(H):
                        last = dve.max_index(best_at[:, a, h, :], best[:, a, h, :], sim_b[a][:, h * K:(h + 1) * K])
                last.then_inc(topk_read.sem, 1)
                chain.link(dve.tensor_tensor(pairs[:, :, :, :], best[:, 0, :, :].unsqueeze(3).to_broadcast([P, H, TOP, TOP]),
                                             best[:, 1, :, :].unsqueeze(2).to_broadcast([P, H, TOP, TOP]), ALU.add))
                chain.wait_apart(passed.sem)
                for h in range(H):
                    last = dve.max(top[:, h, :], pairs[:, h, :, :].rearrange("p a b -> p (a b)"))
                chain.link(last)
                chain.wait_apart(passed.sem)
                for h in range(H):
                    last = dve.max_index(top_at[:, h, :], top[:, h, :], pairs[:, h, :, :].rearrange("p a b -> p (a b)"))
                chain.link(last)
                dve.tensor_tensor(delta[:, :, :], top[:, :, :], top[:, :, 0:1].to_broadcast([P, H, TOP]), ALU.subtract)
                chain.wait()
                flat = top_at[:, :, :].rearrange("p h k -> p (h k)")
                dve.tensor_scalar(coords[:, 0, :], flat, 3, None, ALU.logical_shift_right)
                dve.tensor_scalar(coords[:, 1, :], flat, 7, None, ALU.bitwise_and).then_inc(topk_done.sem, 1)

            def settle(j, t, chain):
                dve.wait_ge(map_done.sem, map_done.at(j, t + 1))
                chain.link(dve.reduce_sum(expert[:, :, :].rearrange("p a b -> p (a b)"),
                                          hit[:, :, :, :, :].rearrange("p a h k i -> p (a h k) i"), axis=AXX))
                dve.wait_ge(exp_done.sem, exp_done.at(j, t + 1))
                chain.link(dve.reduce_sum(total[:, :], expo[:, :, :], axis=AXX))
                chain.wait()
                chain.link(dve.tensor_scalar(upper[:, :], expert[:, 1, :], float(NV), None, ALU.is_ge))
                chain.link(dve.reciprocal(share[:, :], total[:, :]))
                chain.wait()
                twice = [P, 2, PICKS]
                dve.scalar_tensor_tensor(cat[:, 0, :, :], expert[:, 0, :].unsqueeze(1).to_broadcast(twice), 2.0,
                                         upper[:, :].unsqueeze(1).to_broadcast(twice), ALU.mult, ALU.add)
                dve.scalar_tensor_tensor(cat[:, 1, :, :], upper[:, :].unsqueeze(1).to_broadcast(twice), -float(NV),
                                         expert[:, 1, :].unsqueeze(1).to_broadcast(twice), ALU.mult, ALU.add)
                for k in range(2):
                    last = dve.tensor_tensor(cat[:, 2, k, :].rearrange("p (h k) -> p h k", h=H), expo[:, :, :],
                                             share[:, :].unsqueeze(2).to_broadcast([P, H, TOP]), ALU.mult)
                last.then_inc(cat_ready.sem, 1)

            def take_picks(j, t, chain):
                dve.wait_ge(tr_done.sem, tr_done.at(j, t + 1))
                for r in range(2):
                    on = slice(64 * r, 64 * r + 64)
                    view = tr_b[on, 0:2 * P].rearrange("p (a n) -> p a n", a=2)
                    dve.tensor_copy(uv[on, :, :], view[:, :, 64 * r:64 * r + 64])
                    last = dve.tensor_copy(part[on, 0, :], tr_b[on, 2 * P + 64 * r:2 * P + 64 * r + 64])
                chain.link(last)
                chain.wait()
                for r in range(2):
                    on = slice(64 * r, 64 * r + 64)
                    last = dve.tensor_tensor(rest[on, :], tr_b[on, 2 * P + 64 * r:2 * P + 64 * r + 64], part[on, 0, :],
                                             ALU.subtract)
                chain.link(last)
                chain.wait()
                chain.link(dve.tensor_copy(part[:, 1, :], rest[:, :]))
                chain.wait()
                chain.link(dve.tensor_tensor(rest2[:, :], rest[:, :], part[:, 1, :], ALU.subtract))
                chain.wait()
                chain.link(dve.tensor_copy(part[:, 2, :], rest2[:, :]))

            def one_hots(j, t, chain):
                for h in range(2):
                    dve.wait_ge(w_done.sem, w_done.at(j, 8 * t + 4 * h + 4 - 8))
                    cols = slice(HALF * h, HALF * h + HALF)

                    def equal(out, n, which):
                        return dve.tensor_tensor(
                            out.rearrange("p u (a b) -> p u a b", b=4),
                            ramp[:, 0:n, :].unsqueeze(2).to_broadcast([P, n, HALF // 4, 4]),
                            uv[:, which, cols].rearrange("p (a b) -> p a b", b=4).unsqueeze(1).to_broadcast([P, n, HALF // 4, 4]),
                            ALU.is_equal)

                    chain.link(equal(hot_v[h][:, :, :], NV, 1))
                    equal(hot_u[h][:, :, :], P, 0)
                    chain.wait()
                    for r in range(2):
                        on = slice(64 * r, 64 * r + 64)
                        last = dve.tensor_tensor(weigh_v[h][on, :, r, :, :],
                                                 hot_v[h][on, :, :].unsqueeze(1).to_broadcast([64, 3, NV, HALF]),
                                                 part[on, :, cols].unsqueeze(2).to_broadcast([64, 3, NV, HALF]), ALU.mult)
                    last.then_inc(gen_ready.sem, 1)

            def gate(j, t):
                dve.wait_ge(gelu_done.sem, gelu_done.at(j, NV // 2))
                for q in range(8):
                    dve.wait_ge(w_done.sem, w_done.at(j, 8 * t + q + 1))
                    g = gated[:, :, t * P:(t + 1) * P].rearrange("p v (r m) -> p m r v", r=2)[:, 8 * q:8 * q + 8, :, :]
                    dve.tensor_tensor(g, g, w_b[q % 4][:, :].rearrange("p (m r v) -> p m r v", m=8, r=2), ALU.mult) \
                        .then_inc(h_done.sem, 1)

            def add_rows(j, t):
                if t == 0:
                    dve.wait_ge(rows_in.sem, rows_in.at(j, 16))
                dve.wait_ge(up_done.sem, up_done.at(j, t + 1))
                dve.tensor_tensor(x_rows[:, t, :], x_rows[:, t, :], up_b[:, 0:D], ALU.add).then_inc(x2_done.sem, 1)

            def turn(i, more, chain):
                one_hots(i, 0, chain)
                settle(i, 1, chain)
                if more:
                    choose(i + 1, 0, chain)
                take_picks(i, 1, chain)
                gate(i, 0)
                chain.wait()
                one_hots(i, 1, chain)
                if more:
                    settle(i + 1, 0, chain)
                add_rows(i, 0)
                gate(i, 1)
                if more:
                    choose(i + 1, 1, chain)
                add_rows(i, 1)
                if more:
                    take_picks(i + 1, 0, chain)
                    chain.wait()

            first = Chain(dve, dve_own.sem)
            choose(0, 0, first)
            settle(0, 0, first)
            choose(0, 1, first)
            take_picks(0, 0, first)
            first.wait()
            assert first.n == DVE_FIRST, first.n
            with dve.Fori(0, BLOCKS - 1) as i:
                chain = Chain(dve, dve_own.sem, i * DVE_TURN + DVE_FIRST)
                turn(i, True, chain)
                assert chain.n == DVE_TURN, chain.n
            turn(BLOCKS - 1, False, Chain(dve, dve_own.sem, (BLOCKS - 1) * DVE_TURN + DVE_FIRST))


def attend_latents(nc, ctx, x2_dram, wts, out_dram, cst):
    B, S, D = ctx.shape
    N = x2_dram.shape[0] // B
    INNER = wts["wq"].shape[1]
    H, C, T, CH = 8, D // P, N // P, INNER // P
    DH = INNER // H
    F = N + S
    SCALE = DH ** -0.5
    ident, neghalf = cst["ident"], cst["neghalf"]
    own = ExitStack()
    with own:
        def sb(name, shape, dt=F32):
            return own.enter_context(nc.sbuf_tensor(name, shape, dt))

        def sig(name, per=0, start=0):
            return Signal(own.enter_context(nc.semaphore(name)), per, start)

        score_b = [own.enter_context(nc.psum_tensor(f"c_score{i}", [P, 1024], F32)) for i in range(2)]
        turn_b = [own.enter_context(nc.psum_tensor(f"c_turn{i}", [P, 512], F32)) for i in range(2)]
        sum_b = [own.enter_context(nc.psum_tensor(f"c_sum{i}", [P, 512], F32)) for i in range(2)]
        score_v = [b[:, :].rearrange("p (a n) -> p a n", a=2)[:, :, 0:F // 2] for b in score_b]
        pool4 = [score_b[i // 2][:, 512 * (i % 2):512 * (i % 2) + 512] for i in range(4)]

        names = ("wk", "wv", "wq")
        w_hi = {n: sb(f"c_{n}_hi", [P, C, INNER], F32R) for n in names}
        w_lo = {n: sb(f"c_{n}_lo", [P, C, INNER], F32R) for n in names}
        w_out = sb("c_w_out", [P, CH, D])
        ternary = sb("c_ternary", [P, C, D], F32R)
        affine = sb("c_affine", [P, 4, C])
        wscale = sb("c_wscale", [P, 3])
        ones = sb("c_ones", [P, P])
        ctx_k_hi = sb("c_ctx_k_hi", [P, CH, B * S], F32R)
        ctx_k_lo = sb("c_ctx_k_lo", [P, CH, B * S], F32R)
        ctx_v = sb("c_ctx_v", [S, B, INNER])
        xz = sb("c_xz", [P, T, D])
        xr = sb("c_xr", [P, T, D])
        z0 = sb("c_z0", [P, T, D])
        z1 = xz
        zt = sb("c_zt", [P, C, N])
        z_hi = sb("c_z_hi", [P, C, N], F32R)
        z_lo = sb("c_z_lo", [P, C, N], F32R)
        q_hi = [sb(f"c_q_hi{e}", [P, CH, N], F32R) for e in range(2)]
        q_lo = [sb(f"c_q_lo{e}", [P, CH, N], F32R) for e in range(2)]
        k_hi = sb("c_k_hi", [P, CH, F], F32R)
        k_lo = sb("c_k_lo", [P, CH, F], F32R)
        v_rows = sb("c_v_rows", [P, T, INNER])
        v_ctx = sb("c_v_ctx", [S, INNER])
        probs = [sb(f"c_probs{e}", [P, T, F]) for e in range(2)]
        probs_t = [sb(f"c_probs_t{e}", [P, T + 1, N]) for e in range(2)]
        heads = sb("c_heads", [P, CH, N])
        r_hi = sb("c_r_hi", [P, C, N], F32R)
        r_lo = sb("c_r_lo", [P, C, N], F32R)
        x3 = sb("c_x3", [P, T, D])
        nmax = sb("c_nmax", [P, H * T])
        sums = sb("c_sums", [P, H * T])
        inv = sb("c_inv", [P, H * T])
        stats = sb("c_stats", [P, T, 6])
        mean_var = sb("c_mean_var", [P, 3, T, 2])
        var_eps = sb("c_var_eps", [P, 3, T])
        rstd = sb("c_rstd", [P, 3, T])

        ld_w = {n: sig(f"c_ld_{n}") for n in names}
        ld_misc, ld_ctx = sig("c_ld_misc"), sig("c_ld_ctx")
        s_act, s_dve, s_pe, s_pool = sig("c_s_act"), sig("c_s_dve"), sig("c_s_pe"), sig("c_s_pool")
        passed = sig("c_passed")
        xz_in, xr_in = sig("c_xz_in", 16), sig("c_xr_in", 16)
        var_z, rs_z, z0_done, z1_done = sig("c_var_z", 2), sig("c_rs_z", 2), sig("c_z0", 1), sig("c_z1", 1)
        var_x, rs_x, r3_done = sig("c_var_x", 1), sig("c_rs_x", 1), sig("c_r3", 1)
        zhi_done, zlo_done = sig("c_zhi", 1), sig("c_zlo", 1)
        proj_done, proj_act, proj_dve = sig("c_proj", 14), sig("c_proj_act", 14), sig("c_proj_dve", 8)
        vctx_done, kctx_done = sig("c_vctx", 1), sig("c_kctx", 2)
        score_done, max_done, exp_done = sig("c_score", 32), sig("c_max", 32), sig("c_exp", 32, 2)
        inv_done, norm_done = sig("c_inv", 32), sig("c_norm", 32)
        turned, ev_act, ev_dve = sig("c_turned", 40, 10), sig("c_ev_act", 24, 2), sig("c_ev_dve", 16, 2)
        av_done, heads_done = sig("c_av", 4, 4), sig("c_heads", 4, 1)
        wout_done, x3_done = sig("c_wout", 2), sig("c_x3", 2, 2)
        ft_done, f_hi, f_lo = sig("c_ft", 2), sig("c_fhi", 2), sig("c_flo", 2, 2)
        ff_done, y_done, kept = sig("c_ff", 2), sig("c_y", 2, 4), sig("c_kept", 16, 16)
        SETUP_DVE, SETUP_ACT = 12 + CH, 7 + CH + B
        dve_own, pool_own = sig("c_dve_own"), sig("c_pool_own")
        block = own.enter_context(nc.Block())
        w_raw = {"wq": probs[0][:, :, :].rearrange("p a b -> p (a b)")[:, 0:C * INNER].rearrange("p (c n) -> p c n", c=C),
                 "wk": probs[1][:, :, :].rearrange("p a b -> p (a b)")[:, 0:C * INNER].rearrange("p (c n) -> p c n", c=C),
                 "wv": probs_t[0][:, 0:2, :]}
        ctx_rows, lin_rows = xr[:, :, :], x3[:, 0:2, :]
        tern_rows, above, ctx_norm = [heads[:, a:b, :].rearrange("p a b -> p (a b)").rearrange("p (t d) -> p t d", d=D)
                                      for a, b in ((0, 1), (1, 2), (2, 4))]
        ctx_zt = probs_t[1][:, 0:C, :]
        MEDIA_W, MEDIA_B, LAT_W, LAT_B = range(4)
        slots = [(), (0, 1), (2,), (3, 4)]
        SCALAR_CHUNKS = (1, 2, 3)
        pair_turns = {2 * c + 3: c for c in range(CH - 1)}

        def turn_bank(n):
            return turn_b[n % 2] if n < 5 * H - 3 else pool4[n - (5 * H - 3)]

        def ev_wait(eng, j, n):
            turn, n = (-1, n + 5 * H) if n < 0 else (0, n)
            hh, fc = n // 5, n % 5
            if fc in SCALAR_CHUNKS:
                eng.wait_ge(ev_act.sem, ev_act.at(j, 3 * hh + fc + 24 * turn))
            else:
                eng.wait_ge(ev_dve.sem, ev_dve.at(j, 2 * hh + fc // 4 + 1 + 16 * turn))

        @block.sync
        def _(sp):
            def load_z(j):
                if not isinstance(j, int):
                    sp.wait_ge(proj_act.sem, proj_act.at(j, C - 14))
                sp.dma_start(xz[:, :, :], x2_dram[bass.ds(j * N, N), :].rearrange("(t p) d -> p t d", p=P)).then_inc(xz_in.sem, 16)

            sp.dma_start(ctx_rows, ctx.rearrange("b s d -> (b s) d").rearrange("(t p) d -> p t d", p=P)).then_inc(ld_ctx.sem, 16)
            load_z(0)
            for k, name in enumerate(("media_w", "media_b", "lat_w", "lat_b")):
                sp.dma_start(affine[:, k, :], wts[name].rearrange("(c p) -> p c", p=P),
                             allow_slow_non_contiguous=True).then_inc(ld_misc.sem, 16)
            sp.dma_start(lin_rows, wts["lin"].rearrange("(t p) d -> p t d", p=P)).then_inc(ld_misc.sem, 16)
            sp.dma_start(w_out[:, :, :], wts["wout"].rearrange("(c p) d -> p c d", p=P)).then_inc(ld_misc.sem, 16)
            for n in names:
                sp.dma_start(w_raw[n], wts[n].rearrange("(c p) n -> p c n", p=P)).then_inc(ld_w[n].sem, 16)

            def rows_through(j):
                sp.wait_ge(x3_done.sem, x3_done.at(j, 0))
                sp.dma_start(xr[:, :, :], x2_dram[bass.ds(j * N, N), :].rearrange("(t p) d -> p t d", p=P)).then_inc(xr_in.sem, 16)

            def store(j):
                sp.wait_ge(y_done.sem, y_done.at(j, 2))
                sp.dma_start(out_dram[bass.ds(j * N, N), :].rearrange("(t p) d -> p t d", p=P), x3[:, :, :]).then_inc(kept.sem, 16)

            sp.wait_ge(s_dve.sem, SETUP_DVE)
            with sp.Fori(0, B - 1) as i:
                rows_through(i)
                load_z(i + 1)
                store(i)
            rows_through(B - 1)
            store(B - 1)
            sp.wait_ge(kept.sem, kept.at(B, 0))

        @block.gpsimd
        def _(pool):
            chain = Chain(pool, s_pool.sem)
            chain.link(pool.memset(ones[:, :], 1.0))
            for s in (exp_done, turned, ev_act, ev_dve, av_done, heads_done, x3_done, f_lo, y_done, kept):
                pool.sem_inc(s.sem, s.start)

            def rsqrt(chain, var, rs, j, k, which):
                wait_apart(pool, var.sem, var.at(j, k), passed.sem)
                chain.link(pool.tensor_scalar(var_eps[:, which, :], mean_var[:, which, :, 1], EPS, None, ALU.add))
                chain.wait()
                pool.tensor_tensor(rstd[:, which, :], var_eps[:, which, :], neghalf[:, 0:T], ALU.pow).then_inc(rs.sem, 1)

            pool.wait_ge(s_dve.sem, 2)
            chain.link(pool.tensor_scalar(var_eps[:, 2, :], mean_var[:, 2, :, 1], EPS, None, ALU.add))
            chain.wait()
            chain.link(pool.tensor_tensor(rstd[:, 2, :], var_eps[:, 2, :], neghalf[:, 0:T], ALU.pow))
            first = Chain(pool, pool_own.sem)
            rsqrt(first, var_z, rs_z, 0, 1, 0)
            rsqrt(first, var_z, rs_z, 0, 2, 1)
            pool.wait_ge(rs_z.sem, rs_z.at(0, 2))
            for e in range(2):
                for q in (q_hi[e], q_lo[e]):
                    chain.wait()
                    chain.link(pool.memset(q[64 * (1 - e):64 * (1 - e) + 64, :, :].bitcast(U32), 0))

            def values_of_context(j):
                wait_apart(pool, av_done.sem, av_done.at(j, 0), passed.sem)
                for dst, src in ((k_hi, ctx_k_hi), (k_lo, ctx_k_lo)):
                    pool.tensor_copy(dst[:, :, N:F], src[:, :, bass.ds(j * S, S)]).then_inc(kctx_done.sem, 1)
                pool.tensor_copy(v_ctx[:, :], ctx_v[:, bass.ds(j, 1), :].rearrange("p a n -> p (a n)")).then_inc(vctx_done.sem, 1)

            def turn(j, more, chain):
                if more:
                    rsqrt(chain, var_z, rs_z, j + 1, 1, 0)
                    rsqrt(chain, var_z, rs_z, j + 1, 2, 1)
                if more:
                    values_of_context(j + 1)
                rsqrt(chain, var_x, rs_x, j, 1, 2)

            pool.wait_ge(s_act.sem, SETUP_ACT)
            values_of_context(0)
            with pool.Fori(0, B - 1) as i:
                turn(i, True, Chain(pool, pool_own.sem, i * 3 + 2))
            turn(B - 1, False, Chain(pool, pool_own.sem, (B - 1) * 3 + 2))

        @block.tensor
        def _(pe):
            n = [0]

            def setup_step(last):
                last.then_inc(s_pe.sem, 1)
                n[0] += 1

            pe.wait_ge(s_dve.sem, 3)
            for c in range(C):
                for t in range(B * S // P):
                    last = pe.transpose(turn_b[c][:, t * P:(t + 1) * P], ctx_norm[:, t, c * P:(c + 1) * P], ident[:, :])
                setup_step(last)
            pe.wait_ge(s_pool.sem, 1)
            pe.wait_ge(s_dve.sem, 5)
            setup_step(pe.matmul(sum_b[0][:, 0:1], ones[:, :], wscale[:, 0:1], start=True, stop=True))
            pe.wait_ge(s_dve.sem, 9)
            for c in range(C):
                for t in range(D // P):
                    last = pe.transpose(sum_b[c][:, t * P:(t + 1) * P], tern_rows[:, t, c * P:(c + 1) * P], ident[:, :])
                setup_step(last)
            def turn_rows(j, c):
                if c == 0:
                    pe.wait_ge(z1_done.sem, z1_done.at(j, 1))
                    pe.wait_ge(y_done.sem, y_done.at(j, 0 - 2))
                else:
                    pe.wait_ge(proj_act.sem, proj_act.at(j, c))
                for t in range(T):
                    last = pe.transpose(sum_b[1][:, t * P:(t + 1) * P], z1[:, t, c * P:(c + 1) * P], ident[:, :])
                last.then_inc(proj_done.sem, 1)

            def project(j, first, last_one):
                if first == 2:
                    pe.wait_ge(exp_done.sem, exp_done.at(j, 0))
                    pe.wait_ge(zlo_done.sem, zlo_done.at(j, 1))
                for u in range(first, last_one + 1):
                    if 6 <= u < 10:
                        pe.wait_ge(proj_act.sem, proj_act.at(j, u - 4 + 1))
                    elif u >= 10:
                        pe.wait_ge(proj_dve.sem, proj_dve.at(j, u - 10 + 1))
                    o = pool4[u % 4]
                    for d in range(C):
                        if u >= 6:
                            name, c = ("wq", u - 6) if u < 10 else ("wk", u - 10)
                            cols = slice(c * P, (c + 1) * P)
                            last = three_pass(pe, o, w_hi[name][:, d, cols], w_lo[name][:, d, cols],
                                              z_hi[:, d, :], z_lo[:, d, :], d == 0, d == C - 1)
                        else:
                            cols = slice((u - 2) * P, (u - 1) * P)
                            last = three_pass(pe, o, z_hi[:, d, cols], z_lo[:, d, cols],
                                              w_hi["wv"][:, d, :], w_lo["wv"][:, d, :], d == 0, d == C - 1)
                    last.then_inc(proj_done.sem, 1)

            def scores(j, hh, t):
                k = T * hh + t
                if k >= 2:
                    pe.wait_ge(exp_done.sem, exp_done.at(j, k + 1 - 2))
                c, e = hh // 2, hh % 2
                cols = slice(t * P, (t + 1) * P)
                for half in range(2):
                    keys = slice(half * F // 2, (half + 1) * F // 2)
                    last = three_pass(pe, score_v[k % 2][:, half, :], q_hi[e][:, c, cols], q_lo[e][:, c, cols],
                                      k_hi[:, c, keys], k_lo[:, c, keys], True, True)
                last.then_inc(score_done.sem, 1)

            def turn_probs(j, hh, fc):
                n = 5 * hh + fc
                if fc == 0:
                    pe.wait_ge(norm_done.sem, norm_done.at(j, T * hh + T))
                if n < 5 * H - 3:
                    ev_wait(pe, j, n - 2)
                else:
                    pe.wait_ge(exp_done.sem, exp_done.at(j, T * H))
                if n < 2:
                    pe.wait_ge(f_lo.sem, f_lo.at(j, n + 1 - 2))
                w = P if fc < T else S
                if w < P:
                    pe.sem_inc(passed.sem, 1)
                for t in range(T):
                    last = pe.transpose(turn_bank(n)[0:w, t * P:(t + 1) * P], probs[hh % 2][:, t, fc * P:fc * P + w], ident[:, :])
                last.then_inc(turned.sem, 1)

            def weigh_values(j, c):
                for n in (5 * (2 * c + 1) + 3, 5 * (2 * c + 1) + 4):
                    ev_wait(pe, j, n)
                pe.wait_ge(heads_done.sem, heads_done.at(j, c + 1 - 1))
                if c == 0:
                    pe.wait_ge(vctx_done.sem, vctx_done.at(j, 1))
                    pe.wait_ge(y_done.sem, y_done.at(j, 1 - 2))
                for fc in range(T + 1):
                    for e in range(2):
                        cols = slice((2 * c + e) * DH, (2 * c + e + 1) * DH)
                        v = v_rows[:, fc, cols] if fc < T else v_ctx[:, cols]
                        w = P if fc < T else S
                        last = pe.matmul(sum_b[0][DH * e:DH * e + DH, :], v, probs_t[e][0:w, fc, :],
                                         start=(fc == 0), stop=(fc == T))
                last.then_inc(av_done.sem, 1)

            def attend(j, more):
                pe.wait_ge(proj_act.sem, proj_act.at(j, 14))
                pe.wait_ge(proj_dve.sem, proj_dve.at(j, 8))
                pe.wait_ge(kctx_done.sem, kctx_done.at(j, 2))
                for hh in range(H + 1):
                    for t in range(T):
                        if hh < H:
                            scores(j, hh, t)
                        if t == 0 and more and hh == H:
                            turn_rows(j + 1, 1)
                        if t == 1 and hh in pair_turns:
                            weigh_values(j, pair_turns[hh])
                        if hh > 0:
                            for fc in slots[t]:
                                turn_probs(j, hh - 1, fc)
                    if more and hh == H - 1:
                        turn_rows(j + 1, 0)
                weigh_values(j, CH - 1)

            def out_product(j, more):
                pe.wait_ge(heads_done.sem, heads_done.at(j, CH))
                if more:
                    pe.wait_ge(proj_act.sem, proj_act.at(j + 1, C))
                else:
                    pe.wait_ge(y_done.sem, y_done.at(j, 0))
                for half in range(2):
                    for t in (2 * half, 2 * half + 1):
                        for c in range(CH):
                            last = pe.matmul(sum_b[half][:, (t % 2) * D:(t % 2 + 1) * D], heads[:, c, t * P:(t + 1) * P],
                                             w_out[:, c, :], start=(c == 0), stop=(c == CH - 1))
                    last.then_inc(wout_done.sem, 1)

            def ternary_rows(j):
                pe.wait_ge(r3_done.sem, r3_done.at(j, 1))
                for c in range(C):
                    ev_wait(pe, j, 5 * H - 2 + c)
                    for t in range(T):
                        last = pe.transpose(turn_b[c][:, t * P:(t + 1) * P], z0[:, t, c * P:(c + 1) * P], ident[:, :])
                    last.then_inc(ft_done.sem, 1)

            def ternary_product(j):
                pe.wait_ge(f_lo.sem, f_lo.at(j, 2))
                for half in range(2):
                    for t in (2 * half, 2 * half + 1):
                        for c in range(C):
                            o = sum_b[half][:, (t % 2) * D:(t % 2 + 1) * D]
                            pe.matmul(o, r_lo[:, c, t * P:(t + 1) * P], ternary[:, c, :], start=(c == 0), stop=False)
                            last = pe.matmul(o, r_hi[:, c, t * P:(t + 1) * P], ternary[:, c, :], start=False, stop=(c == C - 1))
                    last.then_inc(ff_done.sem, 1)

            pe.wait_ge(s_dve.sem, 10)
            for c in range(CH):
                for d in range(C):
                    last = three_pass(pe, pool4[c], w_hi["wk"][:, d, c * P:(c + 1) * P], w_lo["wk"][:, d, c * P:(c + 1) * P],
                                      r_hi[:, d, :], r_lo[:, d, :], d == 0, d == C - 1)
                setup_step(last)
            pe.wait_ge(s_act.sem, 7)
            for b in range(B):
                if b % 4 == 0:
                    turn_rows(0, b // 4)
                if b < 4:
                    pe.wait_ge(s_dve.sem, 12 + b + 1)
                else:
                    pe.wait_ge(s_act.sem, SETUP_ACT - B + b - 4 + 1)
                for d in range(C):
                    last = three_pass(pe, pool4[b % 4][0:S, :], r_hi[:, d, b * S:(b + 1) * S], r_lo[:, d, b * S:(b + 1) * S],
                                      w_hi["wv"][:, d, :], w_lo["wv"][:, d, :], d == 0, d == C - 1)
                setup_step(last)
            pe.wait_ge(s_act.sem, SETUP_ACT)

            project(0, 2, 13)
            with pe.Fori(0, B - 1) as i:
                attend(i, True)
                project(i + 1, 2, 5)
                out_product(i, True)
                project(i + 1, 6, 11)
                ternary_rows(i)
                project(i + 1, 12, 13)
                ternary_product(i)
            attend(B - 1, False)
            out_product(B - 1, False)
            ternary_rows(B - 1)
            ternary_product(B - 1)

        @block.scalar
        def _(act):
            for n in names:
                act.wait_ge(ld_w[n].sem, 16)
                act.activation(w_hi[n][:, :, :], w_raw[n], ACT.Copy).then_inc(s_act.sem, 1)
            act.wait_ge(ld_misc.sem, 96)
            act.wait_ge(s_pe.sem, 2)
            for c in range(C):
                last = act.activation(ctx_zt[:, c, :], turn_b[c][:, :], ACT.Identity,
                                      bias=affine[:, MEDIA_B, c:c + 1], scale=affine[:, MEDIA_W, c:c + 1])
            last.then_inc(s_act.sem, 1)
            act.wait_ge(s_act.sem, 4)
            act.activation(r_hi[:, :, :], ctx_zt, ACT.Copy).then_inc(s_act.sem, 1)
            for c in range(C):
                act.wait_ge(s_pe.sem, 4 + c)
                act.activation(ternary[:, c, :], sum_b[c][:, 0:D], ACT.Copy, scale=-1.0).then_inc(s_act.sem, 1)
            for c in range(CH):
                act.wait_ge(s_pe.sem, 6 + c)
                act.activation(ctx_k_hi[:, c, :], pool4[c], ACT.Copy).then_inc(s_act.sem, 1)
            def take_rows(j, c):
                if c < C:
                    act.wait_ge(proj_done.sem, proj_done.at(j, c + 1))
                    act.activation(zt[:, c, :], sum_b[1][:, :], ACT.Identity, bias=affine[:, LAT_B, c:c + 1],
                                   scale=affine[:, LAT_W, c:c + 1]).then_inc(proj_act.sem, 1)
                else:
                    act.wait_ge(proj_act.sem, proj_act.at(j, C))
                    act.activation(z_hi[:, :, :], zt[:, :, :], ACT.Copy).then_inc(zhi_done.sem, 1)

            def project(j, first, last_one):
                for u in range(first, last_one + 1):
                    act.wait_ge(proj_done.sem, proj_done.at(j, u + 1))
                    o = pool4[u % 4]
                    if u < 6:
                        last = act.activation(v_rows[:, u - 2, :], o, ACT.Copy)
                    elif u < 10:
                        act.activation(q_hi[0][0:64, u - 6, :], o[0:64, :], ACT.Copy, scale=SCALE)
                        last = act.activation(q_hi[1][64:128, u - 6, :], o[64:128, :], ACT.Copy, scale=SCALE)
                    else:
                        last = act.activation(k_hi[:, u - 10, 0:N], o, ACT.Copy)
                    last.then_inc(proj_act.sem, 1)

            def take_chunk(j, hh, fc):
                n = 5 * hh + fc
                act.wait_ge(turned.sem, turned.at(j, n + 1))
                if fc == 1:
                    act.wait_ge(av_done.sem, av_done.at(j, hh // 2))
                act.activation(probs_t[hh % 2][:, fc, :], turn_bank(n)[:, :], ACT.Copy).then_inc(ev_act.sem, 1)

            def attend(j, more):
                def take_heads(c):
                    act.wait_ge(av_done.sem, av_done.at(j, c + 1))
                    act.activation(heads[:, c, :], sum_b[0][:, :], ACT.Copy).then_inc(heads_done.sem, 1)

                for hh in range(H + 1):
                    if more and hh == H:
                        take_rows(j + 1, 0)
                        take_rows(j + 1, 1)
                    for t in range(T):
                        if hh < H:
                            k = T * hh + t
                            if t == 0:
                                act.wait_ge(turned.sem, turned.at(j, 5 * hh + 5 - 10))
                            act.wait_ge(max_done.sem, max_done.at(j, k + 1))
                            act.activation(probs[hh % 2][:, t, :].rearrange("p (a n) -> p a n", a=2), score_v[k % 2], ACT.Exp, bias=nmax[:, k:k + 1],
                                           accum_out=sums[:, k:k + 1]).then_inc(exp_done.sem, 1)
                        if t == 1 and hh in pair_turns:
                            take_heads(pair_turns[hh])
                        if hh > 0:
                            for fc in slots[t]:
                                if fc in SCALAR_CHUNKS:
                                    take_chunk(j, hh - 1, fc)
                        if t == 1 and more and hh == H:
                            take_rows(j + 1, C)
                take_heads(CH - 1)

            def split_rows(j):
                for c in range(C):
                    act.wait_ge(ft_done.sem, ft_done.at(j, c + 1))
                    act.activation(r_hi[:, c, :], turn_b[c][:, :], ACT.Copy).then_inc(f_hi.sem, 1)

            for b in range(B):
                if b == 0:
                    take_rows(0, 0)
                elif b == 4:
                    take_rows(0, 1)
                    take_rows(0, C)
                act.wait_ge(s_pe.sem, 10 + b)
                act.activation(ctx_v[:, b, :], pool4[b % 4][0:S, :], ACT.Copy).then_inc(s_act.sem, 1)
            act.wait_ge(s_pool.sem, 7)
            project(0, 2, 13)
            with act.Fori(0, B - 1) as i:
                attend(i, True)
                project(i + 1, 2, 11)
                split_rows(i)
                project(i + 1, 12, 13)
            attend(B - 1, False)
            split_rows(B - 1)

        @block.vector
        def _(dve):
            def moments(chain, src, which):
                for t in range(T):
                    last = dve.bn_stats(stats[:, t, :], src[:, t, :])
                chain.link(last)
                chain.wait_apart(passed.sem)
                for t in range(T):
                    last = dve.bn_aggr(mean_var[:, which, t, :], stats[:, t, :])
                return last

            def normalise(dst, src, which):
                for t in range(T):
                    last = dve.tensor_scalar(dst[:, t, :], src[:, t, :], mean_var[:, which, t, 0:1], rstd[:, which, t:t + 1],
                                             ALU.subtract, ALU.mult)
                return last

            def prepare(j, chain, step):
                if step == 0:
                    dve.wait_ge(xz_in.sem, xz_in.at(j, 16))
                    moments(chain, xz, 0).then_inc(var_z.sem, 1)
                elif step == 1:
                    dve.wait_ge(rs_z.sem, rs_z.at(j, 1))
                    dve.wait_ge(var_z.sem, var_z.at(j, 1))
                    normalise(z0, xz, 0).then_inc(z0_done.sem, 1)
                    dve.wait_ge(z0_done.sem, z0_done.at(j, 1))
                    moments(chain, z0, 1).then_inc(var_z.sem, 1)
                else:
                    dve.wait_ge(rs_z.sem, rs_z.at(j, 2))
                    dve.wait_ge(var_z.sem, var_z.at(j, 2))
                    normalise(z1, z0, 1).then_inc(z1_done.sem, 1)

            def split_low(j):
                dve.wait_ge(zhi_done.sem, zhi_done.at(j, 1))
                dve.tensor_tensor(z_lo[:, :, :], zt[:, :, :], z_hi[:, :, :].bitcast(F32), ALU.subtract).then_inc(zlo_done.sem, 1)

            def project(j, first, last_one):
                for u in range(first, last_one + 1):
                    dve.wait_ge(proj_act.sem, proj_act.at(j, u + 1))
                    o = pool4[u % 4]
                    if u < 10:
                        for e in range(2):
                            on = slice(64 * e, 64 * e + 64)
                            last = dve.scalar_tensor_tensor(q_lo[e][on, u - 6, :], o[on, :], SCALE,
                                                            q_hi[e][on, u - 6, :].bitcast(F32), ALU.mult, ALU.subtract)
                    else:
                        last = dve.tensor_tensor(k_lo[:, u - 10, 0:N], o, k_hi[:, u - 10, 0:N].bitcast(F32), ALU.subtract)
                    last.then_inc(proj_dve.sem, 1)

            def invert(j, k):
                dve.wait_ge(exp_done.sem, exp_done.at(j, k + 1))
                dve.reciprocal(inv[:, k:k + 1], sums[:, k:k + 1]).then_inc(inv_done.sem, 1)
                dve.wait_ge(inv_done.sem, inv_done.at(j, k + 1))
                p = probs[k // T % 2][:, k % T, :]
                dve.tensor_scalar(p, p, inv[:, k:k + 1], None, ALU.mult).then_inc(norm_done.sem, 1)

            def take_chunk(j, hh, fc):
                n = 5 * hh + fc
                dve.wait_ge(turned.sem, turned.at(j, n + 1))
                if fc == 0:
                    dve.wait_ge(av_done.sem, av_done.at(j, hh // 2))
                w = P if fc < T else S
                dve.tensor_copy(probs_t[hh % 2][0:w, fc, :], turn_bank(n)[0:w, :]).then_inc(ev_dve.sem, 1)

            def attend(j, more, chain):
                for hh in range(H + 1):
                    for t in range(T):
                        k = T * hh + t
                        if t == 0 and hh > 0:
                            invert(j, k - 1)
                        if hh < H:
                            dve.wait_ge(score_done.sem, score_done.at(j, k + 1))
                            dve.tensor_reduce(out=nmax[:, k:k + 1], in_=score_v[k % 2], op=ALU.max, axis=AXXY,
                                              negate=True).then_inc(max_done.sem, 1)
                        if t > 0 and hh < H:
                            invert(j, k - 1)
                        if t == 1 and more and hh in pair_turns:
                            prepare(j + 1, chain, pair_turns[hh])
                        if hh > 0:
                            for fc in slots[t]:
                                if fc not in SCALAR_CHUNKS:
                                    take_chunk(j, hh - 1, fc)
                if more:
                    split_low(j + 1)

            def add_attention(j, chain, more):
                dve.wait_ge(xr_in.sem, xr_in.at(j, 16))
                dve.wait_ge(kept.sem, kept.at(j, 0))
                for half in range(2):
                    dve.wait_ge(wout_done.sem, wout_done.at(j, half + 1))
                    dve.tensor_tensor(x3[:, 2 * half:2 * half + 2, :], xr[:, 2 * half:2 * half + 2, :],
                                      sum_b[half][:, :].rearrange("p (t d) -> p t d", t=2), ALU.add).then_inc(x3_done.sem, 1)
                dve.wait_ge(x3_done.sem, x3_done.at(j, 2))
                moments(chain, x3, 2).then_inc(var_x.sem, 1)
                if more:
                    project(j + 1, 6, 7)
                dve.wait_ge(rs_x.sem, rs_x.at(j, 1))
                dve.wait_ge(var_x.sem, var_x.at(j, 1))
                normalise(z0, x3, 2).then_inc(r3_done.sem, 1)

            def split_rows(j):
                for c in range(C):
                    dve.wait_ge(f_hi.sem, f_hi.at(j, c + 1))
                    dve.tensor_tensor(r_lo[:, c, :], turn_b[c][:, :], r_hi[:, c, :].bitcast(F32), ALU.subtract).then_inc(f_lo.sem, 1)

            def finish(j):
                for half in range(2):
                    dve.wait_ge(ff_done.sem, ff_done.at(j, half + 1))
                    x = x3[:, 2 * half:2 * half + 2, :].rearrange("p t d -> p (t d)")
                    dve.scalar_tensor_tensor(x, sum_b[half][:, :], wscale[:, 1:2], x, ALU.mult, ALU.add).then_inc(y_done.sem, 1)

            chain = Chain(dve, s_dve.sem)
            dve.wait_ge(ld_ctx.sem, 16)
            chain.link(moments(chain, ctx_rows, 2))
            first = Chain(dve, dve_own.sem)
            chain.wait()
            prepare(0, first, 0)
            dve.wait_ge(s_pool.sem, 3)
            dve.wait_ge(s_dve.sem, 2)
            chain.link(normalise(ctx_norm, ctx_rows, 2))
            prepare(0, first, 1)

            def matrix_low(k):
                n = names[k]
                dve.wait_ge(s_act.sem, k + 1)
                chain.link(dve.tensor_tensor(w_lo[n][:, :, :], w_raw[n], w_hi[n][:, :, :].bitcast(F32), ALU.subtract))

            matrix_low(0)
            dve.wait_ge(ld_misc.sem, 96)
            chain.link(dve.tensor_reduce(out=wscale[:, 0:1], in_=lin_rows.rearrange("p a b -> p (a b)"), op=ALU.add, axis=AXX,
                                         apply_absolute_value=True))
            dve.wait_ge(s_pe.sem, 3)
            chain.link(dve.tensor_scalar(wscale[:, 1:2], sum_b[0][:, 0:1], 1.0 / (D * D), EPS, ALU.mult, ALU.max))
            chain.wait()
            chain.link(dve.tensor_scalar(wscale[:, 2:3], wscale[:, 1:2], -0.5, None, ALU.mult))
            chain.wait()
            chain.link(dve.tensor_scalar(above, lin_rows, -1.0, wscale[:, 2:3], ALU.mult, ALU.is_lt))
            chain.wait()
            chain.link(dve.scalar_tensor_tensor(tern_rows, lin_rows, wscale[:, 2:3], above, ALU.is_lt, ALU.subtract))
            prepare(0, first, 2)
            dve.wait_ge(s_act.sem, 5)
            chain.link(dve.tensor_tensor(r_lo[:, :, :], ctx_zt, r_hi[:, :, :].bitcast(F32), ALU.subtract))
            for k in range(1, len(names)):
                matrix_low(k)
            for c in range(CH):
                dve.wait_ge(s_act.sem, 7 + c + 1)
                chain.link(dve.tensor_tensor(ctx_k_lo[:, c, :], pool4[c], ctx_k_hi[:, c, :].bitcast(F32), ALU.subtract))
            assert chain.n == SETUP_DVE, chain.n

            split_low(0)
            dve.wait_ge(s_pool.sem, 7)
            project(0, 6, 13)
            with dve.Fori(0, B - 1) as i:
                chain = Chain(dve, dve_own.sem, i * 3 + 2)
                attend(i, True, chain)
                add_attention(i, chain, True)
                project(i + 1, 8, 11)
                split_rows(i)
                project(i + 1, 12, 13)
                finish(i)
                assert chain.n == 3, chain.n
            chain = Chain(dve, dve_own.sem, (B - 1) * 3 + 2)
            attend(B - 1, False, chain)
            add_attention(B - 1, chain, False)
            split_rows(B - 1)
            finish(B - 1)


def build(nc, x, ctx, gamma, beta, w_q, keys, key_in, key_out, media_w, media_b, lat_w, lat_b, wq, wk, wv, wout, lin, out):
    B, N, D = x.shape
    with ExitStack() as whole:
        ident = whole.enter_context(nc.sbuf_tensor("ident", [P, P], F32))
        neghalf = whole.enter_context(nc.sbuf_tensor("neghalf", [P, 8], F32))
        bn = whole.enter_context(nc.sbuf_tensor("bn", [P, 2, D // P], F32))
        cst = {"ident": ident, "neghalf": neghalf, "bn": bn, "gamma": gamma, "beta": beta}
        x1 = nc.dram_tensor("x1_rows", (B, N, D), F32).ap()
        xt = nc.dram_tensor("x1_norm_t", (D // P, P, B * N), F32).ap()
        x2 = nc.dram_tensor("x2_rows", (B * N, D), F32).ap()
        with ExitStack() as tables:
            rows = (P, key_in.shape[0] // P, D)
            cst["key_rows"] = tables.enter_context(nc.sbuf_tensor("key_rows", rows, F32))
            cst["key_up"] = tables.enter_context(nc.sbuf_tensor("key_up", rows, F32))
            cst["key_in"], cst["key_out"] = key_in, key_out
            hot_u = [tables.enter_context(nc.sbuf_tensor(f"b_hot_u{h}", [P, P, PICK_HALF], BF16)) for h in range(2)]
            weigh_v = tables.enter_context(nc.sbuf_tensor("b_weigh_v0", [P, 3, 2, rows[1], PICK_HALF], BF16))
            as_f32 = weigh_v[:, :, :, :, :].rearrange("p a b c d -> p (a b c d)").bitcast(F32)
            cst["hot_u"], cst["weigh_v0"] = hot_u, weigh_v
            cst["wq_all"] = [hot_u[h][:, :, :].rearrange("p a b -> p (a b)").bitcast(F32)
                             .rearrange("p (g d) -> p g d", d=D) for h in range(2)]
            cst["keys_rows"] = as_f32[:, 0:1024].rearrange("p (t d) -> p t d", t=4)
            cst["keys_t"] = as_f32[:, 1024:2048].rearrange("p (a n) -> p a n", a=2)
            wq_v = w_q.rearrange("(g p) d -> p g d", p=P)
            cst["key_loads"] = [(cst["keys_rows"], keys.rearrange("h k p d -> (h k) (p d)").rearrange("(t p) d -> p t d", p=P))] \
                + [(cst["wq_all"][h], wq_v[:, 8 * h:8 * h + 8, :]) for h in range(2)]
            attend_context(nc, x, ctx, x1, xt, cst)
            retrieve_experts(nc, xt, x1.rearrange("b n d -> (b n) d"), w_q, keys, x2, cst)
        wts = {"media_w": media_w, "media_b": media_b, "lat_w": lat_w, "lat_b": lat_b,
               "wq": wq, "wk": wk, "wv": wv, "wout": wout, "lin": lin}
        attend_latents(nc, ctx, x2, wts, out.rearrange("b n d -> (b n) d"), cst)


_INS = ["x", "ctx_1024", "L0_ffn_gamma", "L0_ffn_beta", "L0_ffn_w_q", "L0_ffn_keys", "L0_ffn_key_in", "L0_ffn_key_out",
        "L1_xattn_ln_media_w", "L1_xattn_ln_media_b", "L1_xattn_ln_lat_w", "L1_xattn_ln_lat_b",
        "L1_xattn_Wq", "L1_xattn_Wk", "L1_xattn_Wv", "L1_xattn_Wout", "L1_ffn_weight"]
_OUTS = [((8, 512, 256), "float32")]


def kernel(**inputs):
    import numpy as _np
    import concourse.bacc as _bacc
    from concourse import mybir as _mybir
    from concourse.bass_utils import run_bass_kernel_spmd as _run

    nc = _bacc.Bacc("TRN2", target_bir_lowering=False, num_devices=1)
    arrays, args = {}, []
    for name in _INS:
        a = _np.ascontiguousarray(inputs[name])
        arrays[f"in_{name}_dram"] = a
        args.append(nc.dram_tensor(f"in_{name}_dram", a.shape, _mybir.dt.from_np(a.dtype), kind="ExternalInput").ap())
    for i, (shape, dtype) in enumerate(_OUTS):
        dt = _mybir.dt.from_np(_np.dtype(dtype))
        args.append(nc.dram_tensor(f"out_{i}_dram", shape, dt, kind="ExternalOutput").ap())
    build(nc, *args)
    r = _run(nc, [arrays], core_ids=[0])
    got = tuple(r.results[0][f"out_{i}_dram"] for i in range(len(_OUTS)))
    return got if len(got) > 1 else got[0]
```
